# Optimizing a Trainium2 kernel written in Bass

```python
import numpy as np
import jax
import jax.numpy as jnp

def _softmax(x, axis=-1):
    return jax.nn.softmax(x, axis=axis)

def _gelu(x):
    return jax.nn.gelu(x, approximate=True)

def _silu(x):
    return jax.nn.silu(x)

def _sigmoid(x):
    return jax.nn.sigmoid(x)

def _layernorm(x, axis=-1, eps=1e-05):
    m = jnp.mean(x, axis=axis, keepdims=True)
    v = jnp.var(x, axis=axis, keepdims=True)
    return (x - m) / jnp.sqrt(v + eps)

def _scatter_add(tgt, idx, src, axis=0):
    return tgt.at[idx].add(src)

def _segment_sum(src, seg, n):
    return jax.ops.segment_sum(src, seg, n)
kernel_name = 'mk_perceiver_d2_seqx_r8_c49968'

def setup_inputs(seed: int=0):
    np.random.seed(seed)
    _w = jnp.asarray

    def _rec_inputs():
        import jax
        import jax.numpy as jnp
        _rk = jax.random.key(seed)
        x = 7.22e-05 + 1 * jax.random.normal(jax.random.fold_in(_rk, 1), (32, 64, 128), jnp.float32)
        _lenS = 64 - jax.random.randint(jax.random.fold_in(_rk, 7), (32,), 0, max(1, 64 // 4) + 1, jnp.int32)
        _lenS2 = 1601 - jax.random.randint(jax.random.fold_in(_rk, 8), (32,), 0, max(1, 1601 // 4) + 1, jnp.int32)
        _ctx_1024P = jax.random.normal(jax.random.fold_in(_rk, 11), (32, 16, 128), jnp.float32)
        _ctx_1024c = jax.random.dirichlet(jax.random.fold_in(_rk, 511), 0.3 * jnp.ones((16,), jnp.float32), (32, 1601))
        _ctx_1024t = jnp.einsum('bsk,bkd->bsd', _ctx_1024c, _ctx_1024P)
        _ctx_1024t = _ctx_1024t * jax.lax.rsqrt(jnp.mean(jnp.square(_ctx_1024t)) + 1e-12) * 0.953939
        ctx_1024 = 2.81802e-05 + 1.00001 * (_ctx_1024t + 0.3 * jax.random.normal(jax.random.fold_in(_rk, 611), (32, 1601, 128), jnp.float32))
        return (x, ctx_1024)
    x, ctx_1024 = _rec_inputs()

    def _L0_xattn_setup():
        import jax, jax.numpy as jnp
        import numpy as np
        B, NT, NM, C, H, FF = (8, 128, 256, 128, 8, 512)

        def _ln(x, g, b):
            m = x.mean(-1, keepdims=True)
            v = jnp.mean((x - m) ** 2, axis=-1, keepdims=True)
            return (x - m) / jnp.sqrt(v + 1e-05) * g + b
        key = jax.random.key(seed)
        ks = jax.random.split(key, 8)
        w = lambda k, shape, s=0.02: jax.random.normal(k, shape, dtype=jnp.float32) * s
        return {'tgt': jax.random.normal(ks[0], (B, NT, C), dtype=jnp.float32), 'memory': jax.random.normal(ks[1], (B, NM, C), dtype=jnp.float32), 'qkv_w': w(ks[2], (3 * C, C)), 'qkv_b': jnp.zeros((3 * C,), jnp.float32), 'sa_out_w': w(ks[3], (C, C)), 'sa_out_b': jnp.zeros((C,), jnp.float32), 'in_proj_w': w(ks[4], (3 * C, C)), 'in_proj_b': jnp.zeros((3 * C,), jnp.float32), 'mha_out_w': w(ks[5], (C, C)), 'mha_out_b': jnp.zeros((C,), jnp.float32), 'lin1_w': w(ks[6], (FF, C)), 'lin1_b': jnp.zeros((FF,), jnp.float32), 'lin2_w': w(ks[7], (C, FF)), 'lin2_b': jnp.zeros((C,), jnp.float32), 'ln1_g': jnp.ones((C,), jnp.float32), 'ln1_b': jnp.zeros((C,), jnp.float32), 'ln2_g': jnp.ones((C,), jnp.float32), 'ln2_b': jnp.zeros((C,), jnp.float32), 'ln3_g': jnp.ones((C,), jnp.float32), 'ln3_b': jnp.zeros((C,), jnp.float32)}
    _L0_xattn_all = _L0_xattn_setup()
    _L0_xattn_in = {k: v for k, v in _L0_xattn_all.items() if k in ('qkv_w', 'qkv_b', 'sa_out_w', 'sa_out_b', 'in_proj_w', 'in_proj_b', 'mha_out_w', 'mha_out_b', 'lin1_w', 'lin1_b', 'lin2_w', 'lin2_b', 'ln1_g', 'ln1_b', 'ln2_g', 'ln2_b', 'ln3_g', 'ln3_b')}
    del _L0_xattn_all

    def _L0_attn_setup():
        import jax, jax.numpy as jnp
        import numpy as np
        N_HEAD = 16
        PAGE_SIZE = 32
        ROPE_THETA = 10000.0

        def _rope_tables(T, D, dtype):
            inv = 1.0 / ROPE_THETA ** (np.arange(0, D, 2, dtype=np.float32) / D)
            ang = np.outer(np.arange(T, dtype=np.float32), inv)
            return (jnp.asarray(np.cos(ang), dtype), jnp.asarray(np.sin(ang), dtype))

        def _apply_rope(x, cos, sin):
            x1 = x[..., 0::2]
            x2 = x[..., 1::2]
            c = cos[None, :, None, :]
            s = sin[None, :, None, :]
            out = jnp.stack([x1 * c - x2 * s, x1 * s + x2 * c], axis=-1)
            return out.reshape(x.shape)
        key = jax.random.key(seed)
        ks = jax.random.split(key, 6)
        B, T, E = (2, 256, 128)
        L = E // 2
        sc = lambda fan: 1.0 / np.sqrt(fan)
        return {'x': jax.random.normal(ks[0], (B, T, E), jnp.float32), 'wq': jax.random.normal(ks[1], (E, E), jnp.float32) * sc(E), 'w_down': jax.random.normal(ks[2], (E, L), jnp.float32) * sc(E), 'wk_up': jax.random.normal(ks[3], (L, E), jnp.float32) * sc(L), 'wv_up': jax.random.normal(ks[4], (L, E), jnp.float32) * sc(L), 'wo': jax.random.normal(ks[5], (E, E), jnp.float32) * sc(E)}
    _L0_attn_all = _L0_attn_setup()
    _L0_attn_in = {k: v for k, v in _L0_attn_all.items() if k in ('wq', 'w_down', 'wk_up', 'wv_up', 'wo')}
    del _L0_attn_all

    def _L0_ffn_setup():
        import jax, jax.numpy as jnp
        import numpy as np
        H = 128
        I = 64
        E = 32
        TOP_K = 6
        N_GROUP = 8
        TOPK_GROUP = 4
        SCALE = 2.5
        N_SHARED = 2
        SI = I * N_SHARED
        B, S = (2, 128)
        key = jax.random.key(seed)
        ks = jax.random.split(key, 8)
        x = jax.random.normal(ks[0], (B, S, H), jnp.float32)
        gate_weight = jax.random.normal(ks[1], (E, H), jnp.float32) * 0.02
        e_score_correction_bias = jax.random.normal(ks[2], (E,), jnp.float32) * 0.01
        experts_gate_up = jax.random.normal(ks[3], (E, 2 * I, H), jnp.float32) * 0.02
        experts_down = jax.random.normal(ks[4], (E, H, I), jnp.float32) * 0.02
        shared_gate_w = jax.random.normal(ks[5], (SI, H), jnp.float32) * 0.02
        shared_up_w = jax.random.normal(ks[6], (SI, H), jnp.float32) * 0.02
        shared_down_w = jax.random.normal(ks[7], (H, SI), jnp.float32) * 0.02
        return {'x': x, 'gate_weight': gate_weight, 'e_score_correction_bias': e_score_correction_bias, 'experts_gate_up': experts_gate_up, 'experts_down': experts_down, 'shared_gate_w': shared_gate_w, 'shared_up_w': shared_up_w, 'shared_down_w': shared_down_w}
    _L0_ffn_all = _L0_ffn_setup()
    _L0_ffn_in = {k: v for k, v in _L0_ffn_all.items() if k in ('gate_weight', 'e_score_correction_bias', 'experts_gate_up', 'experts_down', 'shared_gate_w', 'shared_up_w', 'shared_down_w')}
    del _L0_ffn_all

    def _L1_xattn_setup():
        import jax, jax.numpy as jnp
        import numpy as np
        D_MODEL = 128
        N_HEADS = 16
        D_K = D_MODEL // N_HEADS
        key = jax.random.key(seed)
        ks = jax.random.split(key, 11)
        B, L, S = (2, 256, 256)
        scale = 1.0 / np.sqrt(D_MODEL)
        return {'x_q': jax.random.normal(ks[0], (B, L, D_MODEL), jnp.float32), 'x_k': jax.random.normal(ks[1], (B, S, D_MODEL), jnp.float32), 'x_v': jax.random.normal(ks[2], (B, S, D_MODEL), jnp.float32), 'W_Q': jax.random.normal(ks[3], (D_MODEL, D_MODEL), jnp.float32) * scale, 'b_Q': jax.random.normal(ks[4], (D_MODEL,), jnp.float32) * 0.01, 'W_K': jax.random.normal(ks[5], (D_MODEL, D_MODEL), jnp.float32) * scale, 'b_K': jax.random.normal(ks[6], (D_MODEL,), jnp.float32) * 0.01, 'W_V': jax.random.normal(ks[7], (D_MODEL, D_MODEL), jnp.float32) * scale, 'b_V': jax.random.normal(ks[8], (D_MODEL,), jnp.float32) * 0.01, 'W_O': jax.random.normal(ks[9], (D_MODEL, D_MODEL), jnp.float32) * scale, 'b_O': jax.random.normal(ks[10], (D_MODEL,), jnp.float32) * 0.01}
    _L1_xattn_all = _L1_xattn_setup()
    _L1_xattn_in = {k: v for k, v in _L1_xattn_all.items() if k in ('W_Q', 'b_Q', 'W_K', 'b_K', 'W_V', 'b_V', 'W_O', 'b_O')}
    del _L1_xattn_all

    def _L1_attn_setup():
        import jax, jax.numpy as jnp
        import numpy as np
        B, S, D, H, K = (2, 256, 128, 16, 16)
        key = jax.random.key(seed)
        ks = jax.random.split(key, 8)
        s = 0.02

        def w(k, shape):
            return s * jax.random.normal(k, shape, jnp.float32)
        return {'x': jax.random.normal(ks[0], (B, S, D), jnp.float32), 'Wq': w(ks[1], (D, D)), 'bq': jnp.zeros((D,), jnp.float32), 'Wk': w(ks[2], (D, D)), 'bk': jnp.zeros((D,), jnp.float32), 'Wv': w(ks[3], (D, D)), 'bv': jnp.zeros((D,), jnp.float32), 'Wo': w(ks[4], (D, D)), 'bo': jnp.zeros((D,), jnp.float32), 'Ws1': w(ks[5], (D, D // 2)), 'bs1': jnp.zeros((D // 2,), jnp.float32), 'Ws2': w(ks[6], (D // 2, 1)), 'bs2': jnp.zeros((1,), jnp.float32)}
    _L1_attn_all = _L1_attn_setup()
    _L1_attn_in = {k: v for k, v in _L1_attn_all.items() if k in ('Wq', 'bq', 'Wk', 'bk', 'Wv', 'bv', 'Wo', 'bo', 'Ws1', 'bs1', 'Ws2', 'bs2')}
    del _L1_attn_all

    def _L1_ffn_setup():
        import jax, jax.numpy as jnp
        import numpy as np
        DIM = 128
        DEPTH = 7
        PAR = 8
        N_NODES = 2 ** (DEPTH + 1) - 1
        WIDTH = PAR * N_NODES
        key = jax.random.key(seed)
        k1, k2, k3, k4 = jax.random.split(key, 4)
        init_k = float(np.sqrt(1.0 / DIM))
        init_k2 = float(np.sqrt(1.0 / ((DEPTH + 1) * PAR)))
        oldx = jax.random.normal(k1, (4, 256, DIM), dtype=jnp.float32)
        W_in = jax.random.uniform(k2, (WIDTH, DIM), jnp.float32, -init_k, init_k)
        b_in = jax.random.uniform(k3, (WIDTH,), jnp.float32, -init_k, init_k)
        W_out = jax.random.uniform(k4, (DIM, WIDTH), jnp.float32, -init_k2, init_k2)
        return {'oldx': oldx, 'W_in': W_in, 'b_in': b_in, 'W_out': W_out}
    _L1_ffn_all = _L1_ffn_setup()
    _L1_ffn_in = {k: v for k, v in _L1_ffn_all.items() if k in ('W_in', 'b_in', 'W_out')}
    del _L1_ffn_all
    return {'x': x, 'ctx_1024': ctx_1024, 'L0_xattn_qkv_w': _L0_xattn_in['qkv_w'], 'L0_xattn_qkv_b': _L0_xattn_in['qkv_b'], 'L0_xattn_sa_out_w': _L0_xattn_in['sa_out_w'], 'L0_xattn_sa_out_b': _L0_xattn_in['sa_out_b'], 'L0_xattn_in_proj_w': _L0_xattn_in['in_proj_w'], 'L0_xattn_in_proj_b': _L0_xattn_in['in_proj_b'], 'L0_xattn_mha_out_w': _L0_xattn_in['mha_out_w'], 'L0_xattn_mha_out_b': _L0_xattn_in['mha_out_b'], 'L0_xattn_lin1_w': _L0_xattn_in['lin1_w'], 'L0_xattn_lin1_b': _L0_xattn_in['lin1_b'], 'L0_xattn_lin2_w': _L0_xattn_in['lin2_w'], 'L0_xattn_lin2_b': _L0_xattn_in['lin2_b'], 'L0_xattn_ln1_g': _L0_xattn_in['ln1_g'], 'L0_xattn_ln1_b': _L0_xattn_in['ln1_b'], 'L0_xattn_ln2_g': _L0_xattn_in['ln2_g'], 'L0_xattn_ln2_b': _L0_xattn_in['ln2_b'], 'L0_xattn_ln3_g': _L0_xattn_in['ln3_g'], 'L0_xattn_ln3_b': _L0_xattn_in['ln3_b'], 'L0_attn_wq': _L0_attn_in['wq'], 'L0_attn_w_down': _L0_attn_in['w_down'], 'L0_attn_wk_up': _L0_attn_in['wk_up'], 'L0_attn_wv_up': _L0_attn_in['wv_up'], 'L0_attn_wo': _L0_attn_in['wo'], 'L0_ffn_gate_weight': _L0_ffn_in['gate_weight'], 'L0_ffn_e_score_correction_bias': _L0_ffn_in['e_score_correction_bias'], 'L0_ffn_experts_gate_up': _L0_ffn_in['experts_gate_up'], 'L0_ffn_experts_down': _L0_ffn_in['experts_down'], 'L0_ffn_shared_gate_w': _L0_ffn_in['shared_gate_w'], 'L0_ffn_shared_up_w': _L0_ffn_in['shared_up_w'], 'L0_ffn_shared_down_w': _L0_ffn_in['shared_down_w'], 'L1_xattn_W_Q': _L1_xattn_in['W_Q'], 'L1_xattn_b_Q': _L1_xattn_in['b_Q'], 'L1_xattn_W_K': _L1_xattn_in['W_K'], 'L1_xattn_b_K': _L1_xattn_in['b_K'], 'L1_xattn_W_V': _L1_xattn_in['W_V'], 'L1_xattn_b_V': _L1_xattn_in['b_V'], 'L1_xattn_W_O': _L1_xattn_in['W_O'], 'L1_xattn_b_O': _L1_xattn_in['b_O'], 'L1_attn_Wq': _L1_attn_in['Wq'], 'L1_attn_bq': _L1_attn_in['bq'], 'L1_attn_Wk': _L1_attn_in['Wk'], 'L1_attn_bk': _L1_attn_in['bk'], 'L1_attn_Wv': _L1_attn_in['Wv'], 'L1_attn_bv': _L1_attn_in['bv'], 'L1_attn_Wo': _L1_attn_in['Wo'], 'L1_attn_bo': _L1_attn_in['bo'], 'L1_attn_Ws1': _L1_attn_in['Ws1'], 'L1_attn_bs1': _L1_attn_in['bs1'], 'L1_attn_Ws2': _L1_attn_in['Ws2'], 'L1_attn_bs2': _L1_attn_in['bs2'], 'L1_ffn_W_in': _L1_ffn_in['W_in'], 'L1_ffn_b_in': _L1_ffn_in['b_in'], 'L1_ffn_W_out': _L1_ffn_in['W_out']}

def reference(x, ctx_1024, L0_xattn_qkv_w, L0_xattn_qkv_b, L0_xattn_sa_out_w, L0_xattn_sa_out_b, L0_xattn_in_proj_w, L0_xattn_in_proj_b, L0_xattn_mha_out_w, L0_xattn_mha_out_b, L0_xattn_lin1_w, L0_xattn_lin1_b, L0_xattn_lin2_w, L0_xattn_lin2_b, L0_xattn_ln1_g, L0_xattn_ln1_b, L0_xattn_ln2_g, L0_xattn_ln2_b, L0_xattn_ln3_g, L0_xattn_ln3_b, L0_attn_wq, L0_attn_w_down, L0_attn_wk_up, L0_attn_wv_up, L0_attn_wo, L0_ffn_gate_weight, L0_ffn_e_score_correction_bias, L0_ffn_experts_gate_up, L0_ffn_experts_down, L0_ffn_shared_gate_w, L0_ffn_shared_up_w, L0_ffn_shared_down_w, L1_xattn_W_Q, L1_xattn_b_Q, L1_xattn_W_K, L1_xattn_b_K, L1_xattn_W_V, L1_xattn_b_V, L1_xattn_W_O, L1_xattn_b_O, L1_attn_Wq, L1_attn_bq, L1_attn_Wk, L1_attn_bk, L1_attn_Wv, L1_attn_bv, L1_attn_Wo, L1_attn_bo, L1_attn_Ws1, L1_attn_bs1, L1_attn_Ws2, L1_attn_bs2, L1_ffn_W_in, L1_ffn_b_in, L1_ffn_W_out):
    import jax
    import jax.numpy as jnp

    def _L0_xattn_ref(tgt, memory, qkv_w, qkv_b, sa_out_w, sa_out_b, in_proj_w, in_proj_b, mha_out_w, mha_out_b, lin1_w, lin1_b, lin2_w, lin2_b, ln1_g, ln1_b, ln2_g, ln2_b, ln3_g, ln3_b):
        import jax, jax.numpy as jnp
        import numpy as np
        B, NT, NM, C, H, FF = (8, 128, 256, 128, 8, 512)

        def _ln(x, g, b):
            m = x.mean(-1, keepdims=True)
            v = jnp.mean((x - m) ** 2, axis=-1, keepdims=True)
            return (x - m) / jnp.sqrt(v + 1e-05) * g + b
        Bx, N, Cx = tgt.shape
        qkv = tgt @ qkv_w.T + qkv_b
        q, k, v = jnp.split(qkv, 3, axis=-1)
        scores = jnp.einsum('bnc,bmc->bnm', q, k) * jnp.sqrt(jnp.float32(Cx))
        diag = jnp.eye(N, dtype=bool)
        scores = jnp.where(diag[None, :, :], scores, -jnp.inf)
        attn = jax.nn.softmax(scores, axis=-1)
        sa = jnp.einsum('bnm,bmc->bnc', attn, v) @ sa_out_w.T + sa_out_b
        x = _ln(tgt + sa, ln1_g, ln1_b)
        d = Cx // H
        wq, wk, wv = jnp.split(in_proj_w, 3, axis=0)
        bq, bk, bv = jnp.split(in_proj_b, 3, axis=0)
        qh = (x @ wq.T + bq).reshape(Bx, N, H, d).transpose(0, 2, 1, 3)
        kh = (memory @ wk.T + bk).reshape(Bx, -1, H, d).transpose(0, 2, 1, 3)
        vh = (memory @ wv.T + bv).reshape(Bx, -1, H, d).transpose(0, 2, 1, 3)
        a = jax.nn.softmax(jnp.einsum('bhnd,bhmd->bhnm', qh, kh) / jnp.sqrt(jnp.float32(d)), axis=-1)
        ca = jnp.einsum('bhnm,bhmd->bhnd', a, vh).transpose(0, 2, 1, 3).reshape(Bx, N, Cx)
        ca = ca @ mha_out_w.T + mha_out_b
        x = _ln(x + ca, ln2_g, ln2_b)
        ff = jax.nn.relu(x @ lin1_w.T + lin1_b) @ lin2_w.T + lin2_b
        return _ln(x + ff, ln3_g, ln3_b)

    def _L0_attn_ref(x, wq, w_down, wk_up, wv_up, wo):
        import jax, jax.numpy as jnp
        import numpy as np
        N_HEAD = 16
        PAGE_SIZE = 32
        ROPE_THETA = 10000.0

        def _rope_tables(T, D, dtype):
            inv = 1.0 / ROPE_THETA ** (np.arange(0, D, 2, dtype=np.float32) / D)
            ang = np.outer(np.arange(T, dtype=np.float32), inv)
            return (jnp.asarray(np.cos(ang), dtype), jnp.asarray(np.sin(ang), dtype))

        def _apply_rope(x, cos, sin):
            x1 = x[..., 0::2]
            x2 = x[..., 1::2]
            c = cos[None, :, None, :]
            s = sin[None, :, None, :]
            out = jnp.stack([x1 * c - x2 * s, x1 * s + x2 * c], axis=-1)
            return out.reshape(x.shape)
        B, T, E = x.shape
        H = N_HEAD
        D = E // H
        q = (x @ wq).reshape(B, T, H, D)
        lat = x @ w_down
        k = (lat @ wk_up).reshape(B, T, H, D)
        v = (lat @ wv_up).reshape(B, T, H, D)
        cos, sin = _rope_tables(T, D, x.dtype)
        q = _apply_rope(q, cos, sin)
        k = _apply_rope(k, cos, sin)
        scale = 1.0 / jnp.sqrt(jnp.asarray(D, x.dtype))
        scores = jnp.einsum('bqhd,bkhd->bhqk', q, k) * scale
        pages = jnp.arange(T) // PAGE_SIZE
        allowed = pages[None, :] <= pages[:, None]
        scores = jnp.where(allowed[None, None], scores, jnp.finfo(scores.dtype).min)
        attn = jax.nn.softmax(scores, axis=-1)
        out = jnp.einsum('bhqk,bkhd->bqhd', attn, v).reshape(B, T, E)
        return out @ wo

    def _L0_ffn_ref(x, gate_weight, e_score_correction_bias, experts_gate_up, experts_down, shared_gate_w, shared_up_w, shared_down_w):
        import jax, jax.numpy as jnp
        import numpy as np
        H = 128
        I = 64
        E = 32
        TOP_K = 6
        N_GROUP = 8
        TOPK_GROUP = 4
        SCALE = 2.5
        N_SHARED = 2
        SI = I * N_SHARED
        B, S = (2, 128)
        b, s, h = x.shape
        xf = x.reshape(-1, h)
        T = xf.shape[0]
        logits = xf.astype(jnp.float32) @ gate_weight.astype(jnp.float32).T
        scores = jax.nn.sigmoid(logits)
        sfc = scores + e_score_correction_bias[None, :]
        gs = E // N_GROUP
        group_scores = sfc.reshape(T, N_GROUP, gs).max(axis=-1)
        _, gidx = jax.lax.top_k(group_scores, TOPK_GROUP)
        gmask = jnp.zeros((T, N_GROUP), bool).at[jnp.arange(T)[:, None], gidx].set(True)
        smask = jnp.repeat(gmask, gs, axis=1)
        masked = jnp.where(smask, sfc, 0.0)
        _, topk_idx = jax.lax.top_k(masked, TOP_K)
        tw = jnp.take_along_axis(scores, topk_idx, axis=1)
        tw = tw / (tw.sum(-1, keepdims=True) + 1e-20)
        tw = (tw * SCALE).astype(xf.dtype)
        combine = jnp.zeros((T, E), xf.dtype).at[jnp.arange(T)[:, None], topk_idx].add(tw)

        def expert_step(acc, inp):
            gu, dn, c = inp
            g = xf @ gu[:I].T
            u = xf @ gu[I:].T
            o = jax.nn.silu(g) * u @ dn.T
            return (acc + c[:, None] * o, None)
        routed, _ = jax.lax.scan(expert_step, jnp.zeros_like(xf), (experts_gate_up, experts_down, combine.T))
        sh = jax.nn.silu(xf @ shared_gate_w.T) * (xf @ shared_up_w.T)
        shared_out = sh @ shared_down_w.T
        return (routed + shared_out).reshape(b, s, h)

    def _L1_xattn_ref(x_q, x_k, x_v, W_Q, b_Q, W_K, b_K, W_V, b_V, W_O, b_O):
        import jax, jax.numpy as jnp
        import numpy as np
        D_MODEL = 128
        N_HEADS = 16
        D_K = D_MODEL // N_HEADS
        B, L, _ = x_q.shape
        S = x_k.shape[1]
        H, dk = (N_HEADS, D_K)
        Q = (x_q @ W_Q + b_Q).reshape(B, L, H, dk).transpose(0, 2, 1, 3)
        K = (x_k @ W_K + b_K).reshape(B, S, H, dk).transpose(0, 2, 1, 3)
        V = (x_v @ W_V + b_V).reshape(B, S, H, dk).transpose(0, 2, 1, 3)
        scores = jnp.einsum('bhld,bhsd->bhls', Q, K) / jnp.sqrt(jnp.float32(dk))
        attn = jax.nn.softmax(scores, axis=-1)
        ctx = jnp.einsum('bhls,bhsd->bhld', attn, V)
        ctx = ctx.transpose(0, 2, 1, 3).reshape(B, L, H * dk)
        out = ctx @ W_O + b_O
        return out

    def _L1_attn_ref(x, Wq, bq, Wk, bk, Wv, bv, Wo, bo, Ws1, bs1, Ws2, bs2):
        import jax, jax.numpy as jnp
        import numpy as np
        B, S, D, H, K = (2, 256, 128, 16, 16)
        Bx, Sx, Dx = x.shape
        Dh = Dx // H
        q = (x @ Wq + bq).reshape(Bx, Sx, H, Dh).transpose(0, 2, 1, 3)
        k = (x @ Wk + bk).reshape(Bx, Sx, H, Dh).transpose(0, 2, 1, 3)
        v = (x @ Wv + bv).reshape(Bx, Sx, H, Dh).transpose(0, 2, 1, 3)
        scores = jnp.einsum('bhqd,bhkd->bhqk', q, k) / np.float32(np.sqrt(Dh))
        imp = jax.nn.sigmoid(jax.nn.relu(x @ Ws1 + bs1) @ Ws2 + bs2)[..., 0]
        _, idx = jax.lax.top_k(imp, K)
        sel = jnp.zeros((Bx, Sx), bool).at[jnp.arange(Bx)[:, None], idx].set(True)
        m2 = sel[:, :, None] | sel[:, None, :]
        masked = jnp.where(m2[:, None, :, :], scores, -jnp.inf)
        w = jax.nn.softmax(masked, axis=-1)
        att = jnp.einsum('bhqk,bhkd->bhqd', w, v).transpose(0, 2, 1, 3).reshape(Bx, Sx, Dx)
        return att @ Wo + bo

    def _L1_ffn_ref(oldx, W_in, b_in, W_out):
        import jax, jax.numpy as jnp
        import numpy as np
        DIM = 128
        DEPTH = 7
        PAR = 8
        N_NODES = 2 ** (DEPTH + 1) - 1
        WIDTH = PAR * N_NODES
        x = oldx.reshape(-1, DIM)
        B = x.shape[0]
        logits = x @ W_in.T + b_in
        decisions = (logits > 0).astype(jnp.int32).reshape(B, PAR, N_NODES)
        acts = jax.nn.silu(logits).reshape(B, PAR, N_NODES)
        current = jnp.zeros((B, PAR), dtype=jnp.int32)
        dmap = jax.nn.one_hot(current, N_NODES, dtype=acts.dtype)
        for d in range(DEPTH):
            cur_platform = 2 ** d - 1
            next_platform = 2 ** (d + 1) - 1
            moves = jnp.take_along_axis(decisions, current[..., None], axis=2)[..., 0]
            current = (current - cur_platform) * 2 + moves + next_platform
            dmap = dmap + jax.nn.one_hot(current, N_NODES, dtype=acts.dtype)
        masked = acts * jax.lax.stop_gradient(dmap)
        out = masked.reshape(B, WIDTH) @ W_out.T
        return out.reshape(oldx.shape)
    x = x + _L0_xattn_ref(_layernorm(x, axis=-1), ctx_1024, L0_xattn_qkv_w, L0_xattn_qkv_b, L0_xattn_sa_out_w, L0_xattn_sa_out_b, L0_xattn_in_proj_w, L0_xattn_in_proj_b, L0_xattn_mha_out_w, L0_xattn_mha_out_b, L0_xattn_lin1_w, L0_xattn_lin1_b, L0_xattn_lin2_w, L0_xattn_lin2_b, L0_xattn_ln1_g, L0_xattn_ln1_b, L0_xattn_ln2_g, L0_xattn_ln2_b, L0_xattn_ln3_g, L0_xattn_ln3_b)
    x = x + _L0_attn_ref(_layernorm(x, axis=-1), L0_attn_wq, L0_attn_w_down, L0_attn_wk_up, L0_attn_wv_up, L0_attn_wo)
    x = x + _L0_ffn_ref(_layernorm(x, axis=-1), L0_ffn_gate_weight, L0_ffn_e_score_correction_bias, L0_ffn_experts_gate_up, L0_ffn_experts_down, L0_ffn_shared_gate_w, L0_ffn_shared_up_w, L0_ffn_shared_down_w)
    x = x + _L1_xattn_ref(_layernorm(x, axis=-1), ctx_1024, ctx_1024, L1_xattn_W_Q, L1_xattn_b_Q, L1_xattn_W_K, L1_xattn_b_K, L1_xattn_W_V, L1_xattn_b_V, L1_xattn_W_O, L1_xattn_b_O)
    x = x + _L1_attn_ref(_layernorm(x, axis=-1), L1_attn_Wq, L1_attn_bq, L1_attn_Wk, L1_attn_bk, L1_attn_Wv, L1_attn_bv, L1_attn_Wo, L1_attn_bo, L1_attn_Ws1, L1_attn_bs1, L1_attn_Ws2, L1_attn_bs2)
    x = x + _L1_ffn_ref(_layernorm(x, axis=-1), L1_ffn_W_in, L1_ffn_b_in, L1_ffn_W_out)
    return x

_drawn_inputs = setup_inputs


def setup_inputs(seed=0):
    import zlib

    import numpy as np

    out = dict(_drawn_inputs(seed))
    spreads = {'L0_xattn_qkv_b': (0.0, 0.451),
     'L0_xattn_sa_out_b': (0.0, 0.1),
     'L0_xattn_in_proj_b': (0.0, 0.435),
     'L0_xattn_mha_out_b': (0.0, 0.1),
     'L0_xattn_lin1_b': (0.0, 0.344),
     'L0_xattn_lin2_b': (0.0, 0.1),
     'L0_xattn_ln1_g': (1.0, 0.2),
     'L0_xattn_ln1_b': (0.0, 0.1),
     'L0_xattn_ln2_g': (1.0, 0.2),
     'L0_xattn_ln2_b': (0.0, 0.1),
     'L0_xattn_ln3_g': (1.0, 0.2),
     'L0_xattn_ln3_b': (0.0, 0.1),
     'L1_attn_bq': (0.0, 0.8),
     'L1_attn_bk': (0.0, 2.0),
     'L1_attn_bv': (0.0, 0.448),
     'L1_attn_bo': (0.0, 0.403),
     'L1_attn_bs1': (0.0, 0.8)}
    factors = {'L0_xattn_in_proj_w': 2.952,
     'L0_ffn_gate_weight': 8.0,
     'L0_ffn_e_score_correction_bias': 8.0,
     'L0_ffn_experts_gate_up': 8.0,
     'L0_ffn_experts_down': 8.0,
     'L0_ffn_shared_gate_w': 7.845,
     'L0_ffn_shared_up_w': 8.0,
     'L0_ffn_shared_down_w': 8.0,
     'L1_xattn_b_Q': 64.0,
     'L1_xattn_b_K': 64.0,
     'L1_xattn_b_V': 20.007,
     'L1_xattn_b_O': 20.536,
     'L1_attn_Wq': 8.0,
     'L1_attn_Wk': 8.0,
     'L1_attn_Wv': 4.222,
     'L1_attn_Wo': 2.905,
     'L1_attn_Ws1': 6.153,
     'L1_attn_Ws2': 6.57,
     'L1_ffn_b_in': 4.546}
    for name, (base, spread) in spreads.items():
        noise = np.random.default_rng([zlib.crc32(name.encode()), seed]).standard_normal(out[name].shape)
        drawn = base * np.exp(spread * noise) if base else spread * noise
        out[name] = jnp.asarray(drawn.astype(out[name].dtype))
    for name, factor in factors.items():
        out[name] = (out[name] * factor).astype(out[name].dtype)
    return out
```

```python
from contextlib import ExitStack

import numpy as np

import concourse.bass as bass
from concourse import mybir

ALU = mybir.AluOpType
ACT = mybir.ActivationFunctionType
AX = mybir.AxisListType
F32 = mybir.dt.float32
BF16 = mybir.dt.bfloat16

B, S, D, NK = 32, 64, 128, 1601
N = B * S
CH = 512
NC = N // CH
EPS = 1e-5
MASKED = -1e30
E, EI, TOPK, NG, TOPG = 32, 64, 6, 8, 4
GS = E // NG
ROUTE_SCALE = 2.5
TREES, NODES, INNER, LEAVES = 8, 255, 127, 128
FF = 512
SEL_K = 16
RAW = 96
ROWS = 98
TILE = 128
KTILES = [(t * TILE, min(TILE, NK - t * TILE)) for t in range(-(-NK // TILE))]
BIG = 3e38


class Attention:

    def __init__(self, name, heads, cross, masked=False, values_k=D):
        self.name, self.H, self.cross, self.masked, self.values_k = name, heads, cross, masked, values_k
        self.d = D // heads
        self.hg = heads // 4
        self.W = heads * S
        per = 32 // (self.d + 1)
        if heads == 16:
            sizes = [3, 3, 3, 3, 2, 2]
        else:
            sizes = [1] * 8
        assert max(sizes) <= per
        self.groups, h, v = [], 0, 0
        bases = {}
        col = 0
        for i, n in enumerate(sizes):
            r, quad = divmod(i, 4)
            if r not in bases:
                bases[r] = col
                col += n * S
            self.groups.append((r, quad, h, n, v, bases[r]))
            h += n
            v += n * (self.d + 1)
        self.rounds = len(bases)
        self.bases = bases
        self.NV, self.NO = v, col
        self.blocks = [sizes[0], sizes[4]]
        self.tiles = KTILES if cross else [(0, S)]
        self.keys = NK if cross else S
        per_exp = 1024 // self.W
        self.exps = [list(range(i, min(i + per_exp, len(self.tiles)))) for i in range(0, len(self.tiles), per_exp)]
        if cross and len(self.exps[-1]) > 1:
            raise ValueError("the short key tile has an Exp of its own")
        self.NE = len(self.exps)
        self.units = heads // 2
        q4 = -(-NK // 4)
        self.kchunks = [(c * q4, min(q4, NK - c * q4)) for c in range(4)] if cross else []
        self.vjobs = [list(range(i, min(i + 3, len(self.tiles)))) for i in range(0, len(self.tiles), 3)]
        if cross:
            self.mjobs = [[(u, c0, n)] for u in range(self.units) for c0, n in self.kchunks]
        else:
            self.mjobs = [[(u, 0, S) for u in range(self.units)]]
        self.rjobs = self.W // 512
        self.jobs = ([("K", j) for j in range(len(self.kchunks))] + [("V", j) for j in range(len(self.vjobs))]
                     + [("M", j) for j in range(len(self.mjobs))] + [("R", j) for j in range(self.rjobs)])
        self.krows = ROWS + 1 if masked else ROWS
        self.scale = 1.0 / float(np.sqrt(self.d))

    def steps(self):
        K, V, M, R = ([j for j in self.jobs if j[0] == k] for k in "KVMR")
        if not self.cross:
            prep = V + M + [("Z", 0)] + R
            return [("S", 0), ("E", 0)], prep, [("P", 0), ("O", 0)]
        n = self.NE
        early = 1 + (n > 8)
        parts = [[] for _ in range(n)]
        parts[0] = K
        late = V[2:]
        parts[1] = V[:1] if early == 2 else V[:2]
        if early == 2:
            parts[2] = V[1:2]
        first, last = early + 1, n - 2
        for i, m in enumerate(M):
            parts[first + i * (last - first + 1) // len(M)].append(m)
        parts[n - 1] = [("Z", 0)] + late
        return parts, R

    def merged(self, main, prep):
        if not self.cross:
            a, p, z = self.steps()
            return (a if main else []) + (p if prep else []) + (z if main else [])
        parts, R = self.steps()
        out = [("S", 0)] if main else []
        for e in range(self.NE):
            if main:
                out.append(("E", e))
                if e + 1 < self.NE:
                    out.append(("S", e + 1))
            if prep:
                out += parts[e]
            if main:
                out.append(("P", e))
        if main:
            out.append(("O", 0))
        if prep:
            out += R
        return out

    def order(self):
        return [s for s in self.merged(False, True) if s[0] in "KVMR"]


WORK = 3


def bank_plan(att):
    order = att.order()
    count = [0] * WORK
    plan = {}
    for u in range(2):
        for j, job in enumerate(order):
            bank = (u * len(order) + j) % WORK
            plan[(u, job)] = (bank, count[bank], j)
            count[bank] += 1
    return plan, count, len(order)


XA0 = Attention("xa0", 8, True)
SA0 = Attention("sa0", 16, False, masked=True, values_k=64)
XA1 = Attention("xa1", 16, True)
SA1 = Attention("sa1", 16, False, masked=True)


W_PARTS = [("mean", D), ("ones", D), ("c_q", D), ("c_k", D), ("c_v", D), ("c_o", D), ("c_wq", D), ("bias", 64),
           ("m_sel", 8),
           ("xa0_k", D), ("xa0_v", XA0.NV), ("xa0_vb", XA0.NV), ("xa0_o", 2 * D), ("xa0_den", 2 * D),
           ("lin1", FF), ("lin2", FF), ("rope", 2 * S), ("sa0_q", 2 * D), ("down", 64), ("sa0_k", 2 * D),
           ("sa0_v", SA0.NV), ("sa0_vb", SA0.NV), ("sa0_o", 2 * D), ("den16", 2 * D),
           ("gate", E), ("gate_b", E), ("shared", 3 * D), ("ident", D),
           ("xa1_q", D), ("xa1_k", D), ("xa1_v", XA1.NV), ("xa1_vb", XA1.NV), ("xa1_o", 2 * D),
           ("sa1_q", D), ("sa1_k", D), ("sa1_v", SA1.NV), ("sa1_vb", SA1.NV), ("sa1_o", 2 * D),
           ("ws1", 64), ("ws2", 1)]
W_AT, _o = {}, 0
for _n, _w in W_PARTS:
    W_AT[_n] = (_o, _w)
    _o += _w
W_COLS = _o
B_PARTS = [("ident16", D), ("tree", INNER + LEAVES + 1), ("hm2", 2), ("hm4", 4), ("krow", 4 * S), ("qrow", 16 * S)]
B_AT, _o = {}, 0
for _n, _w in B_PARTS:
    B_AT[_n] = (_o, _w)
    _o += _w
B_COLS = _o
BIASES = ["c_bq", "c_bk", "c_bv", "c_bo", "g1", "b1", "bq0", "bk0", "bo0", "g2", "b2", "l1b0", "l1b1", "l1b2", "l1b3",
          "l2b", "g3", "b3", "bq1", "bk1", "bo1", "s_bq", "s_bk", "s_bo", "bs1", "bs2", "thr0", "thr1"]
BIAS_AT = {n: i for i, n in enumerate(BIASES)}
assert len(BIASES) <= 64


def bass_perceiver_kernel(nc, xT, ctxT, wpack, bpack, experts, picks, trees, outT, stop=99):
    ctx = ExitStack()
    with ctx:
        def sb(name, shape, dt):
            return ctx.enter_context(nc.sbuf_tensor(name, shape, dt))

        sems = {}

        def sem(name):
            if name not in sems:
                sems[name] = ctx.enter_context(nc.semaphore(name))
            return sems[name]

        ps = ctx.enter_context(nc.psum_tensor("ps", [128, 8, 512], F32))

        W = sb("W", [128, W_COLS], F32)
        WB = sb("WB", [128, B_COLS], BF16)
        X = sb("X", [128, N], F32)
        T = sb("T", [128, N], F32)
        ABO = sb("ABO", [128, 10240], F32)
        A = ABO[:, 0:N]
        Bt = ABO[:, N:2 * N]
        C = sb("C", [128, N], F32)
        QS = sb("QS", [128, 4, N], BF16)
        HL = sb("HL", [128, 2, N], BF16)
        CT = sb("CT", [128, 2, NK], F32)
        KST = sb("KST", [128, 2, 4, NK], BF16)
        KSA = KST[:, :, :, :].rearrange("p a g k -> p (a g k)")[:, 0:4 * N].rearrange("p (g n) -> p g n", g=4)
        KSS = sb("KSS", [128, 2, 4, S], BF16)
        V = sb("V", [128, 2, len(KTILES), 144], F32)
        QW = sb("QW", [128, 2, 16 * S], BF16)
        QSL = sb("QSL", [128, 2, 4, S], BF16)
        Pb = sb("Pb", [128, 2, 1024], F32)
        OE = sb("OE", [128, 2, 320], F32)
        MX = sb("MX", [128, 2, 32], F32)
        MG = sb("MG", [128, 2, 8], F32)
        MH = sb("MH", [128, 2, 8, 2], BF16)
        epst = sb("epst", [128, 1], F32)
        DEC = sb("DEC", [128, 2, CH], BF16)
        NSB = sb("NSB", [B, 2, S], BF16)

        def w(name, a=0, b=None, rows=128):
            o, n = W_AT[name]
            return W[0:rows, o + a:o + (n if b is None else b)]

        def wb(name, rows=128):
            o, n = B_AT[name]
            return WB[0:rows, o:o + n]

        def bias(name, rows=128):
            o = W_AT["bias"][0] + BIAS_AT[name]
            return W[0:rows, o:o + 1]

        def ck(t, c):
            return t[:, c * CH:(c + 1) * CH]

        def hi_bank(c):
            return ps[:, 4 + c, :]

        def lo_bank(c):
            return ps[:, c, :]


        def layernorm(role, eng, call, src, dst, ready, gain=None, shift=None):
            mean_s, xc_s, sq_s, var_s, sd_s, rc_s, scaled_s, out_s = (
                sem(f"ln_{k}") for k in ("mean", "centred", "square", "var", "dev", "recip", "scaled", "out"))
            n = call * NC
            SQ, SD = C, C
            if role == "pe":
                for c in range(NC):
                    if ready is not None:
                        eng.wait_ge(ready[0], ready[1] + c)
                    nc.tensor.matmul(lo_bank(c), w("mean"), ck(src, c), start=True, stop=True).then_inc(mean_s, 1)
                for c in range(NC):
                    eng.wait_ge(sq_s, n + c + 1)
                    nc.tensor.matmul(hi_bank(c), w("mean"), ck(SQ, c), start=True, stop=True).then_inc(var_s, 1)
            if role == "dve":
                for c in range(NC):
                    eng.wait_ge(mean_s, n + c + 1)
                    nc.vector.tensor_tensor(ck(dst, c), ck(src, c), lo_bank(c), ALU.subtract).then_inc(xc_s, 1)
                for c in range(NC):
                    eng.wait_ge(sd_s, n + c + 1)
                    nc.vector.reciprocal(ck(SD, c), ck(SD, c)).then_inc(rc_s, 1)
                    eng.wait_ge(rc_s, n + c + 1)
                    if gain is None:
                        nc.vector.tensor_tensor(ck(dst, c), ck(dst, c), ck(SD, c), ALU.mult).then_inc(out_s, 1)
                    else:
                        nc.vector.scalar_tensor_tensor(ck(dst, c), ck(dst, c), bias(gain), ck(SD, c),
                                                       ALU.mult, ALU.mult).then_inc(scaled_s, 1)
                        eng.wait_ge(scaled_s, n - NC + c + 1)
                        nc.vector.tensor_scalar(ck(dst, c), ck(dst, c), bias(shift), None, ALU.add).then_inc(out_s, 1)
            if role == "act":
                for c in range(NC):
                    eng.wait_ge(xc_s, n + c + 1)
                    nc.scalar.activation(ck(SQ, c), ck(dst, c), ACT.Square).then_inc(sq_s, 1)
                for c in range(NC):
                    eng.wait_ge(var_s, n + c + 1)
                    nc.scalar.activation(ck(SD, c), hi_bank(c), ACT.Sqrt, bias=epst[:, 0:1]).then_inc(sd_s, 1)
            return out_s, n + 1

        def split_rows(role, eng, call, done, stacked, kind):
            stacked_s = sem("stacked")
            if role == "sp":
                eng.wait_ge(done[0], done[1] + NC - 1)
                order = (0, 0, 1) if kind == "q" else (0, 1, 0)
                for g in range(4):
                    for p, part in enumerate(order):
                        eng.dma_start(stacked[32 * p:32 * p + 32, g, :],
                                      HL[32 * g:32 * g + 32, part, :]).then_inc(stacked_s, 16)
            return stacked_s, (call + 1) * 12 * 16

        def project_split(role, eng, call, weights, bname, ready):
            pe_s, hi_s, lo_s = sem("proj_sum"), sem("proj_hi"), sem("proj_lo")
            n = call * NC
            for c in range(NC):
                if role == "pe":
                    eng.wait_ge(ready[0], ready[1] + c)
                    nc.tensor.matmul(lo_bank(c), weights, ck(T, c), start=True, stop=True).then_inc(pe_s, 1)
                if role == "act":
                    eng.wait_ge(pe_s, n + c + 1)
                    nc.scalar.activation(ck(HL[:, 0, :], c), lo_bank(c), ACT.Identity,
                                         bias=bias(bname)).then_inc(hi_s, 1)
                if role == "dve":
                    eng.wait_ge(hi_s, n + c + 1)
                    nc.vector.scalar_tensor_tensor(ck(HL[:, 1, :], c), lo_bank(c), bias(bname), ck(HL[:, 0, :], c),
                                                   ALU.add, ALU.subtract).then_inc(lo_s, 1)
            return lo_s, n + 1


        def attention(role, eng, att, q_ready, src):
            plan, per_pair, n_jobs = bank_plan(att)
            t = att.name
            kind = t if att.cross else "self"
            W_, hg = att.W, att.hg
            Oall = (ABO[:, 6144:6144 + B * att.NO] if att.H == 8 else ABO[:, 0:B * att.NO]).rearrange(
                "p (b o) -> p b o", b=B)
            kst = KST if att.cross else KSS
            s_ctx = [sem(f"{kind}_ctx{i}") for i in range(2)]
            s_q = [sem(f"{kind}_q{i}") for i in range(2)]
            s_kst = [sem(f"{kind}_kst{i}") for i in range(2)]
            s_oout = [sem(f"{kind}_oout{i}") for i in range(2)]
            filled = sem(f"{kind}_filled")
            free = [sem(f"{kind}_free{i}") for i in range(WORK)]
            khi, mx, negm = sem(f"{kind}_khi"), sem(f"{kind}_mx"), sem(f"{kind}_negm")
            qbuilt, scores, exps, pv, oev = (sem(f"{kind}_{k}") for k in ("qbuilt", "scores", "exps", "pv", "oev"))
            ready = sem(f"{kind}_ready")
            mask_dmas = 1 if (att.masked and att is SA1) else 0
            kst_dmas = 3 if att.cross else 1 + mask_dmas
            q_dmas = 1 + mask_dmas

            counted = {}
            if att is SA1:
                for name, n in (("filled", n_jobs), ("mx", 1), ("negm", 1), ("qz", 1), ("qbuilt", 1), ("scores", att.NE),
                                ("exps", att.NE), ("pv", att.NE), ("oev", 1)):
                    counted[f"self_{name}"] = B * n
                for name in ("ctx", "q", "kst", "oout"):
                    for i in range(2):
                        counted[f"self_{name}{i}"] = B // 2 * 16
                for i in range(WORK):
                    counted[f"self_free{i}"] = B // 2 * per_pair[i]
                counted["self_ready"] = 1

            def base(s):
                return counted.get(s.name, 0)

            def settled(eng, role):
                eng.sem_inc(sem(f"{role}_settled"), 1)

            def half(b):
                if isinstance(b, int):
                    return b % 2, b // 2
                i, k = b
                return k % 2, i + k // 2

            def val(b):
                return b if isinstance(b, int) else b[0] * 2 + b[1]

            def bank_of(b, job):
                return plan[(half(b)[0], job)][0]

            def filled_at(b, job):
                return val(b) * n_jobs + plan[(half(b)[0], job)][2] + 1

            def freed_at(b, job):
                u, pair = half(b)
                bank, before, _ = plan[(u, job)]
                return pair * per_pair[bank] + before + 1

            def is_first(b, n=1):
                return isinstance(b, int) and b < n

            def pe_step(main, prep, step):
                k, j = step
                if k == "S":
                    b = main
                    u, _ = half(b)
                    slot = (u * att.NE + j) % 2
                    if j == 0:
                        for r in range(att.rjobs):
                            eng.wait_ge(free[bank_of(b, ("R", r))], base(free[bank_of(b, ("R", r))]) + freed_at(b, ("R", r)))
                    if not (is_first(b) and j < 2):
                        eng.wait_ge(exps, base(exps) + val(b) * att.NE + j - 1)
                    for ti, tile in enumerate(att.exps[j]):
                        k0, n = att.tiles[tile]
                        for g in range(4):
                            col = ti * W_ + g * hg * S
                            mm = nc.tensor.matmul(
                                ps[0:n, 2 * slot + col // 512, col % 512:col % 512 + hg * S],
                                kst[0:att.krows, u, g, k0:k0 + n],
                                QW[0:att.krows, u, g * hg * S:(g + 1) * hg * S], start=True, stop=True)
                    mm.then_inc(scores, 1)
                if k == "P":
                    b = main
                    u, _ = half(b)
                    slot = (u * att.NE + j) % 2
                    if j == 0:
                        last_v = ("V", len(att.vjobs) - 1)
                        for v in range(max(0, last_v[1] - WORK + 1), last_v[1] + 1):
                            eng.wait_ge(free[bank_of(b, ("V", v))], base(free[bank_of(b, ("V", v))]) + freed_at(b, ("V", v)))
                        if not is_first(b):
                            eng.wait_ge(oev, base(oev) + val(b))
                        else:
                            eng.wait_ge(ready, base(ready) + 1)
                    eng.wait_ge(exps, base(exps) + val(b) * att.NE + j + 1)
                    if not att.cross:
                        settled(eng, role)
                    for ti, tile in enumerate(att.exps[j]):
                        _, n = att.tiles[tile]
                        for r, quad, h0, nh, v0, oc in att.groups:
                            m = nh * (att.d + 1)
                            mm = nc.tensor.matmul(
                                ps[32 * quad:32 * quad + m, 4, oc:oc + nh * S], V[0:n, u, tile, v0:v0 + m],
                                Pb[0:n, slot, ti * W_ + h0 * S:ti * W_ + (h0 + nh) * S],
                                start=(tile == 0 and r == 0), stop=(tile == len(att.tiles) - 1),
                                skip_group_check=True, tile_position=(0, 32 * quad))
                    mm.then_inc(pv, 1)
                if k in ("K", "V", "M", "R"):
                    b = prep
                    u, pair = half(b)
                    bank, before, _ = plan[(u, step)]
                    if not (isinstance(b, int) and b // 2 == 0 and before == 0):
                        eng.wait_ge(free[bank], base(free[bank]) + pair * per_pair[bank] + before)
                    pb = ps[:, 5 + bank, :]
                if k == "K":
                    if j == 0:
                        eng.wait_ge(s_ctx[u], base(s_ctx[u]) + pair * 16 + 16)
                    c0, n = att.kchunks[j]
                    nc.tensor.matmul(pb[:, 0:n], w(f"{t}_k"), CT[:, u, c0:c0 + n],
                                     start=True, stop=True).then_inc(filled, 1)
                if k == "V":
                    if j == 0 and not att.cross:
                        eng.wait_ge(s_ctx[u], base(s_ctx[u]) + pair * 16 + 16)
                    if not att.cross:
                        settled(eng, role)
                    kk = att.values_k
                    for i, tile in enumerate(att.vjobs[j]):
                        k0, n = att.tiles[tile]
                        mm = nc.tensor.matmul(pb[0:n, i * att.NV:(i + 1) * att.NV], CT[0:kk, u, k0:k0 + n],
                                              w(f"{t}_v", rows=kk), start=True, stop=True)
                    mm.then_inc(filled, 1)
                if k == "M":
                    if j == 0:
                        eng.wait_ge(qbuilt, base(qbuilt) + val(b) + 1)
                        eng.wait_ge(s_kst[u], base(s_kst[u]) + (pair + 1) * 16 * kst_dmas)
                        if att.masked:
                            eng.wait_ge(s_q[u], base(s_q[u]) + (pair + 1) * 16 * q_dmas)
                    rows = att.krows if att.masked else RAW
                    for i, (unit, c0, n) in enumerate(att.mjobs[j]):
                        mm = nc.tensor.matmul(pb[:, i * S:i * S + n], QW[0:rows, u, unit * 128:(unit + 1) * 128],
                                              kst[0:rows, u, 2 * unit // hg, c0:c0 + n], start=True, stop=True)
                    mm.then_inc(filled, 1)
                if k == "R":
                    if j == 0:
                        eng.wait_ge(negm, base(negm) + val(b) + 1)
                    for i in range(4):
                        mm = nc.tensor.matmul(ps[96:98, 5 + bank, i * 128:(i + 1) * 128], MH[:, u, j * 4 + i, :],
                                              wb("ident16"), start=True, stop=True, tile_position=(0, 96))
                    mm.then_inc(filled, 1)

            def act_step(main, prep, step):
                k, j = step
                if k == "E":
                    b = main
                    u, _ = half(b)
                    slot = (u * att.NE + j) % 2
                    n = att.tiles[att.exps[j][0]][1]
                    cols = len(att.exps[j]) * W_
                    if not (is_first(b, 2) and (b if isinstance(b, int) else 9) * att.NE + j < 2):
                        eng.wait_ge(pv, base(pv) + val(b) * att.NE + j - 1)
                    eng.wait_ge(scores, base(scores) + val(b) * att.NE + j + 1)
                    src_ps = ps[0:n, 2 * slot:2 * slot + 2, :].rearrange("p a c -> p (a c)")[:, 0:cols]
                    nc.scalar.activation(Pb[0:n, slot, 0:cols], src_ps, ACT.Exp, scale=att.scale).then_inc(exps, 1)
                if k == "O":
                    b = main
                    u, pair = half(b)
                    eng.wait_ge(pv, base(pv) + (val(b) + 1) * att.NE)
                    if not is_first(b, 2):
                        eng.wait_ge(s_oout[u], base(s_oout[u]) + pair * 16)
                    nc.scalar.activation(OE[:, u, 0:att.NO], ps[:, 4, 0:att.NO], ACT.Copy).then_inc(oev, 1)
                if k == "K":
                    b = prep
                    if j == 0 and not is_first(b):
                        up, pp = half(b - 1 if isinstance(b, int) else (b[0], b[1] - 1))
                        eng.wait_ge(s_kst[up], base(s_kst[up]) + (pp + 1) * 16 * kst_dmas)
                    c0, n = att.kchunks[j]
                    eng.wait_ge(filled, base(filled) + filled_at(b, step))
                    nc.scalar.activation(HL[:, 0, c0:c0 + n], ps[:, 5 + bank_of(b, step), 0:n], ACT.Identity,
                                         bias=bias(f"bk{t[-1]}")).then_inc(khi, 1)
                if k == "R":
                    b = prep
                    u, _ = half(b)
                    eng.wait_ge(filled, base(filled) + filled_at(b, step))
                    nc.scalar.activation(QW[96:98, u, j * 512:(j + 1) * 512], ps[96:98, 5 + bank_of(b, step), :],
                                         ACT.Copy).then_inc(free[bank_of(b, step)], 1)

            def dve_step(main, prep, step):
                k, j = step
                b = prep
                if k in ("K", "V", "M"):
                    u, pair = half(b)
                    bank = bank_of(b, step)
                    pb = ps[:, 5 + bank, :]
                if k == "K":
                    c0, n = att.kchunks[j]
                    eng.wait_ge(khi, base(khi) + val(b) * len(att.kchunks) + j + 1)
                    nc.vector.scalar_tensor_tensor(HL[:, 1, c0:c0 + n], pb[:, 0:n], bias(f"bk{t[-1]}"),
                                                   HL[:, 0, c0:c0 + n], ALU.add, ALU.subtract).then_inc(free[bank], 1)
                if k == "V":
                    eng.wait_ge(filled, base(filled) + filled_at(b, step))
                    if j == 0 and not is_first(b, 2):
                        eng.wait_ge(pv, base(pv) + (val(b) - 1) * att.NE)
                    ts = att.vjobs[j]
                    n = att.tiles[ts[0]][1]
                    nc.vector.tensor_tensor(
                        V[0:n, u, ts[0]:ts[0] + len(ts), 0:att.NV],
                        pb[0:n, 0:len(ts) * att.NV].rearrange("p (t v) -> p t v", t=len(ts)),
                        w(f"{t}_vb")[0:n, :].unsqueeze(1).broadcast_to([n, len(ts), att.NV]),
                        ALU.add).then_inc(free[bank], 1)
                if k == "M":
                    eng.wait_ge(filled, base(filled) + filled_at(b, step))
                    m = len(att.mjobs[j])
                    if j == 0 and not is_first(b, 2):
                        eng.wait_ge(negm, base(negm) + val(b) - 1)
                    src_ps = pb[:, 0:att.mjobs[j][0][2]] if m == 1 else pb[:, 0:m * S].rearrange("p (a c) -> p a c", a=m)
                    nc.vector.reduce_max(MX[:, u, j * m:(j + 1) * m], src_ps, AX.X).then_inc(free[bank], 1)
                if k == "Z":
                    u, pair = half(b)
                    for m in range(max(0, len(att.mjobs) - WORK), len(att.mjobs)):
                        eng.wait_ge(free[bank_of(b, ("M", m))], base(free[bank_of(b, ("M", m))]) + freed_at(b, ("M", m)))
                    top = MX[:, u, 0:att.units]
                    if att.cross:
                        top = MG[:, u, 0:att.units]
                        nc.vector.reduce_max(top, MX[:, u, 0:att.units * 4].rearrange("p (a c) -> p a c", c=4),
                                             AX.X).then_inc(mx, 1)
                        eng.wait_ge(mx, base(mx) + val(b) * 2 + 1)
                    if not is_first(b, 2):
                        for r in range(att.rjobs):
                            bb = b - 2 if isinstance(b, int) else (b[0] - 1, b[1])
                            eng.wait_ge(free[bank_of(b, ("R", r))], base(free[bank_of(b, ("R", r))]) + freed_at(bb, ("R", r)))
                    nc.vector.tensor_scalar(MH[:, u, 0:att.units, 0], top, -1.0, None, ALU.mult).then_inc(mx, 1)
                    eng.wait_ge(mx, base(mx) + ((val(b) + 1) * (2 if att.cross else 1)))
                    nc.vector.scalar_tensor_tensor(MH[:, u, 0:att.units, 1], top, -1.0, MH[:, u, 0:att.units, 0],
                                                   ALU.mult, ALU.subtract).then_inc(negm, 1)

            def pool_item(b):
                u, pair = half(b)
                eng.wait_ge(s_q[u], base(s_q[u]) + (pair + 1) * 16 * q_dmas)
                if not is_first(b, 2):
                    eng.wait_ge(scores, base(scores) + (val(b) - 1) * att.NE)
                settled(eng, role)
                if att.masked:
                    nc.gpsimd.memset(QW[96:98, u, :], 0.0).then_inc(sem(f"{kind}_qz"), 1)
                hm = wb("hm2" if hg == 2 else "hm4", rows=RAW)
                out = QW[0:RAW, u, 0:W_].rearrange("p (g h q) -> p g h q", g=4, h=hg)
                q4 = QSL[0:RAW, u, :, :].unsqueeze(2).broadcast_to([RAW, 4, hg, S])
                m4 = hm.unsqueeze(1).unsqueeze(3).broadcast_to([RAW, 4, hg, S])
                if att.masked:
                    eng.wait_ge(sem(f"{kind}_qz"), base(sem(f"{kind}_qz")) + val(b) + 1)
                nc.gpsimd.tensor_tensor(out, q4, m4, ALU.mult).then_inc(qbuilt, 1)

            def sp_load(b):
                u, pair = half(b)
                if not is_first(b, 2):
                    bb = b - 2 if isinstance(b, int) else (b[0] - 1, b[1])
                    last_v = ("V", len(att.vjobs) - 1)
                    eng.wait_ge(filled, base(filled) + filled_at(bb, last_v))
                    settled(eng, role)
                if att.cross:
                    eng.dma_start(CT[:, u, :], ctxT[val(b)]).then_inc(s_ctx[u], 16)
                else:
                    kk = att.values_k
                    eng.dma_start(CT[0:kk, u, 0:S], src[0:kk, bass.ds(val(b) * S, S)]).then_inc(s_ctx[u], 16)
                if not is_first(b, 2):
                    eng.wait_ge(qbuilt, base(qbuilt) + val(b) - 1)
                    settled(eng, role)
                eng.dma_start(QSL[0:RAW, u, :, :], QS[0:RAW, :, bass.ds(val(b) * S, S)]).then_inc(s_q[u], 16)
                if not att.cross:
                    if not is_first(b, 2):
                        eng.wait_ge(scores, base(scores) + (val(b) - 1) * att.NE)
                        settled(eng, role)
                    eng.dma_start(KSS[0:RAW, u, :, :], KSA[0:RAW, :, bass.ds(val(b) * S, S)]).then_inc(s_kst[u], 16)
                    if mask_dmas:
                        eng.dma_start(KSS[98:99, u, :, :],
                                      nsel[0:1, 0, bass.ds(val(b) * S, S)].unsqueeze(1).broadcast_to([1, 4, S])
                                      ).then_inc(s_kst[u], 16)
                        eng.dma_start(QW[98:99, u, :].rearrange("p (h q) -> p h q", h=16),
                                      nsel[0:1, 1, bass.ds(val(b) * S, S)].unsqueeze(1).broadcast_to([1, 16, S])
                                      ).then_inc(s_q[u], 16)

            def sp_stack(b):
                u, pair = half(b)
                if not is_first(b, 2):
                    eng.wait_ge(scores, base(scores) + (val(b) - 1) * att.NE)
                    settled(eng, role)
                for j in range(max(0, 4 - WORK), 4):
                    eng.wait_ge(free[bank_of(b, ("K", j))], base(free[bank_of(b, ("K", j))]) + freed_at(b, ("K", j)))
                    settled(eng, role)
                for p, part in enumerate((0, 1, 0)):
                    for g in range(4):
                        ins = eng.dma_start(KST[32 * p:32 * p + 32, u, g, :], HL[32 * g:32 * g + 32, part, 0:NK])
                        ins.then_inc(s_kst[u], 16)

            def sp_out(b):
                u, pair = half(b)
                eng.wait_ge(oev, base(oev) + val(b) + 1)
                settled(eng, role)
                eng.dma_start(Oall[:, val(b), :] if isinstance(b, int) else Oall[:, bass.ds(val(b), 1), :],
                              OE[:, u, 0:att.NO] if isinstance(b, int) else OE[:, u, 0:att.NO].unsqueeze(1)
                              ).then_inc(s_oout[u], 16)

            if att.cross:
                kst_dmas = 12

            if role == "dve":
                eng.wait_ge(q_ready[0], q_ready[1])
                nc.vector.memset(ps[:, 4, :], 0.0).then_inc(ready, 1)
                if att.cross or att is SA0:
                    nc.vector.memset(kst[96:98, :, :, :].rearrange("p a g k -> p (a g k)"), 1.0).then_inc(sem(f"{t}_ones"), 1)
            if role == "pe":
                if att.cross or att is SA0:
                    eng.wait_ge(sem(f"{t}_ones"), 1)
            if role == "sp" or role == "pool":
                eng.wait_ge(q_ready[0], q_ready[1])
            if role == "sp" and att is SA0:
                for u in range(2):
                    o, n = B_AT["krow"]
                    eng.dma_start(KSS[98:99, u, :, :].rearrange("p g k -> p (g k)"), WB[0:1, o:o + n]).then_inc(sem("sa0_mask"), 16)
                    o, n = B_AT["qrow"]
                    eng.dma_start(QW[98:99, u, :], WB[0:1, o:o + n]).then_inc(sem("sa0_mask"), 16)
            if role == "pe" and att is SA0:
                eng.wait_ge(sem("sa0_mask"), 64)

            step_of = {"pe": pe_step, "act": act_step, "dve": dve_step}
            if role in step_of:
                f = step_of[role]

                def item(main, prep):
                    for step in att.merged(main is not None, prep is not None):
                        f(main, prep, step)
                item(None, 0)
                item(0, 1)
                item(1, 2)
                with eng.Fori(1, B // 2 - 1) as i:
                    item((i, 0), (i, 1))
                    item((i, 1), (i, 2))
                item(B - 2, B - 1)
                item(B - 1, None)
            if role == "pool":
                pool_item(0)
                pool_item(1)
                with eng.Fori(1, B // 2) as i:
                    pool_item((i, 0))
                    pool_item((i, 1))
            if role == "sp":
                def sp_item(main, prep, load):
                    if load is not None:
                        sp_load(load)
                    if prep is not None and att.cross:
                        sp_stack(prep)
                    if main is not None:
                        sp_out(main)
                sp_load(0)
                sp_item(None, 0, 1)
                sp_item(0, 1, 2)
                sp_item(1, 2, 3)
                with eng.Fori(1, B // 2 - 1) as i:
                    sp_item((i, 0), (i, 1), (i, 2))
                    sp_item((i, 1), (i, 2), (i, 3))
                sp_item(B - 2, B - 1, None)
                sp_item(B - 1, None, None)
            return s_oout

        def attention_out(role, eng, att, call, wname, den, bname, dst, residual):
            t = att.name
            Oall = (ABO[:, 6144:6144 + B * att.NO] if att.H == 8 else ABO[:, 0:B * att.NO]).rearrange(
                "p (b o) -> p b o", b=B)
            s_oout = [sem(f"{t if att.cross else 'self'}_oout{i}") for i in range(2)]
            sel_s, den_s, rec_s, on_s, pe_s, out_s = (sem(f"ao_{k}") for k in ("sel", "den", "rec", "on", "pe", "out"))
            SEL = Pb[:, :, :]
            nb = CH // S
            n = call * NC
            nsel_before = NC * sum(sum(a.blocks) for a in (XA0, SA0, XA1)[:call])
            n_sel = sum(att.blocks)
            ms = W_AT["m_sel"][0]

            def sel(r, c):
                return SEL[:, r, (c % 2) * CH:(c % 2 + 1) * CH]

            for c in range(NC):
                if role == "dve":
                    if c == 0:
                        for s in s_oout:
                            eng.wait_ge(s, 16 * B // 2 * (2 if att is SA1 else 1))
                    if c >= 2:
                        eng.wait_ge(pe_s, n + c - 1)
                    done = 0
                    for r in range(2):
                        for h in range(att.blocks[r]):
                            blk = Oall[:, nb * c:nb * (c + 1), att.bases[r] + h * S:att.bases[r] + (h + 1) * S]
                            out = sel(r, c).rearrange("p (b q) -> p b q", b=nb)
                            if att.H == 8:
                                ins = nc.vector.tensor_copy(out, blk)
                            elif h == 0:
                                ins = nc.vector.tensor_scalar(out, blk, W[:, ms + 4 * r:ms + 4 * r + 1], None, ALU.mult)
                            else:
                                ins = nc.vector.scalar_tensor_tensor(out, blk, W[:, ms + 4 * r + h:ms + 4 * r + h + 1], out,
                                                                     ALU.mult, ALU.add)
                            ins.then_inc(sel_s, 1)
                            done += 1
                            if done < n_sel:
                                eng.wait_ge(sel_s, nsel_before + c * n_sel + done)
                    for r in range(2):
                        bank = lo_bank(c) if r == 0 else hi_bank(c)
                        eng.wait_ge(den_s, 2 * (n + c) + r + 1)
                        if not (c == 0 and r == 0):
                            eng.wait_ge(on_s, 2 * (n + c) + r)
                        nc.vector.reciprocal(C[:, 0:CH], bank).then_inc(rec_s, 1)
                        eng.wait_ge(rec_s, 2 * (n + c) + r + 1)
                        nc.vector.tensor_tensor(sel(r, c), sel(r, c), C[:, 0:CH], ALU.mult).then_inc(on_s, 1)
                    eng.wait_ge(pe_s, n + c + 1)
                    if bname is None:
                        ins = nc.vector.tensor_tensor(ck(dst, c), lo_bank(c), ck(residual, c), ALU.add)
                    else:
                        ins = nc.vector.scalar_tensor_tensor(ck(dst, c), lo_bank(c), bias(bname), ck(residual, c),
                                                             ALU.add, ALU.add)
                    ins.then_inc(out_s, 1)
                if role == "pe":
                    eng.wait_ge(sel_s, nsel_before + (c + 1) * n_sel)
                    for r in range(2):
                        nc.tensor.matmul(lo_bank(c) if r == 0 else hi_bank(c), w(den, r * D, (r + 1) * D), sel(r, c),
                                         start=True, stop=True).then_inc(den_s, 1)
                    eng.wait_ge(on_s, 2 * (n + c) + 2)
                    for r in range(2):
                        mm = nc.tensor.matmul(lo_bank(c), w(wname, r * D, (r + 1) * D), sel(r, c),
                                              start=(r == 0), stop=(r == 1))
                    mm.then_inc(pe_s, 1)
            return out_s, n + 1


        nsel = sb("nsel", [1, 2, N], BF16)

        def diagonal_attention(role, eng, ready):
            s = {k: sem(f"dg_{k}") for k in ("q", "k", "v", "qev", "prod", "s", "top", "rel", "e", "rec", "av", "an",
                                             "o", "out")}
            root = float(np.sqrt(np.float32(D)))
            for c in range(NC):
                if role == "pe":
                    eng.wait_ge(ready[0], ready[1] + c)
                    nc.tensor.matmul(lo_bank(c), w("c_q"), ck(T, c), start=True, stop=True).then_inc(s["q"], 1)
                    nc.tensor.matmul(hi_bank(c), w("c_k"), ck(T, c), start=True, stop=True).then_inc(s["k"], 1)
                if role == "act":
                    eng.wait_ge(s["q"], c + 1)
                    nc.scalar.activation(ck(A, c), lo_bank(c), ACT.Identity, bias=bias("c_bq")).then_inc(s["qev"], 1)
                if role == "dve":
                    eng.wait_ge(s["qev"], c + 1)
                    eng.wait_ge(s["k"], c + 1)
                    nc.vector.scalar_tensor_tensor(ck(A, c), hi_bank(c), bias("c_bk"), ck(A, c),
                                                   ALU.add, ALU.mult).then_inc(s["prod"], 1)
            for c in range(NC):
                if role == "pe":
                    eng.wait_ge(s["prod"], c + 1)
                    nc.tensor.matmul(hi_bank(c), w("ones"), ck(A, c), start=True, stop=True).then_inc(s["s"], 1)
                    nc.tensor.matmul(lo_bank(c), w("c_v"), ck(T, c), start=True, stop=True).then_inc(s["v"], 1)
                if role == "dve":
                    eng.wait_ge(s["s"], c + 1)
                    nc.vector.tensor_scalar(ck(Bt, c), hi_bank(c), root, None, ALU.mult).then_inc(s["top"], 1)
                    eng.wait_ge(s["top"], c + 1)
                    nc.vector.scalar_tensor_tensor(ck(A, c), hi_bank(c), root, ck(Bt, c),
                                                   ALU.mult, ALU.subtract).then_inc(s["rel"], 1)
                if role == "act":
                    eng.wait_ge(s["rel"], c + 1)
                    nc.scalar.activation(ck(A, c), ck(A, c), ACT.Exp).then_inc(s["e"], 1)
            for c in range(NC):
                if role == "dve":
                    eng.wait_ge(s["e"], c + 1)
                    nc.vector.reciprocal(ck(Bt, c), ck(A, c)).then_inc(s["rec"], 1)
                    eng.wait_ge(s["v"], c + 1)
                    nc.vector.scalar_tensor_tensor(ck(A, c), lo_bank(c), bias("c_bv"), ck(A, c),
                                                   ALU.add, ALU.mult).then_inc(s["av"], 1)
                    eng.wait_ge(s["rec"], c + 1)
                    eng.wait_ge(s["av"], c + 1)
                    nc.vector.tensor_tensor(ck(A, c), ck(A, c), ck(Bt, c), ALU.mult).then_inc(s["an"], 1)
                if role == "pe":
                    eng.wait_ge(s["an"], c + 1)
                    nc.tensor.matmul(lo_bank(c), w("c_o"), ck(A, c), start=True, stop=True).then_inc(s["o"], 1)
            for c in range(NC):
                if role == "dve":
                    eng.wait_ge(s["o"], c + 1)
                    nc.vector.scalar_tensor_tensor(ck(A, c), lo_bank(c), bias("c_bo"), ck(T, c),
                                                   ALU.add, ALU.add).then_inc(s["out"], 1)
            return s["out"], 1

        def dense_ff(role, eng, ready):
            s = {k: sem(f"ff_{k}") for k in ("h", "relu", "y", "out")}
            nf = FF // D
            for f in range(nf + 1):
                for c in range(NC):
                    buf = Bt if f % 2 == 0 else C
                    if f < nf:
                        if role == "pe":
                            if f == 0:
                                eng.wait_ge(ready[0], ready[1] + c)
                            else:
                                eng.wait_ge(s["relu"], (f - 1) * NC + c + 1)
                            nc.tensor.matmul(hi_bank(c), w("lin1", f * D, (f + 1) * D), ck(T, c),
                                             start=True, stop=True).then_inc(s["h"], 1)
                        if role == "act":
                            if f >= 2:
                                eng.wait_ge(s["y"], (f - 2) * NC + c + 1)
                            eng.wait_ge(s["h"], f * NC + c + 1)
                            nc.scalar.activation(ck(buf, c), hi_bank(c), ACT.Relu,
                                                 bias=bias(f"l1b{f}")).then_inc(s["relu"], 1)
                    if f > 0 and role == "pe":
                        g = f - 1
                        buf = Bt if g % 2 == 0 else C
                        eng.wait_ge(s["relu"], g * NC + c + 1)
                        nc.tensor.matmul(lo_bank(c), w("lin2", g * D, (g + 1) * D), ck(buf, c),
                                         start=(g == 0), stop=(g == nf - 1)).then_inc(s["y"], 1)
            for c in range(NC):
                if role == "dve":
                    eng.wait_ge(s["y"], (nf - 1) * NC + c + 1)
                    nc.vector.scalar_tensor_tensor(ck(A, c), lo_bank(c), bias("l2b"), ck(T, c),
                                                   ALU.add, ALU.add).then_inc(s["out"], 1)
            return s["out"], 1

        def add_to_stream(role, eng, ready):
            s = sem("l0_added")
            if role == "dve":
                for c in range(NC):
                    eng.wait_ge(ready[0], ready[1] + c)
                    nc.vector.tensor_tensor(ck(X, c), ck(X, c), ck(T, c), ALU.add).then_inc(s, 1)
            return s, 1

        def rotary(role, eng, call, wname, rows, srcT, ready):
            s = {k: sem(f"rot_{k}") for k in ("pe", "cos", "sin", "rot", "hi", "lo")}
            n = call * NC
            o = W_AT["rope"][0]
            nb = CH // S
            for c in range(NC):
                if role == "pe":
                    eng.wait_ge(ready[0], ready[1] + c)
                    nc.tensor.matmul(lo_bank(c), w(wname, 0, D, rows=rows), srcT[0:rows, c * CH:(c + 1) * CH],
                                     start=True, stop=True)
                    nc.tensor.matmul(hi_bank(c), w(wname, D, 2 * D, rows=rows), srcT[0:rows, c * CH:(c + 1) * CH],
                                     start=True, stop=True).then_inc(s["pe"], 1)
                if role == "dve":
                    def tab(k):
                        return W[:, o + k * S:o + (k + 1) * S].unsqueeze(1).broadcast_to([128, nb, S])
                    eng.wait_ge(s["pe"], n + c + 1)
                    nc.vector.tensor_tensor(ck(A, c).rearrange("p (b q) -> p b q", b=nb),
                                            lo_bank(c).rearrange("p (b q) -> p b q", b=nb), tab(0), ALU.mult
                                            ).then_inc(s["cos"], 1)
                    nc.vector.tensor_tensor(ck(Bt, c).rearrange("p (b q) -> p b q", b=nb),
                                            hi_bank(c).rearrange("p (b q) -> p b q", b=nb), tab(1), ALU.mult
                                            ).then_inc(s["sin"], 1)
                    eng.wait_ge(s["cos"], n + c + 1)
                    eng.wait_ge(s["sin"], n + c + 1)
                    nc.vector.tensor_tensor(ck(A, c), ck(A, c), ck(Bt, c), ALU.add).then_inc(s["rot"], 1)
                if role == "act":
                    eng.wait_ge(s["rot"], n + c + 1)
                    nc.scalar.activation(ck(HL[:, 0, :], c), ck(A, c), ACT.Copy).then_inc(s["hi"], 1)
            for c in range(NC):
                if role == "dve":
                    eng.wait_ge(s["hi"], n + c + 1)
                    nc.vector.tensor_tensor(ck(HL[:, 1, :], c), ck(A, c), ck(HL[:, 0, :], c),
                                            ALU.subtract).then_inc(s["lo"], 1)
            return s["lo"], n + 1

        def moe_stage(role, eng, ready):
            s = {k: sem(f"moe_{k}") for k in ("logit", "score", "chain", "parts", "turned", "weights", "gu", "gate",
                                             "hid", "mid", "down", "out")}
            NT = N // 128
            at = [0]

            def area(n):
                at[0] += n
                return ABO[:, at[0] - n:at[0]]

            SC = area(NT * E).rearrange("p (t e) -> p t e", t=NT)
            SFC = area(NT * E).rearrange("p (t e) -> p t e", t=NT)
            GSC = area(NT * 12).rearrange("p (t e) -> p t e", t=NT)
            GM8 = area(NT * 8).rearrange("p (t e) -> p t e", t=NT)
            GR = area(NT * 12).rearrange("p (t e) -> p t e", t=NT)
            GM = area(NT * 8).rearrange("p (t e) -> p t e", t=NT)
            MK = area(NT * 34).rearrange("p (t e) -> p t e", t=NT)
            MK8 = area(NT * 8).rearrange("p (t e) -> p t e", t=NT)
            MR = area(NT * 34).rearrange("p (t e) -> p t e", t=NT)
            TW = area(NT * E).rearrange("p (t e) -> p t e", t=NT)
            SM = area(NT)
            CBS = area(NT * E).bitcast(BF16).rearrange("p (t e) -> p t e", t=NT)
            CTT = HL[0:2 * E, 0, :]

            if role == "pe":
                for c in range(NC):
                    eng.wait_ge(ready[0], ready[1] + c)
                for t in range(NT):
                    mm = nc.tensor.matmul(ps[:, 0, t * E:(t + 1) * E], T[:, t * 128:(t + 1) * 128], w("gate"),
                                          start=True, stop=True)
                mm.then_inc(s["logit"], 1)
            if role == "act":
                eng.wait_ge(s["logit"], 1)
                nc.scalar.activation(SC, ps[:, 0, :].rearrange("p (t e) -> p t e", t=NT), ACT.Sigmoid
                                     ).then_inc(s["score"], 1)
            if role == "dve":
                n = [0]

                def link(ins):
                    n[0] += 1
                    ins.then_inc(s["chain"], 1)
                    eng.wait_ge(s["chain"], n[0])

                eng.wait_ge(s["score"], 1)
                link(nc.vector.tensor_tensor(SFC, SC, w("gate_b").unsqueeze(1).broadcast_to([128, NT, E]), ALU.add))
                link(nc.vector.memset(GSC[:, :, NG:12], BIG))
                link(nc.vector.memset(MK[:, :, E:34], BIG))
                link(nc.vector.reduce_max(GSC[:, :, 0:NG], SFC.rearrange("p t (g s) -> p t g s", g=NG), AX.X))
                for t in range(NT):
                    link(nc.vector.max(GM8[:, t, :], GSC[:, t, :]))
                for t in range(NT):
                    link(nc.vector.match_replace(GR[:, t, :], GM8[:, t, :], GSC[:, t, :], -BIG))
                link(nc.vector.tensor_scalar(GM, GR[:, :, 0:NG], -BIG, None, ALU.is_equal))
                link(nc.vector.tensor_tensor(MK[:, :, 0:E].rearrange("p t (g s) -> p t g s", g=NG),
                                             SFC.rearrange("p t (g s) -> p t g s", g=NG),
                                             GM.unsqueeze(3).broadcast_to([128, NT, NG, GS]), ALU.mult))
                link(nc.vector.tensor_scalar(MK[:, :, 0:E], MK[:, :, 0:E], 0.0, None, ALU.add))
                for t in range(NT):
                    link(nc.vector.max(MK8[:, t, :], MK[:, t, :]))
                for t in range(NT):
                    link(nc.vector.match_replace(MR[:, t, :], MK8[:, t, :], MK[:, t, :], -BIG))
                link(nc.vector.tensor_scalar(MR[:, :, 0:E], MR[:, :, 0:E], -BIG, None, ALU.is_equal))
                link(nc.vector.tensor_tensor(TW, SC, MR[:, :, 0:E], ALU.mult))
                link(nc.vector.reduce_sum(SM, TW, AX.X))
                link(nc.vector.tensor_scalar(SM, SM, 1e-20, None, ALU.add))
                link(nc.vector.reciprocal(SM, SM))
                link(nc.vector.tensor_tensor(TW, TW, SM.unsqueeze(2).broadcast_to([128, NT, E]), ALU.mult))
                link(nc.vector.tensor_scalar(TW, TW, ROUTE_SCALE, None, ALU.mult))
                link(nc.vector.tensor_copy(CBS[:, :, 0:E], TW))
                nc.vector.tensor_tensor(CBS[:, :, E:2 * E], TW, CBS[:, :, 0:E], ALU.subtract).then_inc(s["parts"], 1)
            if role == "pe":
                eng.wait_ge(s["parts"], 1)
                for t in range(NT):
                    tr = nc.tensor.transpose(ps[0:2 * E, 1 + t // 8, :].bitcast(BF16)[:, t % 8 * 128:(t % 8 + 1) * 128],
                                             CBS[:, t, :], wb("ident16"))
                tr.then_inc(s["turned"], 1)
            if role == "act":
                eng.wait_ge(s["turned"], 1)
                for i in range(2):
                    nc.scalar.activation(CTT[:, i * 1024:(i + 1) * 1024], ps[0:2 * E, 1 + i, :].bitcast(BF16), ACT.Copy
                                         ).then_inc(s["weights"], 1)

            NI = E // 2 + 1
            loads = [sem(f"moe_load{i}") for i in range(2)]

            def ew(item_slot, k):
                if item_slot is None:
                    return w("shared", k * D, (k + 1) * D)
                return CT[:, item_slot, k * D:(k + 1) * D]

            def unit(sweep, item, cc):
                return (item + sweep * NI) * 2 + cc

            def up(sweep, item, slot, cc):
                x = ck(T, 2 * sweep + cc)
                if cc == 0 and slot is not None:
                    eng.wait_ge(loads[slot], (sweep * (NI - 1) * 32 // 2) + ((item - 1 - slot) * 16) + 32)
                if sweep or not (isinstance(item, int) and item == 0):
                    eng.wait_ge(s["hid"], unit(sweep, item, cc) - 1)
                elif cc == 0:
                    eng.wait_ge(s["weights"], 2)
                nc.tensor.matmul(ps[:, 2 + cc, :], ew(slot, 0), x, start=True, stop=True)
                mm = nc.tensor.matmul(ps[:, 4 + cc, :], ew(slot, 1), x, start=True, stop=True)
                if slot is not None:
                    mm = nc.tensor.matmul(ps[:, 6 + cc, :], HL[0:2 * E, 1, slot * 128:(slot + 1) * 128],
                                          ck(CTT, 2 * sweep + cc), start=True, stop=True)
                mm.then_inc(s["gu"], 1)

            def down(sweep, item, slot, cc, last=False):
                c = 2 * sweep + cc
                if slot is None:
                    if sweep:
                        eng.wait_ge(s["out"], cc + 1)
                    nc.tensor.matmul(ps[:, cc, :], w("ident"), ck(X, c), start=True, stop=False)
                eng.wait_ge(s["hid"], unit(sweep, item, cc) + 1)
                nc.tensor.matmul(ps[:, cc, :], ew(slot, 2), Pb[:, 1, cc * CH:(cc + 1) * CH],
                                 start=False, stop=last).then_inc(s["down"], 1)

            def pe_item(sweep, item, slot, prev, prev_slot):
                for cc in range(2):
                    up(sweep, item, slot, cc)
                    down(sweep, prev, prev_slot, cc)

            def act_item(sweep, item):
                for cc in range(2):
                    eng.wait_ge(s["gu"], unit(sweep, item, cc) + 1)
                    nc.scalar.activation(Pb[:, 0, cc * CH:(cc + 1) * CH], ps[:, 2 + cc, :], ACT.Silu
                                         ).then_inc(s["gate"], 1)

            def dve_item(sweep, item, shared=False):
                for cc in range(2):
                    h = Pb[:, 1, cc * CH:(cc + 1) * CH]
                    eng.wait_ge(s["gate"], unit(sweep, item, cc) + 1)
                    if sweep or not (isinstance(item, int) and item == 0):
                        eng.wait_ge(s["down"], unit(sweep, item, cc) - 1)
                    ins = nc.vector.tensor_tensor(h, ps[:, 4 + cc, :], Pb[:, 0, cc * CH:(cc + 1) * CH], ALU.mult)
                    if not shared:
                        ins.then_inc(s["mid"], 1)
                        eng.wait_ge(s["mid"], unit(sweep, item, cc) + 1 - 2 * (sweep + 1))
                        ins = nc.vector.tensor_tensor(h, h, ps[:, 6 + cc, :], ALU.mult)
                    ins.then_inc(s["hid"], 1)

            def sp_item(sweep, item, slot):
                if not isinstance(item, int):
                    eng.wait_ge(s["down"], unit(sweep, item, 0) - 2)
                elif sweep:
                    eng.wait_ge(s["down"], unit(sweep, item, 0) - 4)
                eng.dma_start(CT[:, slot, 0:3 * D], experts[item - 1]).then_inc(loads[slot], 16)
                eng.dma_start(HL[0:2 * E, 1, slot * 128:(slot + 1) * 128], picks[item - 1]).then_inc(loads[slot], 16)

            if role == "sp":
                eng.wait_ge(ready[0], ready[1])
            for sweep in range(2):
                if role == "pe":
                    up(sweep, 0, None, 0)
                    up(sweep, 0, None, 1)
                    pe_item(sweep, 1, 0, 0, None)
                    pe_item(sweep, 2, 1, 1, 0)
                    with eng.Fori(1, NI // 2) as i:
                        pe_item(sweep, i * 2 + 1, 0, i * 2, 1)
                        pe_item(sweep, i * 2 + 2, 1, i * 2 + 1, 0)
                    for cc in range(2):
                        down(sweep, NI - 1, 1, cc, last=True)
                if role == "act":
                    act_item(sweep, 0)
                    with eng.Fori(0, NI // 2) as i:
                        act_item(sweep, i * 2 + 1)
                        act_item(sweep, i * 2 + 2)
                if role == "dve":
                    dve_item(sweep, 0, shared=True)
                    with eng.Fori(0, NI // 2) as i:
                        dve_item(sweep, i * 2 + 1)
                        dve_item(sweep, i * 2 + 2)
                    for cc in range(2):
                        eng.wait_ge(s["down"], unit(sweep, NI - 1, cc) + 1)
                        nc.vector.tensor_copy(ck(X, 2 * sweep + cc), ps[:, cc, :]).then_inc(s["out"], 1)
                if role == "sp":
                    sp_item(sweep, 1, 0)
                    sp_item(sweep, 2, 1)
                    with eng.Fori(1, NI // 2) as i:
                        sp_item(sweep, i * 2 + 1, 0)
                        sp_item(sweep, i * 2 + 2, 1)
            return s["out"], 1

        def tree_stage(role, eng, ready):
            s = {k: sem(f"tree_{k}") for k in ("log", "dec", "acts", "path", "msk", "down", "out")}
            loads = [sem(f"tree_load{i}") for i in range(2)]
            WOFF = (0, INNER, NODES, NODES + D, NODES + 2 * D)
            tree_c = B_AT["tree"][0]

            def tw(slot, k, rows=128, cols=128):
                return CT[0:rows, slot, WOFF[k]:WOFF[k] + cols]

            def unit(sweep, tree, cc):
                return (tree + sweep * TREES) * 2 + cc

            def logits(sweep, tree, slot, cc):
                if cc == 0:
                    eng.wait_ge(loads[slot], sweep * 16 * TREES // 2 + (tree - slot) * 8 + 16)
                x = ck(T, 2 * sweep + cc)
                nc.tensor.matmul(ps[0:INNER, 2 + cc, :], tw(slot, 0, cols=INNER), x, start=True, stop=True)
                nc.tensor.matmul(ps[:, 4 + cc, :], tw(slot, 1), x, start=True, stop=True).then_inc(s["log"], 1)

            def paths(sweep, tree, cc):
                eng.wait_ge(s["dec"], unit(sweep, tree, cc) + 1)
                nc.tensor.matmul(ps[0:INNER, 6, :], WB[0:INNER, tree_c:tree_c + INNER], DEC[0:INNER, cc, :],
                                 start=True, stop=True)
                nc.tensor.matmul(ps[:, 7, :], WB[0:INNER, tree_c + INNER:tree_c + NODES], DEC[0:INNER, cc, :],
                                 start=True, stop=True).then_inc(s["path"], 1)

            def down(sweep, tree, slot, cc, first=False, last=False):
                eng.wait_ge(s["msk"], (unit(sweep, tree, cc) + 1) * 2)
                if first:
                    if sweep:
                        eng.wait_ge(s["out"], cc + 1)
                    nc.tensor.matmul(ps[:, cc, :], w("ident"), ck(X, 2 * sweep + cc), start=True, stop=False)
                nc.tensor.matmul(ps[:, cc, :], tw(slot, 2, rows=INNER), Pb[0:INNER, cc, 0:CH], start=False, stop=False)
                nc.tensor.matmul(ps[:, cc, :], tw(slot, 3), Pb[:, cc, CH:2 * CH], start=False, stop=last
                                 ).then_inc(s["down"], 1)

            def pe_tree(sweep, tree, slot, first=False, last=False):
                logits(sweep, tree, slot, 0)
                if not first:
                    down(sweep, tree - 1, 1 - slot, 1, first=(isinstance(tree, int) and tree == 1))
                paths(sweep, tree, 0)
                logits(sweep, tree, slot, 1)
                down(sweep, tree, slot, 0, first=(isinstance(tree, int) and tree == 0), last=last)
                paths(sweep, tree, 1)

            def biases(slot, leaf, rows):
                return CT[0:rows, slot, WOFF[4] + leaf:WOFF[4] + leaf + 1]

            def act_tree(sweep, tree, slot):
                for cc in range(2):
                    n = unit(sweep, tree, cc)
                    eng.wait_ge(s["log"], n + 1)
                    if sweep or not (isinstance(tree, int) and tree == 0):
                        eng.wait_ge(s["down"], n - 1)
                    nc.scalar.activation(Pb[0:INNER, cc, 0:CH], ps[0:INNER, 2 + cc, :], ACT.Silu,
                                         bias=biases(slot, 0, INNER))
                    nc.scalar.activation(Pb[:, cc, CH:2 * CH], ps[:, 4 + cc, :], ACT.Silu, bias=biases(slot, 1, 128)
                                         ).then_inc(s["acts"], 1)

            def dve_tree(sweep, tree, slot):
                for cc in range(2):
                    n = unit(sweep, tree, cc)
                    eng.wait_ge(s["acts"], n + 1)
                    nc.vector.tensor_scalar(DEC[0:INNER, cc, :], ps[0:INNER, 2 + cc, :], biases(slot, 0, INNER), 0.0,
                                            ALU.add, ALU.is_gt).then_inc(s["dec"], 1)
                    eng.wait_ge(s["path"], n + 1)
                    for k, rows, thr in ((0, INNER, "thr0"), (1, 128, "thr1")):
                        h = Pb[0:rows, cc, k * CH:(k + 1) * CH]
                        nc.vector.scalar_tensor_tensor(h, ps[0:rows, 6 + k, :], bias(thr, rows), h, ALU.is_ge,
                                                       ALU.mult).then_inc(s["msk"], 1)

            def sp_tree(sweep, tree, slot):
                if sweep or not isinstance(tree, int):
                    eng.wait_ge(s["down"], unit(sweep, tree, 0) - 2)
                eng.dma_start(CT[:, slot, 0:WOFF[4] + 2], trees[tree]).then_inc(loads[slot], 16)

            if role == "sp":
                eng.wait_ge(ready[0], ready[1])
            if role == "pe":
                for c in range(NC):
                    eng.wait_ge(ready[0], ready[1] + c)
            for sweep in range(2):
                if role == "pe":
                    pe_tree(sweep, 0, 0, first=True)
                    pe_tree(sweep, 1, 1)
                    with eng.Fori(1, TREES // 2 - 1) as i:
                        pe_tree(sweep, i * 2, 0)
                        pe_tree(sweep, i * 2 + 1, 1)
                    pe_tree(sweep, TREES - 2, 0)
                    pe_tree(sweep, TREES - 1, 1, last=True)
                    down(sweep, TREES - 1, 1, 1, last=True)
                if role == "act":
                    act_tree(sweep, 0, 0)
                    act_tree(sweep, 1, 1)
                    with eng.Fori(1, TREES // 2) as i:
                        act_tree(sweep, i * 2, 0)
                        act_tree(sweep, i * 2 + 1, 1)
                if role == "dve":
                    with eng.Fori(0, TREES // 2) as i:
                        dve_tree(sweep, i * 2, 0)
                        dve_tree(sweep, i * 2 + 1, 1)
                    for cc in range(2):
                        eng.wait_ge(s["down"], unit(sweep, TREES - 1, cc) + 1)
                        nc.vector.tensor_copy(ck(X, 2 * sweep + cc), ps[:, cc, :]).then_inc(s["out"], 1)
                if role == "sp":
                    sp_tree(sweep, 0, 0)
                    sp_tree(sweep, 1, 1)
                    with eng.Fori(1, TREES // 2) as i:
                        sp_tree(sweep, i * 2, 0)
                        sp_tree(sweep, i * 2 + 1, 1)
            return s["out"], 1

        def choice_stage(role, eng, ready):
            s = {k: sem(f"ch_{k}") for k in ("h", "relu", "i", "imp", "rows", "chain", "not", "flat")}
            if role == "pe":
                for c in range(NC):
                    eng.wait_ge(ready[0], ready[1] + c)
                    nc.tensor.matmul(ps[0:64, c, :], w("ws1"), ck(T, c), start=True, stop=True).then_inc(s["h"], 1)
                for c in range(NC):
                    eng.wait_ge(s["relu"], c + 1)
                    nc.tensor.matmul(ps[0:1, 4 + c, :], w("ws2", rows=64), A[0:64, c * CH:(c + 1) * CH],
                                     start=True, stop=True).then_inc(s["i"], 1)
            if role == "act":
                for c in range(NC):
                    eng.wait_ge(s["h"], c + 1)
                    nc.scalar.activation(A[0:64, c * CH:(c + 1) * CH], ps[0:64, c, :], ACT.Relu, bias=bias("bs1", 64)
                                         ).then_inc(s["relu"], 1)
                for c in range(NC):
                    eng.wait_ge(s["i"], c + 1)
                    nc.scalar.activation(Bt[0:1, c * CH:(c + 1) * CH], ps[0:1, 4 + c, :], ACT.Sigmoid, bias=bias("bs2", 1)
                                         ).then_inc(s["imp"], 1)
            IM = C[0:B, 0:S]
            TOP = [C[0:B, 64 + 8 * i:72 + 8 * i] for i in range(2)]
            LEFT = [C[0:B, 128 + S * i:128 + S * (i + 1)] for i in range(2)]
            if role == "sp":
                eng.wait_ge(s["imp"], NC)
                eng.dma_start(IM, Bt[0:1, :].rearrange("a (b q) -> a b q", b=B)).then_inc(s["rows"], 16)
                eng.wait_ge(s["not"], 2)
                for k in range(2):
                    eng.dma_start(nsel[0:1, k, :].rearrange("a (b q) -> a b q", b=B), NSB[:, k, :]).then_inc(s["flat"], 16)
                eng.wait_ge(s["flat"], 32)
            if role == "dve":
                eng.wait_ge(s["rows"], 16)
                cur = IM
                for i in range(SEL_K // 8):
                    nc.vector.max(TOP[i], cur).then_inc(s["chain"], 1)
                    eng.wait_ge(s["chain"], 2 * i + 1)
                    nc.vector.match_replace(LEFT[i], TOP[i], cur, -1.0).then_inc(s["chain"], 1)
                    eng.wait_ge(s["chain"], 2 * i + 2)
                    cur = LEFT[i]
                nc.vector.tensor_scalar(NSB[:, 0, :], cur, 0.0, None, ALU.is_ge).then_inc(s["not"], 1)
                nc.vector.tensor_scalar(NSB[:, 1, :], cur, 0.0, MASKED, ALU.is_ge, ALU.mult).then_inc(s["not"], 1)
            return ready

        def program(role, eng):
            loaded = sem("loaded")
            if role == "sp":
                eng.dma_start(W[:, :], wpack).then_inc(loaded, 16)
                eng.dma_start(WB[:, :], bpack).then_inc(loaded, 16)
                eng.dma_start(X[:, :], xT).then_inc(loaded, 16)
            if role == "dve":
                nc.vector.memset(epst[:, :], EPS).then_inc(sem("eps_set"), 1)
            if role == "act":
                eng.wait_ge(sem("eps_set"), 1)
            eng.wait_ge(loaded, 48)

            s = layernorm(role, eng, 0, X, T, None)
            s = diagonal_attention(role, eng, s)
            s = layernorm(role, eng, 1, A, T, s, gain="g1", shift="b1")
            s = project_split(role, eng, 0, w("c_wq"), "bq0", s)
            s = split_rows(role, eng, 0, s, QS, "q")
            attention(role, eng, XA0, s, None)
            s = attention_out(role, eng, XA0, 0, "xa0_o", "xa0_den", "bo0", A, T)
            s = layernorm(role, eng, 2, A, T, s, gain="g2", shift="b2")
            s = dense_ff(role, eng, s)
            s = layernorm(role, eng, 3, A, T, s, gain="g3", shift="b3")
            s = add_to_stream(role, eng, s)
            if stop == 2:
                return X, s

            s = layernorm(role, eng, 4, X, T, s)
            q_lo = rotary(role, eng, 0, "sa0_q", D, T, s)
            s = split_rows(role, eng, 1, q_lo, QS, "q")
            lat_pe, lat = sem("lat_pe"), sem("lat_out")
            if role == "pe":
                for c in range(NC):
                    eng.wait_ge(q_lo[0], q_lo[1] + c)
                    nc.tensor.matmul(lo_bank(c)[0:64, :], w("down"), ck(T, c), start=True, stop=True).then_inc(lat_pe, 1)
            if role == "act":
                for c in range(NC):
                    eng.wait_ge(lat_pe, c + 1)
                    nc.scalar.activation(C[0:64, c * CH:(c + 1) * CH], lo_bank(c)[0:64, :], ACT.Copy).then_inc(lat, 1)
            if role in ("act", "dve"):
                eng.wait_ge(*s)
            k_lo = rotary(role, eng, 1, "sa0_k", 64, C, (lat, 1))
            s = split_rows(role, eng, 2, k_lo, KSA, "k")
            attention(role, eng, SA0, s, C)
            s = attention_out(role, eng, SA0, 1, "sa0_o", "den16", None, X, X)
            if stop == 3:
                return X, s

            s = layernorm(role, eng, 5, X, T, s)
            s = moe_stage(role, eng, s)
            if role == "pe":
                eng.wait_ge(s[0], NC)
            if stop == 4:
                return X, s

            s = layernorm(role, eng, 6, X, T, s)
            s = project_split(role, eng, 1, w("xa1_q"), "bq1", s)
            s = split_rows(role, eng, 3, s, QS, "q")
            attention(role, eng, XA1, s, None)
            s = attention_out(role, eng, XA1, 2, "xa1_o", "den16", "bo1", X, X)
            if stop == 5:
                return X, s

            s = layernorm(role, eng, 7, X, T, s)
            s = choice_stage(role, eng, s)
            q_lo = project_split(role, eng, 2, w("sa1_q"), "s_bq", s)
            s = split_rows(role, eng, 4, q_lo, QS, "q")
            if role == "pe":
                eng.wait_ge(q_lo[0], q_lo[1] + NC - 1)
            if role in ("act", "dve"):
                eng.wait_ge(*s)
            s = project_split(role, eng, 3, w("sa1_k"), "s_bk", (sem("ln_out"), 7 * NC + 1))
            s = split_rows(role, eng, 5, s, KSA, "k")
            attention(role, eng, SA1, s, T)
            s = attention_out(role, eng, SA1, 3, "sa1_o", "den16", "s_bo", X, X)
            if stop == 6:
                return X, s

            s = layernorm(role, eng, 8, X, T, s)
            s = tree_stage(role, eng, s)
            return X, s

        block = ctx.enter_context(nc.Block())

        @block.tensor
        def _(eng):
            program("pe", eng)

        @block.vector
        def _(eng):
            program("dve", eng)

        @block.scalar
        def _(eng):
            program("act", eng)

        @block.gpsimd
        def _(eng):
            program("pool", eng)

        @block.sync
        def _(eng):
            res, s = program("sp", eng)
            stored = sem("stored")
            eng.wait_ge(s[0], s[1] + NC - 1)
            eng.dma_start(outT, res[:, :]).then_inc(stored, 16)
            eng.wait_ge(stored, 16)



def _values(att, wv, bv):
    wa = np.zeros((wv.shape[0], att.NV), wv.dtype)
    ba = np.zeros((128, att.NV), wv.dtype)
    for r, quad, h0, nh, v0, oc in att.groups:
        for i in range(nh):
            a, h = v0 + i * (att.d + 1), h0 + i
            wa[:, a:a + att.d] = wv[:, h * att.d:(h + 1) * att.d]
            if bv is not None:
                ba[:, a:a + att.d] = bv[h * att.d:(h + 1) * att.d][None, :]
            ba[:, a + att.d] = 1.0
    return wa, ba


def _outputs(att, wo):
    out = np.zeros((128, 2, D), wo.dtype)
    for r, quad, h0, nh, v0, oc in att.groups:
        for i in range(nh):
            a = 32 * quad + i * (att.d + 1)
            out[a:a + att.d, r] = wo[(h0 + i) * att.d:(h0 + i + 1) * att.d]
    return out.reshape(128, 2 * D)


def _denominators(att):
    out = np.zeros((128, 2, D), np.float32)
    for r in range(2):
        source = [att.d] * 128
        for rr, quad, h0, nh, v0, oc in att.groups:
            if rr == r:
                for m in range(32):
                    i = min(m // (att.d + 1), nh - 1)
                    source[32 * quad + m] = 32 * quad + i * (att.d + 1) + att.d
        for m, k in enumerate(source):
            out[k, r, m] = 1.0
    return out.reshape(128, 2 * D)


def _tree_paths():
    path = np.zeros((128, NODES + 1), np.float32)
    need = np.zeros(NODES, np.float32)
    for n in range(NODES):
        k = n
        while k > 0:
            parent, right = (k - 1) // 2, (k - 1) % 2
            path[parent, n] = 1.0 if right else -1.0
            need[n] += right
            k = parent
    return path, need - 0.5


def kernel(**inputs):
    import ml_dtypes
    import concourse.bacc as _bacc
    from concourse.bass_utils import run_bass_kernel_spmd as _run

    i = {k: np.asarray(v) for k, v in inputs.items()}
    z = np.float32
    xT = np.ascontiguousarray(i["x"].reshape(N, D).T)
    ctxT = np.ascontiguousarray(i["ctx_1024"].transpose(0, 2, 1))

    wp = np.zeros((128, W_COLS), z)

    def put(name, a):
        o, n = W_AT[name]
        a = np.asarray(a)
        assert a.shape[1] == n, (name, a.shape, n)
        wp[:a.shape[0], o:o + n] = a

    bs = np.zeros((128, 64), z)

    def put_bias(name, a):
        bs[:len(a), BIAS_AT[name]] = a

    put("mean", np.full((D, D), 1.0 / D, z))
    put("ones", np.ones((D, D), z))
    put("ident", np.eye(D, dtype=z))
    qkv, qb = i["L0_xattn_qkv_w"], i["L0_xattn_qkv_b"]
    for k, n in enumerate("qkv"):
        put(f"c_{n}", qkv[k * D:(k + 1) * D].T)
        put_bias(f"c_b{n}", qb[k * D:(k + 1) * D])
    put("c_o", i["L0_xattn_sa_out_w"].T)
    put_bias("c_bo", i["L0_xattn_sa_out_b"])
    ip, ib = i["L0_xattn_in_proj_w"], i["L0_xattn_in_proj_b"]
    put("c_wq", ip[0:D].T)
    put_bias("bq0", ib[0:D])
    put("xa0_k", ip[D:2 * D].T)
    put_bias("bk0", ib[D:2 * D])
    wa, ba = _values(XA0, ip[2 * D:].T, ib[2 * D:])
    put("xa0_v", wa)
    put("xa0_vb", ba)
    put("xa0_o", _outputs(XA0, i["L0_xattn_mha_out_w"].T))
    put_bias("bo0", i["L0_xattn_mha_out_b"])
    put("xa0_den", _denominators(XA0))
    for k in (1, 2, 3):
        put_bias(f"g{k}", i[f"L0_xattn_ln{k}_g"])
        put_bias(f"b{k}", i[f"L0_xattn_ln{k}_b"])
    put("lin1", i["L0_xattn_lin1_w"].T)
    put("lin2", i["L0_xattn_lin2_w"].T.reshape(4, D, D).transpose(1, 0, 2).reshape(D, FF))
    for f in range(4):
        put_bias(f"l1b{f}", i["L0_xattn_lin1_b"][f * D:(f + 1) * D])
    put_bias("l2b", i["L0_xattn_lin2_b"])

    d = SA0.d
    inv = 1.0 / 10000.0 ** (np.arange(0, d, 2, dtype=z) / d)
    ang = np.outer(np.arange(S, dtype=z), inv)
    cos, sin = np.cos(ang).astype(z), np.sin(ang).astype(z)
    pair = (np.arange(D) % d) // 2
    sign = np.where(np.arange(D) % 2 == 0, -1.0, 1.0).astype(z)
    put("rope", np.concatenate([cos[:, pair].T, sin[:, pair].T * sign[:, None]], axis=1))
    swap = np.arange(D) ^ 1
    wq, wk = i["L0_attn_wq"], i["L0_attn_wk_up"]
    put("sa0_q", np.concatenate([wq, wq[:, swap]], axis=1))
    put("down", i["L0_attn_w_down"])
    put("sa0_k", np.concatenate([wk, wk[:, swap]], axis=1))
    wa, ba = _values(SA0, i["L0_attn_wv_up"], None)
    put("sa0_v", wa)
    put("sa0_vb", ba)
    put("sa0_o", _outputs(SA0, i["L0_attn_wo"]))
    put("den16", _denominators(SA0))
    ms = np.zeros((128, 8), z)
    for r, quad, h0, nh, v0, oc in SA0.groups:
        for k in range(nh):
            a = 32 * quad + k * (d + 1)
            ms[a:a + d + 1, 4 * r + k] = 1.0
    put("m_sel", ms)

    put("gate", i["L0_ffn_gate_weight"].T)
    put("gate_b", np.broadcast_to(i["L0_ffn_e_score_correction_bias"][None, :], (128, E)))
    put("shared", np.concatenate([i["L0_ffn_shared_gate_w"].T, i["L0_ffn_shared_up_w"].T,
                                  i["L0_ffn_shared_down_w"].T], axis=1))
    gu = i["L0_ffn_experts_gate_up"].reshape(E // 2, 2, 2, EI, D)
    gate_up = gu.transpose(0, 4, 2, 1, 3).reshape(E // 2, D, 2 * D)
    dn = i["L0_ffn_experts_down"].reshape(E // 2, 2, D, EI).transpose(0, 1, 3, 2).reshape(E // 2, D, D)
    experts = np.concatenate([gate_up, dn], axis=2)
    picks = np.zeros((E // 2, 2 * E, D), ml_dtypes.bfloat16)
    for p in range(E // 2):
        for k in range(2):
            picks[p, 2 * p + k, k * EI:(k + 1) * EI] = 1.0
            picks[p, E + 2 * p + k, k * EI:(k + 1) * EI] = 1.0

    put("xa1_q", i["L1_xattn_W_Q"])
    put_bias("bq1", i["L1_xattn_b_Q"])
    put("xa1_k", i["L1_xattn_W_K"])
    put_bias("bk1", i["L1_xattn_b_K"])
    wa, ba = _values(XA1, i["L1_xattn_W_V"], i["L1_xattn_b_V"])
    put("xa1_v", wa)
    put("xa1_vb", ba)
    put("xa1_o", _outputs(XA1, i["L1_xattn_W_O"]))
    put_bias("bo1", i["L1_xattn_b_O"])
    put("sa1_q", i["L1_attn_Wq"])
    put_bias("s_bq", i["L1_attn_bq"])
    put("sa1_k", i["L1_attn_Wk"])
    put_bias("s_bk", i["L1_attn_bk"])
    wa, ba = _values(SA1, i["L1_attn_Wv"], i["L1_attn_bv"])
    put("sa1_v", wa)
    put("sa1_vb", ba)
    put("sa1_o", _outputs(SA1, i["L1_attn_Wo"]))
    put_bias("s_bo", i["L1_attn_bo"])
    put("ws1", i["L1_attn_Ws1"])
    put_bias("bs1", i["L1_attn_bs1"])
    put("ws2", i["L1_attn_Ws2"])
    put_bias("bs2", i["L1_attn_bs2"])

    path, thr = _tree_paths()
    put_bias("thr0", thr[:INNER])
    put_bias("thr1", thr[INNER:])
    put("bias", bs)
    wi = i["L1_ffn_W_in"].reshape(TREES, NODES, D).transpose(0, 2, 1)
    wo = i["L1_ffn_W_out"].reshape(D, TREES, NODES).transpose(1, 2, 0)
    bi = i["L1_ffn_b_in"].reshape(TREES, NODES)
    trees = np.zeros((TREES, 128, NODES + 2 * D + 2), z)
    trees[:, :, 0:NODES] = wi
    trees[:, 0:INNER, NODES:NODES + D] = wo[:, 0:INNER]
    trees[:, :, NODES + D:NODES + 2 * D] = wo[:, INNER:]
    trees[:, 0:INNER, NODES + 2 * D] = bi[:, 0:INNER]
    trees[:, :, NODES + 2 * D + 1] = bi[:, INNER:]

    bp = np.zeros((128, B_COLS), ml_dtypes.bfloat16)

    def put16(name, a):
        o, n = B_AT[name]
        bp[:a.shape[0], o:o + n] = a
    put16("ident16", np.eye(D))
    put16("tree", path)
    rows = np.arange(RAW) % 32
    for hg, dd in ((2, 16), (4, 8)):
        put16(f"hm{hg}", (rows[:, None] // dd == np.arange(hg)[None, :]).astype(z))
    page = (np.arange(S) // 32).astype(z)
    put16("krow", np.tile(page, 4)[None, :])
    put16("qrow", np.tile((1.0 - page) * MASKED, 16)[None, :])

    nc = _bacc.Bacc("TRN2", target_bir_lowering=False, num_devices=1)
    arrays, args = {}, []
    for name, a in (("xT", xT), ("ctxT", ctxT), ("wpack", wp), ("bpack", bp), ("experts", experts), ("picks", picks),
                    ("trees", trees)):
        a = np.ascontiguousarray(a)
        arrays[name] = a
        args.append(nc.dram_tensor(name, a.shape, mybir.dt.from_np(a.dtype), kind="ExternalInput").ap())
    args.append(nc.dram_tensor("outT", (D, N), F32, kind="ExternalOutput").ap())
    bass_perceiver_kernel(nc, *args)
    r = _run(nc, [arrays], core_ids=[0])
    return np.ascontiguousarray(r.results[0]["outT"].T).reshape(B, S, D)
```

```python
from contextlib import ExitStack

import numpy as np

import concourse.bass as bass
from concourse import mybir

ALU = mybir.AluOpType
ACT = mybir.ActivationFunctionType
AX = mybir.AxisListType
F32 = mybir.dt.float32
BF16 = mybir.dt.bfloat16

B, S, D, NK = 32, 64, 128, 1601
N = B * S
CH = 512
NC = N // CH
EPS = 1e-5
MASKED = -1e30
E, EI, TOPK, NG, TOPG = 32, 64, 6, 8, 4
GS = E // NG
ROUTE_SCALE = 2.5
TREES, NODES, INNER, LEAVES = 8, 255, 127, 128
FF = 512
SEL_K = 16
RAW = 96
ROWS = 98
TILE = 128
KTILES = [(t * TILE, min(TILE, NK - t * TILE)) for t in range(-(-NK // TILE))]
BIG = 3e38
SLOTS = 4


class Attention:

    def __init__(self, name, heads, cross, masked=False, values_k=D):
        self.name, self.H, self.cross, self.masked, self.values_k = name, heads, cross, masked, values_k
        self.d = D // heads
        self.hg = heads // 4
        self.W = heads * S
        per = 32 // (self.d + 1)
        if heads == 16:
            sizes = [3, 3, 3, 3, 2, 2]
        else:
            sizes = [1] * 8
        assert max(sizes) <= per
        self.groups, h, v = [], 0, 0
        bases = {}
        col = 0
        for i, n in enumerate(sizes):
            r, quad = divmod(i, 4)
            if r not in bases:
                bases[r] = col
                col += n * S
            self.groups.append((r, quad, h, n, v, bases[r]))
            h += n
            v += n * (self.d + 1)
        self.rounds = len(bases)
        self.bases = bases
        self.NV, self.NO = v, col
        self.blocks = [sizes[0], sizes[4]]
        self.tiles = KTILES if cross else [(0, S)]
        self.keys = NK if cross else S
        per_exp = 1024 // self.W
        self.exps = [list(range(i, min(i + per_exp, len(self.tiles)))) for i in range(0, len(self.tiles), per_exp)]
        if cross and len(self.exps[-1]) > 1:
            raise ValueError("the short key tile has an Exp of its own")
        self.NE = len(self.exps)
        self.units = heads // 2
        q4 = -(-NK // 4)
        self.kchunks = [(c * q4, min(q4, NK - c * q4)) for c in range(4)] if cross else []
        self.vjobs = [list(range(i, min(i + 3, len(self.tiles)))) for i in range(0, len(self.tiles), 3)]
        if cross:
            self.mjobs = [[(u, c0, n)] for u in range(self.units) for c0, n in self.kchunks]
        else:
            self.mjobs = [[(u, 0, S) for u in range(self.units)]]
        self.rjobs = self.W // 512
        self.nk = len(self.kchunks)
        self.jobs = ([("K", j) for j in range(len(self.kchunks))] + [("V", j) for j in range(len(self.vjobs))]
                     + [("M", j) for j in range(len(self.mjobs))] + [("R", j) for j in range(self.rjobs)])
        self.krows = ROWS + 1 if masked else ROWS
        self.scale = 1.0 / float(np.sqrt(self.d))

    def merged(self, main, prep, keys):
        K, V, M, R = ([j for j in self.jobs if j[0] == k] for k in "KVMR")
        if not self.cross:
            return (([("S", 0), ("E", 0)] if main else []) + (M + [("Z", 0)] + V + R if prep else [])
                    + ([("P", 0), ("O", 0)] if main else []))
        n = self.NE
        parts = [[] for _ in range(n)]
        first, steps = FIRST, n - 1 - FIRST
        for i, v in enumerate(V):
            parts[min(i, n - 1)].append(v)
        for i, m in enumerate(M):
            parts[first + i * steps // len(M)].append(m)
        parts[n - 1].append(("Z", 0))
        out = [("S", 0)] if main else []
        for e in range(n):
            if main:
                out.append(("E", e))
                if e + 1 < n:
                    out.append(("S", e + 1))
            if prep:
                out += parts[e]
            if keys and e == n - KSTEP:
                out += K
            if main:
                out.append(("P", e))
        if main:
            out.append(("O", 0))
        if prep:
            out += R
        return out


FIRST, KSTEP = 2, 3
WORK = 3


def bank_plan(att):
    order = [s for s in att.merged(False, True, True) if s[0] in "KVMR"]
    count = [0] * WORK
    plan = {}
    for u in range(2):
        for j, job in enumerate(order):
            bank = (u * len(order) + j) % WORK
            plan[(u, job)] = (bank, count[bank], j)
            count[bank] += 1
    lead = [0] * WORK
    first = []
    for j in range(att.nk):
        bank = plan[(1, ("K", j))][0]
        first.append((bank, lead[bank]))
        lead[bank] += 1
    return plan, count, len(order), lead, first


XA0 = Attention("xa0", 8, True)
SA0 = Attention("sa0", 16, False, masked=True, values_k=64)
XA1 = Attention("xa1", 16, True)
SA1 = Attention("sa1", 16, False, masked=True)


W_PARTS = [("mean", 1), ("centre", D), ("ones", D), ("c_q", D), ("c_k", D), ("c_v", D), ("c_o", D), ("c_wq", D), ("bias", 64),
           ("m_sel", 8),
           ("xa0_k", D), ("xa0_v", XA0.NV), ("xa0_vb", XA0.NV), ("xa0_o", 2 * D), ("xa0_den", 2 * D + 32),
           ("lin1", FF), ("lin2", FF), ("rope", 2 * S), ("sa0_q", 2 * D), ("down", 64), ("sa0_k", 2 * D),
           ("sa0_v", SA0.NV), ("sa0_vb", SA0.NV), ("sa0_o", 2 * D), ("den16", 2 * D + 32),
           ("gate", E), ("gate_b", E), ("shared", 3 * D), ("ident", D),
           ("xa1_q", D), ("xa1_k", D), ("xa1_v", XA1.NV), ("xa1_vb", XA1.NV), ("xa1_o", 2 * D),
           ("sa1_q", D), ("sa1_k", D), ("sa1_v", SA1.NV), ("sa1_vb", SA1.NV), ("sa1_o", 2 * D),
           ("ws1", 64), ("ws2", 1)]
W_AT, _o = {}, 0
for _n, _w in W_PARTS:
    W_AT[_n] = (_o, _w)
    _o += _w
W_COLS = _o
B_PARTS = [("ident16", D), ("tree", INNER + LEAVES + 1), ("hm2", 2), ("hm4", 4), ("krow", S), ("qrow", S)]
B_AT, _o = {}, 0
for _n, _w in B_PARTS:
    B_AT[_n] = (_o, _w)
    _o += _w
B_COLS = _o
BIASES = ["c_bq", "c_bk", "c_bv", "c_bo", "g1", "b1", "bq0", "bk0", "bo0", "g2", "b2", "l1b0", "l1b1", "l1b2", "l1b3",
          "l2b", "g3", "b3", "bq1", "bk1", "bo1", "s_bq", "s_bk", "s_bo", "bs1", "bs2", "thr0", "thr1"]
BIAS_AT = {n: i for i, n in enumerate(BIASES)}
assert len(BIASES) <= 64


def bass_perceiver_kernel(nc, xT, ctxT, wpack, bpack, experts, picks, trees, outT, stop=99):
    ctx = ExitStack()
    with ctx:
        def sb(name, shape, dt):
            return ctx.enter_context(nc.sbuf_tensor(name, shape, dt))

        sems = {}

        def sem(name):
            if name not in sems:
                sems[name] = ctx.enter_context(nc.semaphore(name))
            return sems[name]

        ps = ctx.enter_context(nc.psum_tensor("ps", [128, 8, 512], F32))

        W = sb("W", [128, W_COLS], F32)
        WB = sb("WB", [128, B_COLS], BF16)
        X = sb("X", [128, N], F32)
        T = sb("T", [128, N], F32)
        ABO = sb("ABO", [128, 10240], F32)
        A = ABO[:, 0:N]
        Bt = ABO[:, N:2 * N]
        C = sb("C", [128, N], F32)
        QS = sb("QS", [128, 4, N], BF16)
        HL = sb("HL", [128, 2, N], BF16)
        HLQ = ABO[:, 2 * N:3 * N].bitcast(BF16).rearrange("p (a n) -> p a n", a=2)
        CT = sb("CT", [128, 2, NK], F32)
        KST = sb("KST", [128, 2, 4, NK], BF16)
        KSA = KST[:, :, :, :].rearrange("p a g k -> p (a g k)")[:, 0:4 * N].rearrange("p (g n) -> p g n", g=4)
        KSS = sb("KSS", [128, 2, 4, S], BF16)
        V = sb("V", [128, 2, len(KTILES), 144], F32)
        QW = sb("QW", [128, 2, 16 * S], BF16)
        QSL = sb("QSL", [128, 2, 4, S], BF16)
        Pb = sb("Pb", [128, 2, 1024], F32)
        OE = sb("OE", [128, 2, 320], F32)
        MX = sb("MX", [128, 2, 32], F32)
        MG = sb("MG", [128, 2, 8], F32)
        MH = sb("MH", [128, 2, 8, 2], BF16)
        epst = sb("epst", [128, 1], F32)
        WARM = sb("WARM", [128, 1], F32)
        DEV = sb("DEV", [128, 16], F32)
        COL = sb("COL", [128, 64], F32)
        ROW = sb("ROW", [16, 2, CH], F32)
        DEC = sb("DEC", [128, 2, CH], BF16)
        NSB = sb("NSB", [B, 2, S], BF16)

        def w(name, a=0, b=None, rows=128):
            o, n = W_AT[name]
            return W[0:rows, o + a:o + (n if b is None else b)]

        def wb(name, rows=128):
            o, n = B_AT[name]
            return WB[0:rows, o:o + n]

        def bias(name, rows=128):
            o = W_AT["bias"][0] + BIAS_AT[name]
            return W[0:rows, o:o + 1]

        def ck(t, c):
            return t[:, c * CH:(c + 1) * CH]

        def hi_bank(c):
            return ps[:, 4 + c, :]

        def lo_bank(c):
            return ps[:, c, :]


        def spread(role, eng, call, c, ready):
            diag_s, spread_s = sem("diag"), sem("spread")
            n = NC * call + c
            if role == "dve":
                eng.wait_ge(*ready)
                nc.vector.tensor_tensor(ck(C, c).rearrange("p (t q) -> p t q", t=4),
                                        w("ident").unsqueeze(1).broadcast_to([128, 4, 128]),
                                        COL[:, 4 * c:4 * c + 4].unsqueeze(2).broadcast_to([128, 4, 128]), ALU.mult
                                        ).then_inc(diag_s, 1)
            if role == "pe":
                eng.wait_ge(diag_s, n + 1)
                nc.tensor.matmul(hi_bank(c), w("ones"), ck(C, c), start=True, stop=True).then_inc(spread_s, 1)
            return spread_s, NC * call + 1

        def layernorm(role, eng, call, src, dst, ready, gain=None, shift=None):
            mean_s, xc_s, sq_s, var_s, sd_s, rc_s, scaled_s, out_s = (
                sem(f"ln_{k}") for k in ("mean", "centred", "square", "var", "dev", "recip", "scaled", "out"))
            n = call * NC
            rows = call + (call > 0)
            if role == "pe":
                for c in range(NC):
                    if ready is not None:
                        eng.wait_ge(ready[0], ready[1] + c)
                    nc.tensor.matmul(lo_bank(c), w("centre"), ck(src, c), start=True, stop=True).then_inc(mean_s, 1)
                for c in range(NC):
                    eng.wait_ge(sq_s, n + c + 1)
                    for i in range(4):
                        t = 4 * c + i
                        mm = nc.tensor.matmul(hi_bank(c // 2 * 2)[:, t % 8:t % 8 + 1], C[:, t * 128:(t + 1) * 128],
                                              w("mean", 0, 1), start=True, stop=True)
                    if c % 2:
                        mm.then_inc(var_s, 1)
            if role == "dve":
                for c in range(NC):
                    eng.wait_ge(mean_s, n + c + 1)
                    nc.vector.tensor_copy(ck(dst, c), lo_bank(c)).then_inc(xc_s, 1)
            if role == "act":
                nc.scalar.activation(WARM[:, :], epst[:, :], ACT.Sqrt)
                for c in range(NC):
                    eng.wait_ge(xc_s, n + c + 1)
                    nc.scalar.activation(ck(C, c), ck(dst, c), ACT.Square).then_inc(sq_s, 1)
            for h in range(2):
                if role == "act":
                    eng.wait_ge(var_s, 2 * call + h + 1)
                    nc.scalar.activation(DEV[:, 8 * h:8 * h + 8], hi_bank(2 * h)[:, 0:8], ACT.Sqrt, bias=epst[:, 0:1]
                                         ).then_inc(sd_s, 1)
                if role == "dve":
                    eng.wait_ge(sd_s, 2 * call + h + 1)
                    nc.vector.reciprocal(COL[:, 8 * h:8 * h + 8], DEV[:, 8 * h:8 * h + 8]).then_inc(rc_s, 1)
            for c in range(NC):
                spread_s, first = spread(role, eng, rows, c, (rc_s, 2 * call + c // 2 + 1))
            for c in range(NC):
                if role == "dve":
                    eng.wait_ge(xc_s, n + c + 1)
                    eng.wait_ge(spread_s, first + c)
                    if gain is None:
                        nc.vector.tensor_tensor(ck(dst, c), ck(dst, c), hi_bank(c), ALU.mult).then_inc(out_s, 1)
                    else:
                        nc.vector.scalar_tensor_tensor(ck(dst, c), ck(dst, c), bias(gain), hi_bank(c),
                                                       ALU.mult, ALU.mult).then_inc(scaled_s, 1)
                if role == "act" and gain is not None:
                    eng.wait_ge(scaled_s, n - NC + c + 1)
                    nc.scalar.activation(ck(dst, c), ck(dst, c), ACT.Identity, bias=bias(shift)).then_inc(out_s, 1)
            return out_s, n + 1

        def split_rows(role, eng, call, done, stacked, kind):
            stacked_s = sem("stacked")
            if role == "sp":
                eng.wait_ge(done[0], done[1] + NC - 1)
                order, parts = ((0, 0, 1), HLQ) if kind == "q" else ((0, 1, 0), HL)
                for g in range(4):
                    for p, part in enumerate(order):
                        eng.dma_start(stacked[32 * p:32 * p + 32, g, :],
                                      parts[32 * g:32 * g + 32, part, :]).then_inc(stacked_s, 16)
            return stacked_s, (call + 1) * 12 * 16

        def project_split(role, eng, call, weights, bname, ready, parts):
            pe_s, hi_s, lo_s = sem("proj_sum"), sem("proj_hi"), sem("proj_lo")
            n = call * NC
            for c in range(NC):
                if role == "pe":
                    eng.wait_ge(ready[0], ready[1] + c)
                    nc.tensor.matmul(lo_bank(c), weights, ck(T, c), start=True, stop=True).then_inc(pe_s, 1)
                if role == "act":
                    eng.wait_ge(pe_s, n + c + 1)
                    nc.scalar.activation(ck(parts[:, 0, :], c), lo_bank(c), ACT.Identity,
                                         bias=bias(bname)).then_inc(hi_s, 1)
                if role == "dve":
                    eng.wait_ge(hi_s, n + c + 1)
                    nc.vector.scalar_tensor_tensor(ck(parts[:, 1, :], c), lo_bank(c), bias(bname), ck(parts[:, 0, :], c),
                                                   ALU.add, ALU.subtract).then_inc(lo_s, 1)
            return lo_s, n + 1


        def load_contexts(role, eng, att, ready):
            if role == "sp":
                eng.wait_ge(*ready)
                for u in range(2):
                    eng.dma_start(CT[:, u, :], ctxT[u]).then_inc(sem(f"{att.name}_ctx{u}"), 16)

        def attention(role, eng, att, q_ready, src, banks_ready):
            plan, per_pair, n_jobs, lead, first_keys = bank_plan(att)
            t = att.name
            kind = t if att.cross else "self"
            W_, hg = att.W, att.hg
            Oall = (ABO[:, 6144:6144 + B * att.NO] if att.H == 8 else ABO[:, 0:B * att.NO]).rearrange(
                "p (b o) -> p b o", b=B)
            kst = KST if att.cross else KSS
            s_ctx = [sem(f"{kind}_ctx{i}") for i in range(2)]
            s_q = [sem(f"{kind}_q{i}") for i in range(2)]
            s_kst = [sem(f"{kind}_kst{i}") for i in range(2)]
            s_oout = [sem(f"{kind}_oout{i}") for i in range(2)]
            filled = sem(f"{kind}_filled")
            free = [sem(f"{kind}_free{i}") for i in range(WORK)]
            khi, mx, negm = sem(f"{kind}_khi"), sem(f"{kind}_mx"), sem(f"{kind}_negm")
            qbuilt, scores, exps, pv, oev = (sem(f"{kind}_{k}") for k in ("qbuilt", "scores", "exps", "pv", "oev"))
            ready = sem(f"{kind}_ready")
            kst_dmas = 12 if att.cross else 1
            rows = att.krows if att.masked else RAW

            counted = {}
            if att is SA1:
                for name, n in (("filled", n_jobs), ("mx", 1), ("negm", 1), ("qbuilt", 1), ("scores", att.NE),
                                ("exps", att.NE), ("pv", att.NE), ("oev", 1)):
                    counted[f"self_{name}"] = B * n
                for name in ("ctx", "q", "kst", "oout"):
                    for i in range(2):
                        counted[f"self_{name}{i}"] = B // 2 * 16
                for i in range(WORK):
                    counted[f"self_free{i}"] = B // 2 * per_pair[i]
                counted["self_ready"] = 1

            def base(s):
                return counted.get(s.name, 0)

            def settled(eng, role):
                eng.sem_inc(sem(f"{role}_settled"), 1)

            def half(b):
                if isinstance(b, int):
                    return b % 2, b // 2
                i, k = b
                return k % 2, i + k // 2

            def val(b):
                return b if isinstance(b, int) else b[0] * 2 + b[1]

            def cycle(b, job):
                if job[0] != "K":
                    return b
                return b - 1 if isinstance(b, int) else (b[0], b[1] - 1)

            def at_lead(b, job):
                return job[0] == "K" and isinstance(b, int) and b == 0

            def after_last_keys(b, job):
                return (att.cross and job[0] != "K" and isinstance(b, int) and b == B - 1
                        and plan[(0, job)][2] > plan[(0, ("K", 0))][2])

            def bank_of(b, job):
                if at_lead(b, job):
                    return first_keys[job[1]][0]
                return plan[(half(cycle(b, job))[0], job)][0]

            def filled_at(b, job):
                if at_lead(b, job):
                    return job[1] + 1
                c = cycle(b, job)
                keys = att.nk if after_last_keys(b, job) else 0
                return att.nk + val(c) * n_jobs + plan[(half(c)[0], job)][2] + 1 - keys

            def held_before(b, job):
                if at_lead(b, job):
                    return first_keys[job[1]][1]
                u, pair = half(cycle(b, job))
                bank, before, _ = plan[(u, job)]
                if after_last_keys(b, job):
                    before -= sum(plan[(u, ("K", j))][0] == bank for j in range(att.nk))
                return lead[bank] + pair * per_pair[bank] + before

            def freed_at(b, job):
                return held_before(b, job) + 1

            def is_first(b, n=1):
                return isinstance(b, int) and b < n

            def pe_step(main, prep, step):
                k, j = step
                if k == "S":
                    b = main
                    u, _ = half(b)
                    slot = (u * att.NE + j) % 2
                    if j == 0:
                        for r in range(att.rjobs):
                            eng.wait_ge(free[bank_of(b, ("R", r))], base(free[bank_of(b, ("R", r))]) + freed_at(b, ("R", r)))
                    if not (is_first(b) and j < 2):
                        eng.wait_ge(exps, base(exps) + val(b) * att.NE + j - 1)
                    for ti, tile in enumerate(att.exps[j]):
                        k0, n = att.tiles[tile]
                        for g in range(4):
                            col = ti * W_ + g * hg * S
                            mm = nc.tensor.matmul(
                                ps[0:n, 2 * slot + col // 512, col % 512:col % 512 + hg * S],
                                kst[0:att.krows, u, g, k0:k0 + n],
                                QW[0:att.krows, u, g * hg * S:(g + 1) * hg * S], start=True, stop=True)
                    mm.then_inc(scores, 1)
                if k == "P":
                    b = main
                    u, _ = half(b)
                    slot = (u * att.NE + j) % 2
                    if j == 0:
                        last_v = ("V", len(att.vjobs) - 1)
                        for v in range(max(0, last_v[1] - WORK + 1), last_v[1] + 1):
                            eng.wait_ge(free[bank_of(b, ("V", v))], base(free[bank_of(b, ("V", v))]) + freed_at(b, ("V", v)))
                        if not is_first(b):
                            eng.wait_ge(oev, base(oev) + val(b))
                        else:
                            eng.wait_ge(ready, base(ready) + 1)
                    eng.wait_ge(exps, base(exps) + val(b) * att.NE + j + 1)
                    if not att.cross:
                        settled(eng, role)
                    for ti, tile in enumerate(att.exps[j]):
                        _, n = att.tiles[tile]
                        for r, quad, h0, nh, v0, oc in att.groups:
                            m = nh * (att.d + 1)
                            mm = nc.tensor.matmul(
                                ps[32 * quad:32 * quad + m, 4, oc:oc + nh * S], V[0:n, u, tile, v0:v0 + m],
                                Pb[0:n, slot, ti * W_ + h0 * S:ti * W_ + (h0 + nh) * S],
                                start=(tile == 0 and r == 0), stop=(tile == len(att.tiles) - 1),
                                skip_group_check=True, tile_position=(0, 32 * quad))
                    mm.then_inc(pv, 1)
                if k in ("K", "V", "M", "R"):
                    b = prep
                    u, pair = half(b)
                    bank = bank_of(b, step)
                    before = held_before(b, step)
                    if not (isinstance(before, int) and before == 0):
                        eng.wait_ge(free[bank], base(free[bank]) + before)
                    pb = ps[:, 5 + bank, :]
                if k == "K":
                    if j == 0:
                        eng.wait_ge(s_ctx[u], base(s_ctx[u]) + pair * 16 + 16)
                    c0, n = att.kchunks[j]
                    nc.tensor.matmul(pb[:, 0:n], w(f"{t}_k"), CT[:, u, c0:c0 + n],
                                     start=True, stop=True).then_inc(filled, 1)
                if k == "V":
                    if j == 0 and not att.cross:
                        eng.wait_ge(s_ctx[u], base(s_ctx[u]) + pair * 16 + 16)
                    if not att.cross:
                        settled(eng, role)
                    kk = att.values_k
                    for i, tile in enumerate(att.vjobs[j]):
                        k0, n = att.tiles[tile]
                        mm = nc.tensor.matmul(pb[0:n, i * att.NV:(i + 1) * att.NV], CT[0:kk, u, k0:k0 + n],
                                              w(f"{t}_v", rows=kk), start=True, stop=True)
                    mm.then_inc(filled, 1)
                if k == "M":
                    if j == 0:
                        eng.wait_ge(qbuilt, base(qbuilt) + val(b) + 1)
                        eng.wait_ge(s_kst[u], base(s_kst[u]) + (pair + 1) * 16 * kst_dmas)
                    for i, (unit, c0, n) in enumerate(att.mjobs[j]):
                        mm = nc.tensor.matmul(pb[:, i * S:i * S + n], QW[0:rows, u, unit * 128:(unit + 1) * 128],
                                              kst[0:rows, u, 2 * unit // hg, c0:c0 + n], start=True, stop=True)
                    mm.then_inc(filled, 1)
                if k == "R":
                    if j == 0:
                        eng.wait_ge(negm, base(negm) + val(b) + 1)
                    for i in range(4):
                        mm = nc.tensor.matmul(ps[96:98, 5 + bank, i * 128:(i + 1) * 128], MH[:, u, j * 4 + i, :],
                                              wb("ident16"), start=True, stop=True, tile_position=(0, 96))
                    mm.then_inc(filled, 1)

            def act_step(main, prep, step):
                k, j = step
                if k == "E":
                    b = main
                    u, _ = half(b)
                    slot = (u * att.NE + j) % 2
                    n = att.tiles[att.exps[j][0]][1]
                    cols = len(att.exps[j]) * W_
                    if not (is_first(b, 2) and (b if isinstance(b, int) else 9) * att.NE + j < 2):
                        eng.wait_ge(pv, base(pv) + val(b) * att.NE + j - 1)
                    eng.wait_ge(scores, base(scores) + val(b) * att.NE + j + 1)
                    src_ps = ps[0:n, 2 * slot:2 * slot + 2, :].rearrange("p a c -> p (a c)")[:, 0:cols]
                    nc.scalar.activation(Pb[0:n, slot, 0:cols], src_ps, ACT.Exp, scale=att.scale).then_inc(exps, 1)
                if k == "O":
                    b = main
                    u, pair = half(b)
                    eng.wait_ge(pv, base(pv) + (val(b) + 1) * att.NE)
                    if not is_first(b, 2):
                        eng.wait_ge(s_oout[u], base(s_oout[u]) + pair * 16)
                    nc.scalar.activation(OE[:, u, 0:att.NO], ps[:, 4, 0:att.NO], ACT.Copy).then_inc(oev, 1)
                if k == "K":
                    b = prep
                    if j == 0 and not is_first(b):
                        up, pp = half(b - 1 if isinstance(b, int) else (b[0], b[1] - 1))
                        eng.wait_ge(s_kst[up], base(s_kst[up]) + (pp + 1) * 16 * kst_dmas)
                    c0, n = att.kchunks[j]
                    eng.wait_ge(filled, base(filled) + filled_at(b, step))
                    nc.scalar.activation(HL[:, 0, c0:c0 + n], ps[:, 5 + bank_of(b, step), 0:n], ACT.Identity,
                                         bias=bias(f"bk{t[-1]}")).then_inc(khi, 1)
                if k == "R":
                    b = prep
                    u, _ = half(b)
                    eng.wait_ge(filled, base(filled) + filled_at(b, step))
                    nc.scalar.activation(QW[96:98, u, j * 512:(j + 1) * 512], ps[96:98, 5 + bank_of(b, step), :],
                                         ACT.Copy).then_inc(free[bank_of(b, step)], 1)

            def dve_step(main, prep, step):
                k, j = step
                b = prep
                if k in ("K", "V", "M"):
                    u, pair = half(b)
                    bank = bank_of(b, step)
                    pb = ps[:, 5 + bank, :]
                if k == "K":
                    c0, n = att.kchunks[j]
                    eng.wait_ge(khi, base(khi) + val(b) * len(att.kchunks) + j + 1)
                    nc.vector.scalar_tensor_tensor(HL[:, 1, c0:c0 + n], pb[:, 0:n], bias(f"bk{t[-1]}"),
                                                   HL[:, 0, c0:c0 + n], ALU.add, ALU.subtract).then_inc(free[bank], 1)
                if k == "V":
                    eng.wait_ge(filled, base(filled) + filled_at(b, step))
                    if j == 0 and not is_first(b, 2):
                        eng.wait_ge(pv, base(pv) + (val(b) - 1) * att.NE)
                    ts = att.vjobs[j]
                    n = att.tiles[ts[0]][1]
                    nc.vector.tensor_tensor(
                        V[0:n, u, ts[0]:ts[0] + len(ts), 0:att.NV],
                        pb[0:n, 0:len(ts) * att.NV].rearrange("p (t v) -> p t v", t=len(ts)),
                        w(f"{t}_vb")[0:n, :].unsqueeze(1).broadcast_to([n, len(ts), att.NV]),
                        ALU.add).then_inc(free[bank], 1)
                if k == "M":
                    eng.wait_ge(filled, base(filled) + filled_at(b, step))
                    m = len(att.mjobs[j])
                    if j == 0 and not is_first(b, 2):
                        eng.wait_ge(negm, base(negm) + val(b) - 1)
                    src_ps = pb[:, 0:att.mjobs[j][0][2]] if m == 1 else pb[:, 0:m * S].rearrange("p (a c) -> p a c", a=m)
                    nc.vector.reduce_max(MX[:, u, j * m:(j + 1) * m], src_ps, AX.X).then_inc(free[bank], 1)
                if k == "Z":
                    u, pair = half(b)
                    for m in range(max(0, len(att.mjobs) - WORK), len(att.mjobs)):
                        eng.wait_ge(free[bank_of(b, ("M", m))], base(free[bank_of(b, ("M", m))]) + freed_at(b, ("M", m)))
                    top = MX[:, u, 0:att.units]
                    if att.cross:
                        top = MG[:, u, 0:att.units]
                        nc.vector.reduce_max(top, MX[:, u, 0:att.units * 4].rearrange("p (a c) -> p a c", c=4),
                                             AX.X).then_inc(mx, 1)
                        eng.wait_ge(mx, base(mx) + val(b) * 2 + 1)
                    if not is_first(b, 2):
                        for r in range(att.rjobs):
                            bb = b - 2 if isinstance(b, int) else (b[0] - 1, b[1])
                            eng.wait_ge(free[bank_of(b, ("R", r))], base(free[bank_of(b, ("R", r))]) + freed_at(bb, ("R", r)))
                    nc.vector.tensor_scalar(MH[:, u, 0:att.units, 0], top, -1.0, None, ALU.mult).then_inc(mx, 1)
                    eng.wait_ge(mx, base(mx) + ((val(b) + 1) * (2 if att.cross else 1)))
                    nc.vector.scalar_tensor_tensor(MH[:, u, 0:att.units, 1], top, -1.0, MH[:, u, 0:att.units, 0],
                                                   ALU.mult, ALU.subtract).then_inc(negm, 1)

            def pool_item(b):
                u, pair = half(b)
                eng.wait_ge(s_q[u], base(s_q[u]) + (pair + 1) * 16)
                if not is_first(b, 2):
                    eng.wait_ge(scores, base(scores) + (val(b) - 1) * att.NE)
                settled(eng, role)
                hm = wb("hm2" if hg == 2 else "hm4", rows=rows)
                out = QW[0:rows, u, 0:W_].rearrange("p (g h q) -> p g h q", g=4, h=hg)
                q4 = QSL[0:rows, u, :, :].unsqueeze(2).broadcast_to([rows, 4, hg, S])
                m4 = hm.unsqueeze(1).unsqueeze(3).broadcast_to([rows, 4, hg, S])
                nc.gpsimd.tensor_tensor(out, q4, m4, ALU.mult).then_inc(qbuilt, 1)

            def sp_context(b):
                u, pair = half(b)
                if not is_first(b, 2):
                    bb = b - 2 if isinstance(b, int) else (b[0] - 1, b[1])
                    last_v = ("V", len(att.vjobs) - 1)
                    eng.wait_ge(filled, base(filled) + filled_at(bb, last_v))
                    settled(eng, role)
                if not att.cross:
                    kk = att.values_k
                    eng.dma_start(CT[0:kk, u, 0:S], src[0:kk, bass.ds(val(b) * S, S)]).then_inc(s_ctx[u], 16)
                elif not is_first(b, 2):
                    eng.dma_start(CT[:, u, :], ctxT[val(b)]).then_inc(s_ctx[u], 16)

            def sp_queries(b):
                u, pair = half(b)
                if not is_first(b, 2):
                    eng.wait_ge(qbuilt, base(qbuilt) + val(b) - 1)
                    settled(eng, role)
                eng.dma_start(QSL[0:rows, u, :, :], QS[0:rows, :, bass.ds(val(b) * S, S)]).then_inc(s_q[u], 16)

            def sp_keys(b):
                u, pair = half(b)
                if not att.cross:
                    if not is_first(b, 2):
                        eng.wait_ge(scores, base(scores) + (val(b) - 1) * att.NE)
                        settled(eng, role)
                    eng.dma_start(KSS[0:rows, u, :, :], KSA[0:rows, :, bass.ds(val(b) * S, S)]).then_inc(s_kst[u], 16)

            def sp_stack(b):
                u, pair = half(b)
                if not is_first(b, 2):
                    eng.wait_ge(scores, base(scores) + (val(b) - 1) * att.NE)
                    settled(eng, role)
                for j in range(max(0, 4 - WORK), 4):
                    eng.wait_ge(free[bank_of(b, ("K", j))], base(free[bank_of(b, ("K", j))]) + freed_at(b, ("K", j)))
                    settled(eng, role)
                for p, part in enumerate((0, 1, 0)):
                    for g in range(4):
                        ins = eng.dma_start(KST[32 * p:32 * p + 32, u, g, :], HL[32 * g:32 * g + 32, part, 0:NK])
                        ins.then_inc(s_kst[u], 16)

            def sp_out(b):
                u, pair = half(b)
                eng.wait_ge(oev, base(oev) + val(b) + 1)
                settled(eng, role)
                eng.dma_start(Oall[:, val(b), :] if isinstance(b, int) else Oall[:, bass.ds(val(b), 1), :],
                              OE[:, u, 0:att.NO] if isinstance(b, int) else OE[:, u, 0:att.NO].unsqueeze(1)
                              ).then_inc(s_oout[u], 16)

            if role == "dve":
                eng.wait_ge(*banks_ready)
                nc.vector.memset(ps[:, 4, :], 0.0).then_inc(ready, 1)
            if role == "pe" and att is not SA1:
                eng.wait_ge(sem("ones_set"), 3)
            if role == "pool" or (role == "sp" and not att.cross):
                eng.wait_ge(*q_ready)
            if role == "sp" and att.masked:
                eng.wait_ge(sem("mask_rows"), 16 * (2 if att is SA0 else 2 + 8))

            step_of = {"pe": pe_step, "act": act_step, "dve": dve_step}
            if role in step_of:
                f = step_of[role]

                def item(main, prep, keys):
                    for step in att.merged(main is not None, prep is not None, keys is not None):
                        f(main, keys if step[0] == "K" else prep, step)
                if att.cross:
                    item(None, None, 0)
                item(None, 0, 1)
                item(0, 1, 2)
                item(1, 2, 3)
                with eng.Fori(1, B // 2 - 1) as i:
                    item((i, 0), (i, 1), (i, 2))
                    item((i, 1), (i, 2), (i, 3))
                item(B - 2, B - 1, None)
                item(B - 1, None, None)
            if role == "pool":
                pool_item(0)
                pool_item(1)
                with eng.Fori(1, B // 2) as i:
                    pool_item((i, 0))
                    pool_item((i, 1))
            if role == "sp":
                def sp_item(main, ahead):
                    if ahead is not None:
                        sp_context(ahead)
                        if att.cross and is_first(ahead):
                            sp_stack(ahead)
                            eng.wait_ge(*q_ready)
                        sp_queries(ahead)
                        if att.cross and not is_first(ahead):
                            sp_stack(ahead)
                    if main is not None:
                        sp_out(main)
                def sp_self(main, ahead):
                    if ahead is not None:
                        sp_context(ahead)
                        sp_queries(ahead)
                    if main is not None:
                        sp_out(main)
                    if ahead is not None:
                        sp_keys(ahead)
                if att.cross:
                    sp_item(None, 0)
                    sp_item(None, 1)
                    sp_item(0, 2)
                    sp_item(1, 3)
                    with eng.Fori(1, B // 2 - 1) as i:
                        sp_item((i, 0), (i, 2))
                        sp_item((i, 1), (i, 3))
                    sp_item(B - 2, None)
                    sp_item(B - 1, None)
                else:
                    sp_self(None, 0)
                    sp_self(None, 1)
                    sp_self(None, 2)
                    sp_self(0, 3)
                    sp_self(1, 4)
                    with eng.Fori(1, B // 2 - 2) as i:
                        sp_self((i, 0), (i, 3))
                        sp_self((i, 1), (i, 4))
                    sp_self(B - 4, B - 1)
                    sp_self(B - 3, None)
                    sp_self(B - 2, None)
                    sp_self(B - 1, None)
            return s_oout

        def attention_out(role, eng, att, call, wname, den, bname, dst, residual):
            t = att.name
            Oall = (ABO[:, 6144:6144 + B * att.NO] if att.H == 8 else ABO[:, 0:B * att.NO]).rearrange(
                "p (b o) -> p b o", b=B)
            s_oout = [sem(f"{t if att.cross else 'self'}_oout{i}") for i in range(2)]
            scaled_s, sel_s, den_s, rec_s, turned_s, flat_s, spread_s, on_s, pe_s, out_s = (
                sem(f"ao_{k}") for k in ("scaled", "sel", "den", "rec", "turned", "flat", "spread", "on", "pe", "out"))
            SEL = Pb[:, :, :]
            nb = CH // S
            H = att.H
            n = call * NC
            more = sum(att.blocks) - 2
            sel_before = NC * sum(sum(a.blocks) - 2 for a in (XA0, SA0, XA1)[:call])
            ms = W_AT["m_sel"][0]

            def sel(r, c):
                return SEL[:, r, (c % 2) * CH:(c % 2 + 1) * CH]

            def block(r, h, c):
                return Oall[:, nb * c:nb * (c + 1), att.bases[r] + h * S:att.bases[r] + (h + 1) * S]

            def by_item(x):
                return x.rearrange("p (b q) -> p b q", b=nb)

            def select(c):
                if role == "act":
                    if c == 0:
                        for s in s_oout:
                            eng.wait_ge(s, 16 * B // 2 * (2 if att is SA1 else 1))
                    if c >= 2:
                        eng.wait_ge(pe_s, n + c - 1)
                    for r in range(2):
                        nc.scalar.activation(by_item(sel(r, c)), block(r, 0, c), ACT.Copy,
                                             scale=1.0 if H == 8 else W[:, ms + 4 * r:ms + 4 * r + 1]
                                             ).then_inc(scaled_s, 1)
                if role == "dve":
                    done = 0
                    for r in range(2):
                        eng.wait_ge(scaled_s, 2 * (n + c) + r + 1)
                        for h in range(1, att.blocks[r]):
                            if h > 1:
                                eng.wait_ge(sel_s, sel_before + c * more + done)
                            nc.vector.scalar_tensor_tensor(
                                by_item(sel(r, c)), block(r, h, c), W[:, ms + 4 * r + h:ms + 4 * r + h + 1],
                                by_item(sel(r, c)), ALU.mult, ALU.add).then_inc(sel_s, 1)
                            done += 1

            def denominators(c):
                if role == "pe":
                    eng.wait_ge(scaled_s, 2 * (n + c) + 2)
                    if more:
                        eng.wait_ge(sel_s, sel_before + (c + 1) * more)
                    for i in range(4):
                        for r in range(2):
                            mm = nc.tensor.matmul(lo_bank(c)[:, i * H:(i + 1) * H], sel(r, c)[:, i * 128:(i + 1) * 128],
                                                  w(den, r * 16, r * 16 + H), start=(r == 0), stop=(r == 1))
                    mm.then_inc(den_s, 1)
                if role == "dve":
                    eng.wait_ge(den_s, n + c + 1)
                    if c:
                        eng.wait_ge(turned_s, n + c)
                    nc.vector.reciprocal(COL[:, 0:4 * H], lo_bank(c)[:, 0:4 * H]).then_inc(rec_s, 1)
                if role == "pe":
                    eng.wait_ge(rec_s, n + c + 1)
                    for i in range(4):
                        mm = nc.tensor.matmul(hi_bank(c)[0:H, i * 128:(i + 1) * 128], COL[:, i * H:(i + 1) * H],
                                              w("ident"), start=True, stop=True)
                    mm.then_inc(turned_s, 1)
                if role == "act":
                    if c >= 2:
                        eng.wait_ge(spread_s, 2 * (n + c) - 2)
                    eng.wait_ge(turned_s, n + c + 1)
                    nc.scalar.activation(ROW[0:H, c % 2, :], hi_bank(c)[0:H, :], ACT.Copy).then_inc(flat_s, 1)
                if role == "pe":
                    eng.wait_ge(flat_s, n + c + 1)
                    for r in range(2):
                        nc.tensor.matmul(lo_bank(c) if r == 0 else hi_bank(c), w(den, 32 + r * D, 32 + (r + 1) * D, rows=H),
                                         ROW[0:H, c % 2, :], start=True, stop=True).then_inc(spread_s, 1)

            def project(c):
                if role == "dve":
                    for r in range(2):
                        eng.wait_ge(spread_s, 2 * (n + c) + r + 1)
                        nc.vector.tensor_tensor(sel(r, c), sel(r, c), lo_bank(c) if r == 0 else hi_bank(c),
                                                ALU.mult).then_inc(on_s, 1)
                if role == "pe":
                    for r in range(2):
                        eng.wait_ge(on_s, 2 * (n + c) + r + 1)
                        mm = nc.tensor.matmul(lo_bank(c), w(wname, r * D, (r + 1) * D), sel(r, c),
                                              start=(r == 0), stop=(r == 1))
                    mm.then_inc(pe_s, 1)

            def store(c):
                if role == "dve":
                    eng.wait_ge(pe_s, n + c + 1)
                    if bname is None:
                        ins = nc.vector.tensor_tensor(ck(dst, c), lo_bank(c), ck(residual, c), ALU.add)
                    else:
                        ins = nc.vector.scalar_tensor_tensor(ck(dst, c), lo_bank(c), bias(bname), ck(residual, c),
                                                             ALU.add, ALU.add)
                    ins.then_inc(out_s, 1)

            select(0)
            denominators(0)
            for c in range(NC):
                if c + 1 < NC and c % 2 == 0:
                    select(c + 1)
                    denominators(c + 1)
                project(c)
                store(c)
                if c + 1 < NC and c % 2 == 1:
                    select(c + 1)
                    denominators(c + 1)
            return out_s, n + 1


        def diagonal_attention(role, eng, ready):
            s = {k: sem(f"dg_{k}") for k in ("q", "k", "v", "qev", "prod", "s", "top", "rel", "e", "rec", "vev", "p",
                                             "an", "o", "out")}
            root = float(np.sqrt(np.float32(D)))
            for c in range(NC):
                if role == "pe":
                    eng.wait_ge(ready[0], ready[1] + c)
                    nc.tensor.matmul(lo_bank(c), w("c_q"), ck(T, c), start=True, stop=True).then_inc(s["q"], 1)
                    nc.tensor.matmul(hi_bank(c), w("c_k"), ck(T, c), start=True, stop=True).then_inc(s["k"], 1)
                if role == "act":
                    eng.wait_ge(s["q"], c + 1)
                    nc.scalar.activation(ck(A, c), lo_bank(c), ACT.Identity, bias=bias("c_bq")).then_inc(s["qev"], 1)
                if role == "dve":
                    eng.wait_ge(s["qev"], c + 1)
                    eng.wait_ge(s["k"], c + 1)
                    nc.vector.scalar_tensor_tensor(ck(A, c), hi_bank(c), bias("c_bk"), ck(A, c),
                                                   ALU.add, ALU.mult).then_inc(s["prod"], 1)
            for c in range(NC):
                if role == "pe":
                    eng.wait_ge(s["prod"], c + 1)
                    nc.tensor.matmul(lo_bank(c), w("c_v"), ck(T, c), start=True, stop=True).then_inc(s["v"], 1)
                    for i in range(4):
                        t = 4 * c + i
                        mm = nc.tensor.matmul(hi_bank(c // 2 * 2)[:, t % 8:t % 8 + 1], A[:, t * 128:(t + 1) * 128],
                                              w("ones", 0, 1), start=True, stop=True)
                    if c % 2:
                        mm.then_inc(s["s"], 1)
                if role == "act":
                    eng.wait_ge(s["v"], c + 1)
                    nc.scalar.activation(ck(Bt, c), lo_bank(c), ACT.Identity, bias=bias("c_bv")).then_inc(s["vev"], 1)
            for h in range(2):
                cols = slice(8 * h, 8 * h + 8)
                if role == "dve":
                    eng.wait_ge(s["s"], h + 1)
                    nc.vector.tensor_scalar(DEV[:, cols], hi_bank(2 * h)[:, 0:8], root, None, ALU.mult
                                            ).then_inc(s["top"], 1)
                    eng.wait_ge(s["top"], h + 1)
                    nc.vector.scalar_tensor_tensor(COL[:, cols], hi_bank(2 * h)[:, 0:8], root, DEV[:, cols],
                                                   ALU.mult, ALU.subtract).then_inc(s["rel"], 1)
                if role == "act":
                    eng.wait_ge(s["rel"], h + 1)
                    nc.scalar.activation(COL[:, cols], COL[:, cols], ACT.Exp).then_inc(s["e"], 1)
            for h in range(2):
                cols = slice(8 * h, 8 * h + 8)
                if role == "dve":
                    eng.wait_ge(s["e"], h + 1)
                    nc.vector.reciprocal(DEV[:, cols], COL[:, cols]).then_inc(s["rec"], 1)
                    eng.wait_ge(s["rec"], h + 1)
                    nc.vector.tensor_tensor(COL[:, cols], COL[:, cols], DEV[:, cols], ALU.mult).then_inc(s["p"], 1)
            for c in range(NC):
                spread_s, first = spread(role, eng, 1, c, (s["p"], c // 2 + 1))
            for c in range(NC):
                if role == "dve":
                    eng.wait_ge(s["vev"], c + 1)
                    eng.wait_ge(spread_s, first + c)
                    nc.vector.tensor_tensor(ck(A, c), ck(Bt, c), hi_bank(c), ALU.mult).then_inc(s["an"], 1)
                if role == "pe":
                    eng.wait_ge(s["an"], c + 1)
                    nc.tensor.matmul(lo_bank(c), w("c_o"), ck(A, c), start=True, stop=True).then_inc(s["o"], 1)
            for c in range(NC):
                if role == "dve":
                    eng.wait_ge(s["o"], c + 1)
                    nc.vector.scalar_tensor_tensor(ck(A, c), lo_bank(c), bias("c_bo"), ck(T, c),
                                                   ALU.add, ALU.add).then_inc(s["out"], 1)
            return s["out"], 1

        def dense_ff(role, eng, ready):
            s = {k: sem(f"ff_{k}") for k in ("h", "relu", "y", "out")}
            nf = FF // D
            for f in range(nf + 1):
                for c in range(NC):
                    buf = Bt if f % 2 == 0 else C
                    if f < nf:
                        if role == "pe":
                            if f == 0:
                                eng.wait_ge(ready[0], ready[1] + c)
                            else:
                                eng.wait_ge(s["relu"], (f - 1) * NC + c + 1)
                            nc.tensor.matmul(hi_bank(c), w("lin1", f * D, (f + 1) * D), ck(T, c),
                                             start=True, stop=True).then_inc(s["h"], 1)
                        if role == "act":
                            if f >= 2:
                                eng.wait_ge(s["y"], (f - 2) * NC + c + 1)
                            eng.wait_ge(s["h"], f * NC + c + 1)
                            nc.scalar.activation(ck(buf, c), hi_bank(c), ACT.Relu,
                                                 bias=bias(f"l1b{f}")).then_inc(s["relu"], 1)
                    if f > 0 and role == "pe":
                        g = f - 1
                        buf = Bt if g % 2 == 0 else C
                        eng.wait_ge(s["relu"], g * NC + c + 1)
                        nc.tensor.matmul(lo_bank(c), w("lin2", g * D, (g + 1) * D), ck(buf, c),
                                         start=(g == 0), stop=(g == nf - 1)).then_inc(s["y"], 1)
            for c in range(NC):
                if role == "dve":
                    eng.wait_ge(s["y"], (nf - 1) * NC + c + 1)
                    nc.vector.scalar_tensor_tensor(ck(A, c), lo_bank(c), bias("l2b"), ck(T, c),
                                                   ALU.add, ALU.add).then_inc(s["out"], 1)
            return s["out"], 1

        def add_to_stream(role, eng, ready):
            s = sem("l0_added")
            if role == "dve":
                for c in range(NC):
                    eng.wait_ge(ready[0], ready[1] + c)
                    nc.vector.tensor_tensor(ck(X, c), ck(X, c), ck(T, c), ALU.add).then_inc(s, 1)
            return s, 1

        def rotary(role, eng, call, wname, rows, srcT, ready, parts):
            s = {k: sem(f"rot_{k}") for k in ("pe", "cos", "sin", "rot", "hi", "lo")}
            n = call * NC
            o = W_AT["rope"][0]
            nb = CH // S
            for c in range(NC):
                if role == "pe":
                    eng.wait_ge(ready[0], ready[1] + c)
                    nc.tensor.matmul(lo_bank(c), w(wname, 0, D, rows=rows), srcT[0:rows, c * CH:(c + 1) * CH],
                                     start=True, stop=True)
                    nc.tensor.matmul(hi_bank(c), w(wname, D, 2 * D, rows=rows), srcT[0:rows, c * CH:(c + 1) * CH],
                                     start=True, stop=True).then_inc(s["pe"], 1)
                if role == "dve":
                    def tab(k):
                        return W[:, o + k * S:o + (k + 1) * S].unsqueeze(1).broadcast_to([128, nb, S])
                    eng.wait_ge(s["pe"], n + c + 1)
                    nc.vector.tensor_tensor(ck(A, c).rearrange("p (b q) -> p b q", b=nb),
                                            lo_bank(c).rearrange("p (b q) -> p b q", b=nb), tab(0), ALU.mult
                                            ).then_inc(s["cos"], 1)
                    nc.vector.tensor_tensor(ck(Bt, c).rearrange("p (b q) -> p b q", b=nb),
                                            hi_bank(c).rearrange("p (b q) -> p b q", b=nb), tab(1), ALU.mult
                                            ).then_inc(s["sin"], 1)
                    eng.wait_ge(s["cos"], n + c + 1)
                    eng.wait_ge(s["sin"], n + c + 1)
                    nc.vector.tensor_tensor(ck(A, c), ck(A, c), ck(Bt, c), ALU.add).then_inc(s["rot"], 1)
                if role == "act":
                    eng.wait_ge(s["rot"], n + c + 1)
                    nc.scalar.activation(ck(parts[:, 0, :], c), ck(A, c), ACT.Copy).then_inc(s["hi"], 1)
            for c in range(NC):
                if role == "dve":
                    eng.wait_ge(s["hi"], n + c + 1)
                    nc.vector.tensor_tensor(ck(parts[:, 1, :], c), ck(A, c), ck(parts[:, 0, :], c),
                                            ALU.subtract).then_inc(s["lo"], 1)
            return s["lo"], n + 1

        def moe_stage(role, eng, ready):
            s = {k: sem(f"moe_{k}") for k in ("logit", "score", "chain", "parts", "turned", "weights", "gu", "gate",
                                             "hid", "mid", "down", "out")}
            NT = N // 128
            at = [0]

            def area(n):
                at[0] += n
                return ABO[:, at[0] - n:at[0]]

            SC = area(NT * E).rearrange("p (t e) -> p t e", t=NT)
            SFC = area(NT * E).rearrange("p (t e) -> p t e", t=NT)
            GSC = area(NT * 12).rearrange("p (t e) -> p t e", t=NT)
            GM8 = area(NT * 8).rearrange("p (t e) -> p t e", t=NT)
            GR = area(NT * 12).rearrange("p (t e) -> p t e", t=NT)
            GM = area(NT * 8).rearrange("p (t e) -> p t e", t=NT)
            MK = area(NT * 34).rearrange("p (t e) -> p t e", t=NT)
            MK8 = area(NT * 8).rearrange("p (t e) -> p t e", t=NT)
            MR = area(NT * 34).rearrange("p (t e) -> p t e", t=NT)
            TW = area(NT * E).rearrange("p (t e) -> p t e", t=NT)
            SM = area(NT)
            CBS = area(NT * E).bitcast(BF16).rearrange("p (t e) -> p t e", t=NT)
            CTT = HL[0:2 * E, 0, :]

            if role == "pe":
                for c in range(NC):
                    eng.wait_ge(ready[0], ready[1] + c)
                for t in range(NT):
                    mm = nc.tensor.matmul(ps[:, 0, t * E:(t + 1) * E], T[:, t * 128:(t + 1) * 128], w("gate"),
                                          start=True, stop=True)
                mm.then_inc(s["logit"], 1)
            if role == "act":
                eng.wait_ge(s["logit"], 1)
                nc.scalar.activation(SC, ps[:, 0, :].rearrange("p (t e) -> p t e", t=NT), ACT.Sigmoid
                                     ).then_inc(s["score"], 1)
            if role == "dve":
                n = [0]

                def link(ins, wait=True):
                    n[0] += 1
                    ins.then_inc(s["chain"], 1)
                    if wait:
                        eng.wait_ge(s["chain"], n[0])

                eng.wait_ge(s["score"], 1)
                link(nc.vector.tensor_tensor(SFC, SC, w("gate_b").unsqueeze(1).broadcast_to([128, NT, E]), ALU.add))
                link(nc.vector.memset(GSC[:, :, NG:12], BIG))
                link(nc.vector.memset(MK[:, :, E:34], BIG))
                link(nc.vector.reduce_max(GSC[:, :, 0:NG], SFC.rearrange("p t (g s) -> p t g s", g=NG), AX.X))
                for t in range(NT):
                    link(nc.vector.max(GM8[:, t, :], GSC[:, t, :]), t == NT - 1)
                for t in range(NT):
                    link(nc.vector.match_replace(GR[:, t, :], GM8[:, t, :], GSC[:, t, :], -BIG), t == NT - 1)
                link(nc.vector.tensor_scalar(GM, GR[:, :, 0:NG], -BIG, None, ALU.is_equal))
                link(nc.vector.tensor_tensor(MK[:, :, 0:E].rearrange("p t (g s) -> p t g s", g=NG),
                                             SFC.rearrange("p t (g s) -> p t g s", g=NG),
                                             GM.unsqueeze(3).broadcast_to([128, NT, NG, GS]), ALU.mult))
                link(nc.vector.tensor_scalar(MK[:, :, 0:E], MK[:, :, 0:E], 0.0, None, ALU.add))
                for t in range(NT):
                    link(nc.vector.max(MK8[:, t, :], MK[:, t, :]), t == NT - 1)
                for t in range(NT):
                    link(nc.vector.match_replace(MR[:, t, :], MK8[:, t, :], MK[:, t, :], -BIG), t == NT - 1)
                link(nc.vector.tensor_scalar(MR[:, :, 0:E], MR[:, :, 0:E], -BIG, None, ALU.is_equal))
                link(nc.vector.tensor_tensor(TW, SC, MR[:, :, 0:E], ALU.mult))
                link(nc.vector.reduce_sum(SM, TW, AX.X))
                link(nc.vector.tensor_scalar(SM, SM, 1e-20, None, ALU.add))
                link(nc.vector.reciprocal(SM, SM))
                link(nc.vector.tensor_tensor(TW, TW, SM.unsqueeze(2).broadcast_to([128, NT, E]), ALU.mult))
                link(nc.vector.tensor_scalar(TW, TW, ROUTE_SCALE, None, ALU.mult))
                link(nc.vector.tensor_copy(CBS[:, :, 0:E], TW))
                nc.vector.tensor_tensor(CBS[:, :, E:2 * E], TW, CBS[:, :, 0:E], ALU.subtract).then_inc(s["parts"], 1)
            if role == "act":
                eng.wait_ge(s["turned"], 1)
                for i in range(2):
                    nc.scalar.activation(CTT[:, i * 1024:(i + 1) * 1024], ps[0:2 * E, 6 + i, :].bitcast(BF16), ACT.Copy
                                         ).then_inc(s["weights"], 1)

            NI = E // 2 + 1
            loads = [sem(f"moe_load{i}") for i in range(SLOTS)]

            def ew(item_slot, k):
                if item_slot is None:
                    return w("shared", k * D, (k + 1) * D)
                return CT[:, item_slot // 2, (item_slot % 2 * 3 + k) * D:(item_slot % 2 * 3 + k + 1) * D]

            def unit(sweep, item, cc):
                return (item + sweep * NI) * 2 + cc

            def up(sweep, item, slot, cc):
                x = ck(T, 2 * sweep + cc)
                if cc == 0 and slot is not None:
                    eng.wait_ge(loads[slot], (sweep * (NI - 1) * 32 // SLOTS) + ((item - 1 - slot) * (32 // SLOTS)) + 32)
                if sweep or not (isinstance(item, int) and item == 0):
                    eng.wait_ge(s["hid"], unit(sweep, item, cc) - 1)
                if not sweep and slot == 0 and isinstance(item, int) and cc == 0:
                    eng.wait_ge(s["weights"], 2)
                nc.tensor.matmul(ps[:, 2 + cc, :], ew(slot, 0), x, start=True, stop=True)
                mm = nc.tensor.matmul(ps[:, 4 + cc, :], ew(slot, 1), x, start=True, stop=True)
                if slot is not None:
                    mm = nc.tensor.matmul(ps[:, 6 + cc, :], HL[0:2 * E, 1, slot * 128:(slot + 1) * 128],
                                          ck(CTT, 2 * sweep + cc), start=True, stop=True)
                mm.then_inc(s["gu"], 1)

            def down(sweep, item, slot, cc, last=False):
                c = 2 * sweep + cc
                if slot is None:
                    if sweep:
                        eng.wait_ge(s["out"], cc + 1)
                    nc.tensor.matmul(ps[:, cc, :], w("ident"), ck(X, c), start=True, stop=False)
                eng.wait_ge(s["hid"], unit(sweep, item, cc) + 1)
                nc.tensor.matmul(ps[:, cc, :], ew(slot, 2), Pb[:, 1, cc * CH:(cc + 1) * CH],
                                 start=False, stop=last).then_inc(s["down"], 1)

            def pe_item(sweep, item, slot, prev, prev_slot):
                for cc in range(2):
                    up(sweep, item, slot, cc)
                    down(sweep, prev, prev_slot, cc)

            def act_item(sweep, item):
                for cc in range(2):
                    eng.wait_ge(s["gu"], unit(sweep, item, cc) + 1)
                    nc.scalar.activation(Pb[:, 0, cc * CH:(cc + 1) * CH], ps[:, 2 + cc, :], ACT.Silu
                                         ).then_inc(s["gate"], 1)

            def dve_item(sweep, item, shared=False):
                for cc in range(2):
                    h = Pb[:, 1, cc * CH:(cc + 1) * CH]
                    eng.wait_ge(s["gate"], unit(sweep, item, cc) + 1)
                    if sweep or not (isinstance(item, int) and item == 0):
                        eng.wait_ge(s["down"], unit(sweep, item, cc) - 1)
                    ins = nc.vector.tensor_tensor(h, ps[:, 4 + cc, :], Pb[:, 0, cc * CH:(cc + 1) * CH], ALU.mult)
                    if not shared:
                        ins.then_inc(s["mid"], 1)
                        eng.wait_ge(s["mid"], unit(sweep, item, cc) + 1 - 2 * (sweep + 1))
                        ins = nc.vector.tensor_tensor(h, h, ps[:, 6 + cc, :], ALU.mult)
                    ins.then_inc(s["hid"], 1)

            def sp_item(sweep, item, slot):
                if not isinstance(item, int):
                    eng.wait_ge(s["down"], unit(sweep, item, 0) - 2 * SLOTS + 2)
                elif sweep:
                    eng.wait_ge(s["down"], unit(sweep, item, 0) - 2 * SLOTS)
                eng.dma_start(CT[:, slot // 2, slot % 2 * 3 * D:(slot % 2 + 1) * 3 * D], experts[item - 1]
                              ).then_inc(loads[slot], 16)
                eng.dma_start(HL[0:2 * E, 1, slot * 128:(slot + 1) * 128], picks[item - 1]).then_inc(loads[slot], 16)

            if role == "sp":
                eng.wait_ge(ready[0], ready[1])
            for sweep in range(2):
                if role == "pe":
                    up(sweep, 0, None, 0)
                    up(sweep, 0, None, 1)
                    if sweep == 0:
                        eng.wait_ge(s["parts"], 1)
                        for t in range(NT):
                            tr = nc.tensor.transpose(ps[0:2 * E, 6 + t // 8, :].bitcast(BF16)[:, t % 8 * 128:(t % 8 + 1) * 128],
                                                     CBS[:, t, :], wb("ident16"))
                        tr.then_inc(s["turned"], 1)
                    pe_item(sweep, 1, 0, 0, None)
                    for k in range(1, SLOTS):
                        pe_item(sweep, k + 1, k, k, k - 1)
                    with eng.Fori(1, NI // SLOTS) as i:
                        for k in range(SLOTS):
                            pe_item(sweep, i * SLOTS + (k + 1), k, i * SLOTS + k, (k - 1) % SLOTS)
                    for cc in range(2):
                        down(sweep, NI - 1, SLOTS - 1, cc, last=True)
                if role == "act":
                    act_item(sweep, 0)
                    with eng.Fori(0, NI // 2) as i:
                        act_item(sweep, i * 2 + 1)
                        act_item(sweep, i * 2 + 2)
                if role == "dve":
                    dve_item(sweep, 0, shared=True)
                    with eng.Fori(0, NI // 2) as i:
                        dve_item(sweep, i * 2 + 1)
                        dve_item(sweep, i * 2 + 2)
                    for cc in range(2):
                        eng.wait_ge(s["down"], unit(sweep, NI - 1, cc) + 1)
                        nc.vector.tensor_copy(ck(X, 2 * sweep + cc), ps[:, cc, :]).then_inc(s["out"], 1)
                if role == "sp":
                    for k in range(SLOTS):
                        sp_item(sweep, k + 1, k)
                    with eng.Fori(1, NI // SLOTS) as i:
                        for k in range(SLOTS):
                            sp_item(sweep, i * SLOTS + (k + 1), k)
            return s["out"], 1

        def tree_stage(role, eng, ready):
            s = {k: sem(f"tree_{k}") for k in ("log", "dec", "acts", "path", "msk", "down", "out")}
            loads = [sem(f"tree_load{i}") for i in range(SLOTS)]
            WOFF = (0, INNER, NODES, NODES + D, NODES + 2 * D)
            TCOLS = WOFF[4] + 2
            tree_c = B_AT["tree"][0]

            def tw(slot, k, rows=128, cols=128):
                o = slot % 2 * TCOLS + WOFF[k]
                return CT[0:rows, slot // 2, o:o + cols]

            def unit(sweep, tree, cc):
                return (tree + sweep * TREES) * 2 + cc

            def logits(sweep, tree, slot, cc):
                if cc == 0:
                    eng.wait_ge(loads[slot], sweep * 16 * TREES // SLOTS + (tree - slot) * (16 // SLOTS) + 16)
                x = ck(T, 2 * sweep + cc)
                nc.tensor.matmul(ps[0:INNER, 2 + cc, :], tw(slot, 0, cols=INNER), x, start=True, stop=True)
                nc.tensor.matmul(ps[:, 4 + cc, :], tw(slot, 1), x, start=True, stop=True).then_inc(s["log"], 1)

            def paths(sweep, tree, cc):
                eng.wait_ge(s["dec"], unit(sweep, tree, cc) + 1)
                nc.tensor.matmul(ps[0:INNER, 6, :], WB[0:INNER, tree_c:tree_c + INNER], DEC[0:INNER, cc, :],
                                 start=True, stop=True)
                nc.tensor.matmul(ps[:, 7, :], WB[0:INNER, tree_c + INNER:tree_c + NODES], DEC[0:INNER, cc, :],
                                 start=True, stop=True).then_inc(s["path"], 1)

            def down(sweep, tree, slot, cc, first=False, last=False):
                eng.wait_ge(s["msk"], (unit(sweep, tree, cc) + 1) * 2)
                if first:
                    if sweep:
                        eng.wait_ge(s["out"], cc + 1)
                    nc.tensor.matmul(ps[:, cc, :], w("ident"), ck(X, 2 * sweep + cc), start=True, stop=False)
                nc.tensor.matmul(ps[:, cc, :], tw(slot, 2, rows=INNER), Pb[0:INNER, cc, 0:CH], start=False, stop=False)
                nc.tensor.matmul(ps[:, cc, :], tw(slot, 3), Pb[:, cc, CH:2 * CH], start=False, stop=last
                                 ).then_inc(s["down"], 1)

            def pe_tree(sweep, tree, slot, first=False, last=False):
                logits(sweep, tree, slot, 0)
                if not first:
                    down(sweep, tree - 1, (slot - 1) % SLOTS, 1, first=(isinstance(tree, int) and tree == 1))
                paths(sweep, tree, 0)
                logits(sweep, tree, slot, 1)
                down(sweep, tree, slot, 0, first=(isinstance(tree, int) and tree == 0), last=last)
                paths(sweep, tree, 1)

            def biases(slot, leaf, rows):
                o = slot % 2 * TCOLS + WOFF[4] + leaf
                return CT[0:rows, slot // 2, o:o + 1]

            def act_tree(sweep, tree, slot):
                for cc in range(2):
                    n = unit(sweep, tree, cc)
                    eng.wait_ge(s["log"], n + 1)
                    if sweep or not (isinstance(tree, int) and tree == 0):
                        eng.wait_ge(s["down"], n - 1)
                    nc.scalar.activation(Pb[0:INNER, cc, 0:CH], ps[0:INNER, 2 + cc, :], ACT.Silu,
                                         bias=biases(slot, 0, INNER))
                    nc.scalar.activation(Pb[:, cc, CH:2 * CH], ps[:, 4 + cc, :], ACT.Silu, bias=biases(slot, 1, 128)
                                         ).then_inc(s["acts"], 1)

            def dve_tree(sweep, tree, slot):
                for cc in range(2):
                    n = unit(sweep, tree, cc)
                    eng.wait_ge(s["acts"], n + 1)
                    nc.vector.tensor_scalar(DEC[0:INNER, cc, :], ps[0:INNER, 2 + cc, :], biases(slot, 0, INNER), 0.0,
                                            ALU.add, ALU.is_gt).then_inc(s["dec"], 1)
                    eng.wait_ge(s["path"], n + 1)
                    for k, rows, thr in ((0, INNER, "thr0"), (1, 128, "thr1")):
                        h = Pb[0:rows, cc, k * CH:(k + 1) * CH]
                        nc.vector.scalar_tensor_tensor(h, ps[0:rows, 6 + k, :], bias(thr, rows), h, ALU.is_ge,
                                                       ALU.mult).then_inc(s["msk"], 1)

            def sp_tree(sweep, tree, slot):
                if sweep or tree >= SLOTS:
                    eng.wait_ge(s["down"], unit(sweep, tree, 0) - 2 * SLOTS + 2)
                eng.dma_start(CT[:, slot // 2, slot % 2 * TCOLS:(slot % 2 + 1) * TCOLS], trees[tree]
                              ).then_inc(loads[slot], 16)

            if role == "sp":
                eng.wait_ge(ready[0], ready[1])
            if role == "pe":
                for c in range(NC):
                    eng.wait_ge(ready[0], ready[1] + c)
            for sweep in range(2):
                if role == "pe":
                    for tree in range(TREES):
                        pe_tree(sweep, tree, tree % SLOTS, first=(tree == 0), last=(tree == TREES - 1))
                    down(sweep, TREES - 1, (TREES - 1) % SLOTS, 1, last=True)
                if role == "act":
                    for tree in range(TREES):
                        act_tree(sweep, tree, tree % SLOTS)
                if role == "dve":
                    for tree in range(TREES):
                        dve_tree(sweep, tree, tree % SLOTS)
                    for cc in range(2):
                        eng.wait_ge(s["down"], unit(sweep, TREES - 1, cc) + 1)
                        nc.vector.tensor_copy(ck(X, 2 * sweep + cc), ps[:, cc, :]).then_inc(s["out"], 1)
                if role == "sp":
                    for tree in range(TREES):
                        sp_tree(sweep, tree, tree % SLOTS)
            return s["out"], 1

        def choice_stage(role, eng, ready):
            s = {k: sem(f"ch_{k}") for k in ("h", "relu", "i", "imp", "rows", "chain", "not")}
            if role == "pe":
                for c in range(NC):
                    eng.wait_ge(ready[0], ready[1] + c)
                    nc.tensor.matmul(ps[0:64, c, :], w("ws1"), ck(T, c), start=True, stop=True).then_inc(s["h"], 1)
                for c in range(NC):
                    eng.wait_ge(s["relu"], c + 1)
                    nc.tensor.matmul(ps[0:1, 4 + c, :], w("ws2", rows=64), A[0:64, c * CH:(c + 1) * CH],
                                     start=True, stop=True).then_inc(s["i"], 1)
            if role == "act":
                for c in range(NC):
                    eng.wait_ge(s["h"], c + 1)
                    nc.scalar.activation(A[0:64, c * CH:(c + 1) * CH], ps[0:64, c, :], ACT.Relu, bias=bias("bs1", 64)
                                         ).then_inc(s["relu"], 1)
                for c in range(NC):
                    eng.wait_ge(s["i"], c + 1)
                    nc.scalar.activation(Bt[0:1, c * CH:(c + 1) * CH], ps[0:1, 4 + c, :], ACT.Sigmoid, bias=bias("bs2", 1)
                                         ).then_inc(s["imp"], 1)
            IM = C[0:B, 0:S]
            TOP = [C[0:B, 64 + 8 * i:72 + 8 * i] for i in range(2)]
            LEFT = [C[0:B, 128 + S * i:128 + S * (i + 1)] for i in range(2)]
            if role == "sp":
                eng.wait_ge(s["imp"], NC)
                eng.dma_start(IM, Bt[0:1, :].rearrange("a (b q) -> a b q", b=B)).then_inc(s["rows"], 16)
                eng.wait_ge(s["not"], 2)
                for k, stacked in enumerate((KSA, QS)):
                    for g in range(4):
                        eng.dma_start(stacked[98:99, g, :].rearrange("a (b q) -> a b q", b=B), NSB[:, k, :]
                                      ).then_inc(sem("mask_rows"), 16)
            if role == "dve":
                eng.wait_ge(s["rows"], 16)
                cur = IM
                for i in range(SEL_K // 8):
                    nc.vector.max(TOP[i], cur).then_inc(s["chain"], 1)
                    eng.wait_ge(s["chain"], 2 * i + 1)
                    nc.vector.match_replace(LEFT[i], TOP[i], cur, -1.0).then_inc(s["chain"], 1)
                    eng.wait_ge(s["chain"], 2 * i + 2)
                    cur = LEFT[i]
                nc.vector.tensor_scalar(NSB[:, 0, :], cur, 0.0, None, ALU.is_ge).then_inc(s["not"], 1)
                nc.vector.tensor_scalar(NSB[:, 1, :], cur, 0.0, MASKED, ALU.is_ge, ALU.mult).then_inc(s["not"], 1)
            return ready

        def program(role, eng):
            loaded = sem("loaded")
            if role == "sp":
                eng.dma_start(W[:, :], wpack).then_inc(loaded, 16)
                eng.dma_start(WB[:, :], bpack).then_inc(loaded, 16)
                eng.dma_start(X[:, :], xT).then_inc(loaded, 16)
            if role == "dve":
                nc.vector.memset(epst[:, :], EPS).then_inc(sem("eps_set"), 1)
            if role == "pool":
                for keys in (KST, KSS):
                    nc.gpsimd.memset(keys[96:98, :, :, :].rearrange("p a g k -> p (a g k)"), 1.0
                                     ).then_inc(sem("ones_set"), 1)
                nc.gpsimd.memset(QS[96:98, :, :].rearrange("p g n -> p (g n)"), 0.0).then_inc(sem("ones_set"), 1)
            if role == "act":
                eng.wait_ge(sem("eps_set"), 1)
            eng.wait_ge(loaded, 48)

            s = layernorm(role, eng, 0, X, T, None)
            s = diagonal_attention(role, eng, s)
            s = layernorm(role, eng, 1, A, T, s, gain="g1", shift="b1")
            load_contexts(role, eng, XA0, (loaded, 48))
            q_lo = project_split(role, eng, 0, w("c_wq"), "bq0", s, HLQ)
            s = split_rows(role, eng, 0, q_lo, QS, "q")
            attention(role, eng, XA0, s, None, (q_lo[0], q_lo[1] + NC - 1))
            s = attention_out(role, eng, XA0, 0, "xa0_o", "xa0_den", "bo0", A, T)
            s = layernorm(role, eng, 2, A, T, s, gain="g2", shift="b2")
            s = dense_ff(role, eng, s)
            s = layernorm(role, eng, 3, A, T, s, gain="g3", shift="b3")
            s = add_to_stream(role, eng, s)
            if stop == 2:
                return X, s

            if role == "sp":
                for stacked, row in ((KSA, "krow"), (QS, "qrow")):
                    eng.dma_start(stacked[98:99, :, :].rearrange("a g (b q) -> a (g b) q", b=B),
                                  wb(row, rows=1).unsqueeze(1).broadcast_to([1, 4 * B, S])).then_inc(sem("mask_rows"), 16)
            s = layernorm(role, eng, 4, X, T, s)
            q_lo = rotary(role, eng, 0, "sa0_q", D, T, s, HLQ)
            s = split_rows(role, eng, 1, q_lo, QS, "q")
            lat_pe, lat = sem("lat_pe"), sem("lat_out")
            if role == "pe":
                for c in range(NC):
                    eng.wait_ge(q_lo[0], q_lo[1] + c)
                    nc.tensor.matmul(lo_bank(c)[0:64, :], w("down"), ck(T, c), start=True, stop=True).then_inc(lat_pe, 1)
            if role == "act":
                for c in range(NC):
                    eng.wait_ge(lat_pe, c + 1)
                    nc.scalar.activation(C[0:64, c * CH:(c + 1) * CH], lo_bank(c)[0:64, :], ACT.Copy).then_inc(lat, 1)
            k_lo = rotary(role, eng, 1, "sa0_k", 64, C, (lat, 1), HL)
            s = split_rows(role, eng, 2, k_lo, KSA, "k")
            attention(role, eng, SA0, s, C, (k_lo[0], k_lo[1] + NC - 1))
            s = attention_out(role, eng, SA0, 1, "sa0_o", "den16", None, X, X)
            if stop == 3:
                return X, s

            s = layernorm(role, eng, 5, X, T, s)
            s = moe_stage(role, eng, s)
            if role == "pe":
                eng.wait_ge(s[0], NC)
            if stop == 4:
                return X, s

            load_contexts(role, eng, XA1, (s[0], NC))
            s = layernorm(role, eng, 6, X, T, s)
            q_lo = project_split(role, eng, 1, w("xa1_q"), "bq1", s, HLQ)
            s = split_rows(role, eng, 3, q_lo, QS, "q")
            attention(role, eng, XA1, s, None, (q_lo[0], q_lo[1] + NC - 1))
            s = attention_out(role, eng, XA1, 2, "xa1_o", "den16", "bo1", X, X)
            if stop == 5:
                return X, s

            s = layernorm(role, eng, 7, X, T, s)
            s = choice_stage(role, eng, s)
            q_lo = project_split(role, eng, 2, w("sa1_q"), "s_bq", s, HLQ)
            s = split_rows(role, eng, 4, q_lo, QS, "q")
            if role == "pe":
                eng.wait_ge(q_lo[0], q_lo[1] + NC - 1)
            k_lo = project_split(role, eng, 3, w("sa1_k"), "s_bk", (sem("ln_out"), 7 * NC + 1), HL)
            s = split_rows(role, eng, 5, k_lo, KSA, "k")
            attention(role, eng, SA1, s, T, (k_lo[0], k_lo[1] + NC - 1))
            s = attention_out(role, eng, SA1, 3, "sa1_o", "den16", "s_bo", X, X)
            if stop == 6:
                return X, s

            s = layernorm(role, eng, 8, X, T, s)
            s = tree_stage(role, eng, s)
            return X, s

        block = ctx.enter_context(nc.Block())

        @block.tensor
        def _(eng):
            program("pe", eng)

        @block.vector
        def _(eng):
            program("dve", eng)

        @block.scalar
        def _(eng):
            program("act", eng)

        @block.gpsimd
        def _(eng):
            program("pool", eng)

        @block.sync
        def _(eng):
            res, s = program("sp", eng)
            stored = sem("stored")
            eng.wait_ge(s[0], s[1] + NC - 1)
            eng.dma_start(outT, res[:, :]).then_inc(stored, 16)
            eng.wait_ge(stored, 16)



def _values(att, wv, bv):
    wa = np.zeros((wv.shape[0], att.NV), wv.dtype)
    ba = np.zeros((128, att.NV), wv.dtype)
    for r, quad, h0, nh, v0, oc in att.groups:
        for i in range(nh):
            a, h = v0 + i * (att.d + 1), h0 + i
            wa[:, a:a + att.d] = wv[:, h * att.d:(h + 1) * att.d]
            if bv is not None:
                ba[:, a:a + att.d] = bv[h * att.d:(h + 1) * att.d][None, :]
            ba[:, a + att.d] = 1.0
    return wa, ba


def _outputs(att, wo):
    out = np.zeros((128, 2, D), wo.dtype)
    for r, quad, h0, nh, v0, oc in att.groups:
        for i in range(nh):
            a = 32 * quad + i * (att.d + 1)
            out[a:a + att.d, r] = wo[(h0 + i) * att.d:(h0 + i + 1) * att.d]
    return out.reshape(128, 2 * D)


def _denominators(att):
    pick = np.zeros((128, 2, 16), np.float32)
    spread = np.zeros((128, 2, D), np.float32)
    for r, quad, h0, nh, v0, oc in att.groups:
        for i in range(nh):
            a = 32 * quad + i * (att.d + 1)
            pick[a + att.d, r, h0 + i] = 1.0
            spread[h0 + i, r, a:a + att.d] = 1.0
    return np.concatenate([pick.reshape(128, 32), spread.reshape(128, 2 * D)], axis=1)


def _tree_paths():
    path = np.zeros((128, NODES + 1), np.float32)
    need = np.zeros(NODES, np.float32)
    for n in range(NODES):
        k = n
        while k > 0:
            parent, right = (k - 1) // 2, (k - 1) % 2
            path[parent, n] = 1.0 if right else -1.0
            need[n] += right
            k = parent
    return path, need - 0.5


def kernel(**inputs):
    import ml_dtypes
    import concourse.bacc as _bacc
    from concourse.bass_utils import run_bass_kernel_spmd as _run

    i = {k: np.asarray(v) for k, v in inputs.items()}
    z = np.float32
    xT = np.ascontiguousarray(i["x"].reshape(N, D).T)
    ctxT = np.ascontiguousarray(i["ctx_1024"].transpose(0, 2, 1))

    wp = np.zeros((128, W_COLS), z)

    def put(name, a):
        o, n = W_AT[name]
        a = np.asarray(a)
        assert a.shape[1] == n, (name, a.shape, n)
        wp[:a.shape[0], o:o + n] = a

    bs = np.zeros((128, 64), z)

    def put_bias(name, a):
        bs[:len(a), BIAS_AT[name]] = a

    put("mean", np.full((D, 1), 1.0 / D, z))
    put("centre", np.eye(D, dtype=z) - z(1.0 / D))
    put("ones", np.ones((D, D), z))
    put("ident", np.eye(D, dtype=z))
    qkv, qb = i["L0_xattn_qkv_w"], i["L0_xattn_qkv_b"]
    for k, n in enumerate("qkv"):
        put(f"c_{n}", qkv[k * D:(k + 1) * D].T)
        put_bias(f"c_b{n}", qb[k * D:(k + 1) * D])
    put("c_o", i["L0_xattn_sa_out_w"].T)
    put_bias("c_bo", i["L0_xattn_sa_out_b"])
    ip, ib = i["L0_xattn_in_proj_w"], i["L0_xattn_in_proj_b"]
    put("c_wq", ip[0:D].T)
    put_bias("bq0", ib[0:D])
    put("xa0_k", ip[D:2 * D].T)
    put_bias("bk0", ib[D:2 * D])
    wa, ba = _values(XA0, ip[2 * D:].T, ib[2 * D:])
    put("xa0_v", wa)
    put("xa0_vb", ba)
    put("xa0_o", _outputs(XA0, i["L0_xattn_mha_out_w"].T))
    put_bias("bo0", i["L0_xattn_mha_out_b"])
    put("xa0_den", _denominators(XA0))
    for k in (1, 2, 3):
        put_bias(f"g{k}", i[f"L0_xattn_ln{k}_g"])
        put_bias(f"b{k}", i[f"L0_xattn_ln{k}_b"])
    put("lin1", i["L0_xattn_lin1_w"].T)
    put("lin2", i["L0_xattn_lin2_w"].T.reshape(4, D, D).transpose(1, 0, 2).reshape(D, FF))
    for f in range(4):
        put_bias(f"l1b{f}", i["L0_xattn_lin1_b"][f * D:(f + 1) * D])
    put_bias("l2b", i["L0_xattn_lin2_b"])

    d = SA0.d
    inv = 1.0 / 10000.0 ** (np.arange(0, d, 2, dtype=z) / d)
    ang = np.outer(np.arange(S, dtype=z), inv)
    cos, sin = np.cos(ang).astype(z), np.sin(ang).astype(z)
    pair = (np.arange(D) % d) // 2
    sign = np.where(np.arange(D) % 2 == 0, -1.0, 1.0).astype(z)
    put("rope", np.concatenate([cos[:, pair].T, sin[:, pair].T * sign[:, None]], axis=1))
    swap = np.arange(D) ^ 1
    wq, wk = i["L0_attn_wq"], i["L0_attn_wk_up"]
    put("sa0_q", np.concatenate([wq, wq[:, swap]], axis=1))
    put("down", i["L0_attn_w_down"])
    put("sa0_k", np.concatenate([wk, wk[:, swap]], axis=1))
    wa, ba = _values(SA0, i["L0_attn_wv_up"], None)
    put("sa0_v", wa)
    put("sa0_vb", ba)
    put("sa0_o", _outputs(SA0, i["L0_attn_wo"]))
    put("den16", _denominators(SA0))
    ms = np.zeros((128, 8), z)
    for r, quad, h0, nh, v0, oc in SA0.groups:
        for k in range(nh):
            a = 32 * quad + k * (d + 1)
            ms[a:a + d + 1, 4 * r + k] = 1.0
    put("m_sel", ms)

    put("gate", i["L0_ffn_gate_weight"].T)
    put("gate_b", np.broadcast_to(i["L0_ffn_e_score_correction_bias"][None, :], (128, E)))
    put("shared", np.concatenate([i["L0_ffn_shared_gate_w"].T, i["L0_ffn_shared_up_w"].T,
                                  i["L0_ffn_shared_down_w"].T], axis=1))
    gu = i["L0_ffn_experts_gate_up"].reshape(E // 2, 2, 2, EI, D)
    gate_up = gu.transpose(0, 4, 2, 1, 3).reshape(E // 2, D, 2 * D)
    dn = i["L0_ffn_experts_down"].reshape(E // 2, 2, D, EI).transpose(0, 1, 3, 2).reshape(E // 2, D, D)
    experts = np.concatenate([gate_up, dn], axis=2)
    picks = np.zeros((E // 2, 2 * E, D), ml_dtypes.bfloat16)
    for p in range(E // 2):
        for k in range(2):
            picks[p, 2 * p + k, k * EI:(k + 1) * EI] = 1.0
            picks[p, E + 2 * p + k, k * EI:(k + 1) * EI] = 1.0

    put("xa1_q", i["L1_xattn_W_Q"])
    put_bias("bq1", i["L1_xattn_b_Q"])
    put("xa1_k", i["L1_xattn_W_K"])
    put_bias("bk1", i["L1_xattn_b_K"])
    wa, ba = _values(XA1, i["L1_xattn_W_V"], i["L1_xattn_b_V"])
    put("xa1_v", wa)
    put("xa1_vb", ba)
    put("xa1_o", _outputs(XA1, i["L1_xattn_W_O"]))
    put_bias("bo1", i["L1_xattn_b_O"])
    put("sa1_q", i["L1_attn_Wq"])
    put_bias("s_bq", i["L1_attn_bq"])
    put("sa1_k", i["L1_attn_Wk"])
    put_bias("s_bk", i["L1_attn_bk"])
    wa, ba = _values(SA1, i["L1_attn_Wv"], i["L1_attn_bv"])
    put("sa1_v", wa)
    put("sa1_vb", ba)
    put("sa1_o", _outputs(SA1, i["L1_attn_Wo"]))
    put_bias("s_bo", i["L1_attn_bo"])
    put("ws1", i["L1_attn_Ws1"])
    put_bias("bs1", i["L1_attn_bs1"])
    put("ws2", i["L1_attn_Ws2"])
    put_bias("bs2", i["L1_attn_bs2"])

    path, thr = _tree_paths()
    put_bias("thr0", thr[:INNER])
    put_bias("thr1", thr[INNER:])
    put("bias", bs)
    wi = i["L1_ffn_W_in"].reshape(TREES, NODES, D).transpose(0, 2, 1)
    wo = i["L1_ffn_W_out"].reshape(D, TREES, NODES).transpose(1, 2, 0)
    bi = i["L1_ffn_b_in"].reshape(TREES, NODES)
    trees = np.zeros((TREES, 128, NODES + 2 * D + 2), z)
    trees[:, :, 0:NODES] = wi
    trees[:, 0:INNER, NODES:NODES + D] = wo[:, 0:INNER]
    trees[:, :, NODES + D:NODES + 2 * D] = wo[:, INNER:]
    trees[:, 0:INNER, NODES + 2 * D] = bi[:, 0:INNER]
    trees[:, :, NODES + 2 * D + 1] = bi[:, INNER:]

    bp = np.zeros((128, B_COLS), ml_dtypes.bfloat16)

    def put16(name, a):
        o, n = B_AT[name]
        bp[:a.shape[0], o:o + n] = a
    put16("ident16", np.eye(D))
    put16("tree", path)
    rows = np.arange(RAW) % 32
    for hg, dd in ((2, 16), (4, 8)):
        heads = (rows[:, None] // dd == np.arange(hg)[None, :]).astype(z)
        put16(f"hm{hg}", np.concatenate([heads, np.ones((3, hg), z)]))
    page = (np.arange(S) // 32).astype(z)
    put16("krow", page[None, :])
    put16("qrow", ((1.0 - page) * MASKED)[None, :])

    nc = _bacc.Bacc("TRN2", target_bir_lowering=False, num_devices=1)
    arrays, args = {}, []
    for name, a in (("xT", xT), ("ctxT", ctxT), ("wpack", wp), ("bpack", bp), ("experts", experts), ("picks", picks),
                    ("trees", trees)):
        a = np.ascontiguousarray(a)
        arrays[name] = a
        args.append(nc.dram_tensor(name, a.shape, mybir.dt.from_np(a.dtype), kind="ExternalInput").ap())
    args.append(nc.dram_tensor("outT", (D, N), F32, kind="ExternalOutput").ap())
    bass_perceiver_kernel(nc, *args)
    r = _run(nc, [arrays], core_ids=[0])
    return np.ascontiguousarray(r.results[0]["outT"].T).reshape(B, S, D)
```

```python
from contextlib import ExitStack

import numpy as np

import concourse.bass as bass
from concourse import mybir

ALU = mybir.AluOpType
ACT = mybir.ActivationFunctionType
AX = mybir.AxisListType
F32 = mybir.dt.float32
BF16 = mybir.dt.bfloat16

B, S, D, NK = 32, 64, 128, 1601
N = B * S
CH = 512
NC = N // CH
EPS = 1e-5
MASKED = -1e30
E, EI, TOPK, NG, TOPG = 32, 64, 6, 8, 4
GS = E // NG
ROUTE_SCALE = 2.5
TREES, NODES, INNER, LEAVES = 8, 255, 127, 128
FF = 512
SEL_K = 16
RAW = 96
ROWS = 98
TILE = 128
KTILES = [(t * TILE, min(TILE, NK - t * TILE)) for t in range(-(-NK // TILE))]
BIG = 3e38
SLOTS = 4


class Attention:

    def __init__(self, name, heads, cross, masked=False, values_k=D):
        self.name, self.H, self.cross, self.masked, self.values_k = name, heads, cross, masked, values_k
        self.d = D // heads
        self.hg = heads // 4
        self.W = heads * S
        per = 32 // (self.d + 1)
        if heads == 16:
            sizes = [3, 3, 3, 3, 2, 2]
        else:
            sizes = [1] * 8
        assert max(sizes) <= per
        self.groups, h, v = [], 0, 0
        bases = {}
        col = 0
        for i, n in enumerate(sizes):
            r, quad = divmod(i, 4)
            if r not in bases:
                bases[r] = col
                col += n * S
            self.groups.append((r, quad, h, n, v, bases[r]))
            h += n
            v += n * (self.d + 1)
        self.rounds = len(bases)
        self.bases = bases
        self.NV, self.NO = v, col
        self.blocks = [sizes[0], sizes[4]]
        self.tiles = KTILES if cross else [(0, S)]
        self.keys = NK if cross else S
        per_exp = 1024 // self.W
        self.exps = [list(range(i, min(i + per_exp, len(self.tiles)))) for i in range(0, len(self.tiles), per_exp)]
        if cross and len(self.exps[-1]) > 1:
            raise ValueError("the short key tile has an Exp of its own")
        self.NE = len(self.exps)
        self.units = heads // 2
        q4 = -(-NK // 4)
        self.kchunks = [(c * q4, min(q4, NK - c * q4)) for c in range(4)] if cross else []
        self.vjobs = [list(range(i, min(i + 3, len(self.tiles)))) for i in range(0, len(self.tiles), 3)]
        if cross:
            self.mjobs = [[(u, c0, n)] for u in range(self.units) for c0, n in self.kchunks]
        else:
            self.mjobs = [[(u, 0, S) for u in range(self.units)]]
        self.rjobs = self.W // 512
        self.nk = len(self.kchunks)
        self.jobs = ([("K", j) for j in range(len(self.kchunks))] + [("V", j) for j in range(len(self.vjobs))]
                     + [("M", j) for j in range(len(self.mjobs))] + [("R", j) for j in range(self.rjobs)])
        self.krows = ROWS + 1 if masked else ROWS
        self.scale = 1.0 / float(np.sqrt(self.d))

    def merged(self, main, prep, keys):
        K, V, M, R = ([j for j in self.jobs if j[0] == k] for k in "KVMR")
        if not self.cross:
            return (([("S", 0), ("E", 0)] if main else []) + (M + [("Z", 0)] + V + R if prep else [])
                    + ([("P", 0), ("O", 0)] if main else []))
        n = self.NE
        parts = [[] for _ in range(n)]
        first, steps = FIRST, n - 1 - FIRST
        for i, v in enumerate(V):
            parts[i // 2 if self.H == 16 else i].append(v)
        for i, m in enumerate(M):
            parts[first + i * steps // len(M)].append(m)
        parts[n - 1].append(("Z", 0))
        out = [("S", 0)] if main else []
        for e in range(n):
            if main:
                out.append(("E", e))
                if e + 1 < n:
                    out.append(("S", e + 1))
            if prep:
                out += parts[e]
            if keys and e == n - KSTEP:
                out += K
            if main:
                out.append(("P", e))
        if main:
            out.append(("O", 0))
        if prep:
            out += R
        return out


FIRST, KSTEP = 2, 3
WORK = 3


def bank_plan(att):
    order = [s for s in att.merged(False, True, True) if s[0] in "KVMR"]
    count = [0] * WORK
    plan = {}
    for u in range(2):
        for j, job in enumerate(order):
            bank = (u * len(order) + j) % WORK
            plan[(u, job)] = (bank, count[bank], j)
            count[bank] += 1
    lead = [0] * WORK
    first = []
    for j in range(att.nk):
        bank = plan[(1, ("K", j))][0]
        first.append((bank, lead[bank]))
        lead[bank] += 1
    return plan, count, len(order), lead, first


XA0 = Attention("xa0", 8, True)
SA0 = Attention("sa0", 16, False, masked=True, values_k=64)
XA1 = Attention("xa1", 16, True)
SA1 = Attention("sa1", 16, False, masked=True)


W_PARTS = [("mean", 1), ("centre", D), ("ones", D), ("c_q", D), ("c_k", D), ("c_v", D), ("c_o", D), ("c_wq", D), ("bias", 64),
           ("m_sel", 8), ("quad", 4), ("ident", D), ("xa0_k", D),
           ("xa0_v", XA0.NV), ("xa0_vb", XA0.NV), ("xa0_o", 2 * D), ("xa0_den", 2 * D + 64),
           ("lin1", FF), ("lin2", FF), ("rope", 2 * S), ("sa0_q", 2 * D), ("down", 64), ("sa0_k", 2 * D),
           ("sa0_v", SA0.NV), ("sa0_vb", SA0.NV), ("sa0_o", 2 * D), ("den16", 2 * D + 64),
           ("gate", E), ("gate_b", E), ("shared", 3 * D),
           ("xa1_q", D), ("xa1_k", D), ("xa1_v", XA1.NV), ("xa1_vb", XA1.NV), ("xa1_o", 2 * D),
           ("sa1_q", D), ("sa1_k", D), ("sa1_v", SA1.NV), ("sa1_vb", SA1.NV), ("sa1_o", 2 * D),
           ("ws1", 64), ("ws2", 1)]
W_AT, _o = {}, 0
for _n, _w in W_PARTS:
    W_AT[_n] = (_o, _w)
    _o += _w
W_COLS = _o
W_EARLY = W_AT["xa0_v"][0]
B_PARTS = [("ident16", D), ("tree", INNER + LEAVES + 1), ("hm2", 2), ("hm4", 4), ("krow", S), ("qrow", S)]
B_AT, _o = {}, 0
for _n, _w in B_PARTS:
    B_AT[_n] = (_o, _w)
    _o += _w
B_COLS = _o
BIASES = ["c_bq", "c_bk", "c_bv", "c_bo", "g1", "b1", "bq0", "bk0", "bo0", "g2", "b2", "l1b0", "l1b1", "l1b2", "l1b3",
          "l2b", "g3", "b3", "bq1", "bk1", "bo1", "s_bq", "s_bk", "s_bo", "bs1", "bs2", "thr0", "thr1"]
BIAS_AT = {n: i for i, n in enumerate(BIASES)}
assert len(BIASES) <= 64


def bass_perceiver_kernel(nc, xT, ctxT, wpack, bpack, experts, picks, trees, outT):
    ctx = ExitStack()
    with ctx:
        def sb(name, shape, dt):
            return ctx.enter_context(nc.sbuf_tensor(name, shape, dt))

        sems = {}

        def sem(name):
            if name not in sems:
                sems[name] = ctx.enter_context(nc.semaphore(name))
            return sems[name]

        ps = ctx.enter_context(nc.psum_tensor("ps", [128, 8, 512], F32))

        W = sb("W", [128, W_COLS], F32)
        WB = sb("WB", [128, B_COLS], BF16)
        X = sb("X", [128, N], F32)
        T = sb("T", [128, N], F32)
        ABO = sb("ABO", [128, 10240], F32)
        A = ABO[:, 0:N]
        Bt = ABO[:, N:2 * N]
        C = sb("C", [128, N], F32)
        QS = sb("QS", [128, 4, N], BF16)
        HL = sb("HL", [128, 2, N], BF16)
        HLQ = ABO[:, 2 * N:3 * N].bitcast(BF16).rearrange("p (a n) -> p a n", a=2)
        CT = sb("CT", [128, 2, NK], F32)
        KST = sb("KST", [128, 2, 4, NK], BF16)
        KSA = KST[:, :, :, :].rearrange("p a g k -> p (a g k)")[:, 0:4 * N].rearrange("p (g n) -> p g n", g=4)
        KSS = sb("KSS", [128, 2, 4, S], BF16)
        V = sb("V", [128, 2, len(KTILES), 144], F32)
        QW = sb("QW", [128, 2, 16 * S], BF16)
        QSL = sb("QSL", [128, 2, 4, S], BF16)
        Pb = sb("Pb", [128, 2, 1024], F32)
        OE = sb("OE", [128, 2, 320], F32)
        MX = sb("MX", [128, 2, 32], F32)
        MG = sb("MG", [128, 2, 8], F32)
        MH = sb("MH", [128, 2, 8, 2], BF16)
        epst = sb("epst", [128, 1], F32)
        WARM = sb("WARM", [128, 1], F32)
        DEV = sb("DEV", [128, 16], F32)
        COL = sb("COL", [128, 16], F32)
        DEC = sb("DEC", [128, 2, CH], BF16)
        NSB = sb("NSB", [B, 2, S], BF16)

        def w(name, a=0, b=None, rows=128):
            o, n = W_AT[name]
            return W[0:rows, o + a:o + (n if b is None else b)]

        def wb(name, rows=128):
            o, n = B_AT[name]
            return WB[0:rows, o:o + n]

        def bias(name, rows=128):
            o = W_AT["bias"][0] + BIAS_AT[name]
            return W[0:rows, o:o + 1]

        def ck(t, c):
            return t[:, c * CH:(c + 1) * CH]

        def hi_bank(c):
            return ps[:, 4 + c, :]

        def lo_bank(c):
            return ps[:, c, :]


        def spread(role, eng, call, c, ready):
            diag_s, spread_s = sem("diag"), sem("spread")
            n = NC * call + c
            if role == "dve":
                eng.wait_ge(*ready)
                nc.vector.tensor_tensor(ck(C, c).rearrange("p (t q) -> p t q", t=4),
                                        w("ident").unsqueeze(1).broadcast_to([128, 4, 128]),
                                        COL[:, 4 * c:4 * c + 4].unsqueeze(2).broadcast_to([128, 4, 128]), ALU.mult
                                        ).then_inc(diag_s, 1)
            if role == "pe":
                eng.wait_ge(diag_s, n + 1)
                nc.tensor.matmul(hi_bank(c), w("ones"), ck(C, c), start=True, stop=True).then_inc(spread_s, 1)
            return spread_s, NC * call + 1

        def layernorm(role, eng, call, src, dst, ready, gain=None, shift=None):
            mean_s, xc_s, sq_s, var_s, sd_s, rc_s, scaled_s, out_s = (
                sem(f"ln_{k}") for k in ("mean", "centred", "square", "var", "dev", "recip", "scaled", "out"))
            n = call * NC
            rows = call + (call > 0)
            if role == "pe":
                for c in range(NC):
                    if ready is not None:
                        eng.wait_ge(ready[0], ready[1] + c)
                    nc.tensor.matmul(lo_bank(c), w("centre"), ck(src, c), start=True, stop=True).then_inc(mean_s, 1)
                for c in range(NC):
                    eng.wait_ge(sq_s, n + c + 1)
                    for i in range(4):
                        t = 4 * c + i
                        mm = nc.tensor.matmul(hi_bank(c // 2 * 2)[:, t % 8:t % 8 + 1], C[:, t * 128:(t + 1) * 128],
                                              w("mean", 0, 1), start=True, stop=True)
                    if c % 2:
                        mm.then_inc(var_s, 1)
            if role == "dve":
                for c in range(NC):
                    eng.wait_ge(mean_s, n + c + 1)
                    nc.vector.tensor_copy(ck(dst, c), lo_bank(c)).then_inc(xc_s, 1)
            if role == "act":
                nc.scalar.activation(WARM[:, :], epst[:, :], ACT.Sqrt)
                for c in range(NC):
                    eng.wait_ge(xc_s, n + c + 1)
                    nc.scalar.activation(ck(C, c), ck(dst, c), ACT.Square).then_inc(sq_s, 1)
            for h in range(2):
                if role == "act":
                    eng.wait_ge(var_s, 2 * call + h + 1)
                    nc.scalar.activation(DEV[:, 8 * h:8 * h + 8], hi_bank(2 * h)[:, 0:8], ACT.Sqrt, bias=epst[:, 0:1]
                                         ).then_inc(sd_s, 1)
                if role == "dve":
                    eng.wait_ge(sd_s, 2 * call + h + 1)
                    nc.vector.reciprocal(COL[:, 8 * h:8 * h + 8], DEV[:, 8 * h:8 * h + 8]).then_inc(rc_s, 1)
            for c in range(NC):
                spread_s, first = spread(role, eng, rows, c, (rc_s, 2 * call + c // 2 + 1))
            for c in range(NC):
                if role == "dve":
                    eng.wait_ge(xc_s, n + c + 1)
                    eng.wait_ge(spread_s, first + c)
                    if gain is None:
                        nc.vector.tensor_tensor(ck(dst, c), ck(dst, c), hi_bank(c), ALU.mult).then_inc(out_s, 1)
                    else:
                        nc.vector.scalar_tensor_tensor(ck(dst, c), ck(dst, c), bias(gain), hi_bank(c),
                                                       ALU.mult, ALU.mult).then_inc(scaled_s, 1)
                if role == "act" and gain is not None:
                    eng.wait_ge(scaled_s, n - NC + c + 1)
                    nc.scalar.activation(ck(dst, c), ck(dst, c), ACT.Identity, bias=bias(shift)).then_inc(out_s, 1)
            return out_s, n + 1

        def split_rows(role, eng, call, done, stacked, kind):
            stacked_s = sem("stacked")
            if role == "sp":
                eng.wait_ge(done[0], done[1] + NC - 1)
                order, parts = ((0, 0, 1), HLQ) if kind == "q" else ((0, 1, 0), HL)
                for g in range(4):
                    for p, part in enumerate(order):
                        eng.dma_start(stacked[32 * p:32 * p + 32, g, :],
                                      parts[32 * g:32 * g + 32, part, :]).then_inc(stacked_s, 16)
            return stacked_s, (call + 1) * 12 * 16

        def project_split(role, eng, call, weights, bname, ready, parts):
            pe_s, hi_s, lo_s = sem("proj_sum"), sem("proj_hi"), sem("proj_lo")
            n = call * NC
            for c in range(NC):
                if role == "pe":
                    eng.wait_ge(ready[0], ready[1] + c)
                    nc.tensor.matmul(lo_bank(c), weights, ck(T, c), start=True, stop=True).then_inc(pe_s, 1)
                if role == "act":
                    eng.wait_ge(pe_s, n + c + 1)
                    nc.scalar.activation(ck(parts[:, 0, :], c), lo_bank(c), ACT.Identity,
                                         bias=bias(bname)).then_inc(hi_s, 1)
                if role == "dve":
                    eng.wait_ge(hi_s, n + c + 1)
                    nc.vector.scalar_tensor_tensor(ck(parts[:, 1, :], c), lo_bank(c), bias(bname), ck(parts[:, 0, :], c),
                                                   ALU.add, ALU.subtract).then_inc(lo_s, 1)
            return lo_s, n + 1


        def load_context(role, eng, att, item):
            if role == "sp":
                eng.dma_start(CT[:, item, :], ctxT[item]).then_inc(sem(f"cross_ctx{item}"), 16)

        def attention(role, eng, att, part, inputs_ready, src=None, banks_ready=None):
            plan, per_pair, n_jobs, lead, first_keys = bank_plan(att)
            t = att.name
            kind = "cross" if att.cross else "self"
            W_, hg = att.W, att.hg
            Oall = (ABO[:, 6144:6144 + B * att.NO] if att.H == 8 else ABO[:, 0:B * att.NO]).rearrange(
                "p (b o) -> p b o", b=B)
            kst = KST if att.cross else KSS
            s_ctx = [sem(f"{kind}_ctx{i}") for i in range(2)]
            s_q = [sem(f"{kind}_q{i}") for i in range(2)]
            s_kst = [sem(f"{kind}_kst{i}") for i in range(2)]
            s_oout = [sem(f"{kind}_oout{i}") for i in range(2)]
            filled = sem(f"{kind}_filled")
            free = [sem(f"{kind}_free{i}") for i in range(WORK)]
            khi, mx, negm = sem(f"{kind}_khi"), sem(f"{kind}_mx"), sem(f"{kind}_negm")
            qbuilt, scores, exps, pv, oev = (sem(f"{kind}_{k}") for k in ("qbuilt", "scores", "exps", "pv", "oev"))
            ready = sem(f"{kind}_ready")
            kst_dmas = 12 if att.cross else 1
            rows = att.krows if att.masked else RAW

            counted = {}
            if att is SA1 or att is XA1:
                prev = XA0 if att.cross else SA0
                _, prev_pair, prev_jobs, _, _ = bank_plan(prev)
                for name, n in (("filled", prev_jobs), ("khi", prev.nk), ("mx", 2 if prev.cross else 1), ("negm", 1),
                                ("qbuilt", 1), ("scores", prev.NE), ("exps", prev.NE), ("pv", prev.NE), ("oev", 1)):
                    counted[f"{kind}_{name}"] = B * n
                for name, n in (("ctx", 1), ("q", 1), ("kst", kst_dmas), ("oout", 1)):
                    for i in range(2):
                        counted[f"{kind}_{name}{i}"] = B // 2 * 16 * n
                for i in range(WORK):
                    counted[f"{kind}_free{i}"] = B // 2 * prev_pair[i]
                counted[f"{kind}_ready"] = 1

            def base(s):
                return counted.get(s.name, 0)

            def settled(eng, role):
                eng.sem_inc(sem(f"{role}_settled"), 1)

            def half(b):
                if isinstance(b, int):
                    return b % 2, b // 2
                i, k = b
                return k % 2, i + k // 2

            def val(b):
                return b if isinstance(b, int) else b[0] * 2 + b[1]

            def cycle(b, job):
                if job[0] != "K":
                    return b
                return b - 1 if isinstance(b, int) else (b[0], b[1] - 1)

            def at_lead(b, job):
                return job[0] == "K" and isinstance(b, int) and b == 0

            def after_last_keys(b, job):
                return (att.cross and job[0] != "K" and isinstance(b, int) and b == B - 1
                        and plan[(0, job)][2] > plan[(0, ("K", 0))][2])

            def bank_of(b, job):
                if at_lead(b, job):
                    return first_keys[job[1]][0]
                return plan[(half(cycle(b, job))[0], job)][0]

            def filled_at(b, job):
                if at_lead(b, job):
                    return job[1] + 1
                c = cycle(b, job)
                keys = att.nk if after_last_keys(b, job) else 0
                return att.nk + val(c) * n_jobs + plan[(half(c)[0], job)][2] + 1 - keys

            def held_before(b, job):
                if at_lead(b, job):
                    return first_keys[job[1]][1]
                u, pair = half(cycle(b, job))
                bank, before, _ = plan[(u, job)]
                if after_last_keys(b, job):
                    before -= sum(plan[(u, ("K", j))][0] == bank for j in range(att.nk))
                return lead[bank] + pair * per_pair[bank] + before

            def freed_at(b, job):
                return held_before(b, job) + 1

            def is_first(b, n=1):
                return isinstance(b, int) and b < n

            def pe_step(main, prep, step):
                k, j = step
                if k == "S":
                    b = main
                    u, _ = half(b)
                    slot = (u * att.NE + j) % 2
                    if j == 0:
                        for r in range(att.rjobs):
                            eng.wait_ge(free[bank_of(b, ("R", r))], base(free[bank_of(b, ("R", r))]) + freed_at(b, ("R", r)))
                    if not (is_first(b) and j < 2):
                        eng.wait_ge(exps, base(exps) + val(b) * att.NE + j - 1)
                    for ti, tile in enumerate(att.exps[j]):
                        k0, n = att.tiles[tile]
                        for g in range(4):
                            col = ti * W_ + g * hg * S
                            mm = nc.tensor.matmul(
                                ps[0:n, 2 * slot + col // 512, col % 512:col % 512 + hg * S],
                                kst[0:att.krows, u, g, k0:k0 + n],
                                QW[0:att.krows, u, g * hg * S:(g + 1) * hg * S], start=True, stop=True)
                    mm.then_inc(scores, 1)
                if k == "P":
                    b = main
                    u, _ = half(b)
                    slot = (u * att.NE + j) % 2
                    if j == 0:
                        last_v = ("V", len(att.vjobs) - 1)
                        for v in range(max(0, last_v[1] - WORK + 1), last_v[1] + 1):
                            eng.wait_ge(free[bank_of(b, ("V", v))], base(free[bank_of(b, ("V", v))]) + freed_at(b, ("V", v)))
                        if not is_first(b):
                            eng.wait_ge(oev, base(oev) + val(b))
                        else:
                            eng.wait_ge(ready, base(ready) + 1)
                    eng.wait_ge(exps, base(exps) + val(b) * att.NE + j + 1)
                    if not att.cross:
                        settled(eng, role)
                    for ti, tile in enumerate(att.exps[j]):
                        _, n = att.tiles[tile]
                        for r, quad, h0, nh, v0, oc in att.groups:
                            m = nh * (att.d + 1)
                            mm = nc.tensor.matmul(
                                ps[32 * quad:32 * quad + m, 4, oc:oc + nh * S], V[0:n, u, tile, v0:v0 + m],
                                Pb[0:n, slot, ti * W_ + h0 * S:ti * W_ + (h0 + nh) * S],
                                start=(tile == 0 and r == 0), stop=(tile == len(att.tiles) - 1),
                                skip_group_check=True, tile_position=(0, 32 * quad))
                    mm.then_inc(pv, 1)
                if k in ("K", "V", "M", "R"):
                    b = prep
                    u, pair = half(b)
                    bank = bank_of(b, step)
                    before = held_before(b, step)
                    if not (isinstance(before, int) and before == 0):
                        eng.wait_ge(free[bank], base(free[bank]) + before)
                    pb = ps[:, 5 + bank, :]
                if k == "K":
                    if j == 0:
                        eng.wait_ge(s_ctx[u], base(s_ctx[u]) + pair * 16 + 16)
                    c0, n = att.kchunks[j]
                    nc.tensor.matmul(pb[:, 0:n], w(f"{t}_k"), CT[:, u, c0:c0 + n],
                                     start=True, stop=True).then_inc(filled, 1)
                if k == "V":
                    if j == 0 and not att.cross:
                        eng.wait_ge(s_ctx[u], base(s_ctx[u]) + pair * 16 + 16)
                    if not att.cross:
                        settled(eng, role)
                    kk = att.values_k
                    for i, tile in enumerate(att.vjobs[j]):
                        k0, n = att.tiles[tile]
                        mm = nc.tensor.matmul(pb[0:n, i * att.NV:(i + 1) * att.NV], CT[0:kk, u, k0:k0 + n],
                                              w(f"{t}_v", rows=kk), start=True, stop=True)
                    mm.then_inc(filled, 1)
                if k == "M":
                    if j == 0:
                        eng.wait_ge(qbuilt, base(qbuilt) + val(b) + 1)
                        eng.wait_ge(s_kst[u], base(s_kst[u]) + (pair + 1) * 16 * kst_dmas)
                    for i, (unit, c0, n) in enumerate(att.mjobs[j]):
                        mm = nc.tensor.matmul(pb[:, i * S:i * S + n], QW[0:rows, u, unit * 128:(unit + 1) * 128],
                                              kst[0:rows, u, 2 * unit // hg, c0:c0 + n], start=True, stop=True)
                    mm.then_inc(filled, 1)
                if k == "R":
                    if j == 0:
                        eng.wait_ge(negm, base(negm) + val(b) + 1)
                    for i in range(4):
                        mm = nc.tensor.matmul(ps[96:98, 5 + bank, i * 128:(i + 1) * 128], MH[:, u, j * 4 + i, :],
                                              wb("ident16"), start=True, stop=True, tile_position=(0, 96))
                    mm.then_inc(filled, 1)

            def act_step(main, prep, step):
                k, j = step
                if k == "E":
                    b = main
                    u, _ = half(b)
                    slot = (u * att.NE + j) % 2
                    n = att.tiles[att.exps[j][0]][1]
                    cols = len(att.exps[j]) * W_
                    if not (is_first(b, 2) and (b if isinstance(b, int) else 9) * att.NE + j < 2):
                        eng.wait_ge(pv, base(pv) + val(b) * att.NE + j - 1)
                    eng.wait_ge(scores, base(scores) + val(b) * att.NE + j + 1)
                    src_ps = ps[0:n, 2 * slot:2 * slot + 2, :].rearrange("p a c -> p (a c)")[:, 0:cols]
                    nc.scalar.activation(Pb[0:n, slot, 0:cols], src_ps, ACT.Exp, scale=att.scale).then_inc(exps, 1)
                if k == "O":
                    b = main
                    u, pair = half(b)
                    eng.wait_ge(pv, base(pv) + (val(b) + 1) * att.NE)
                    if not is_first(b, 2):
                        eng.wait_ge(s_oout[u], base(s_oout[u]) + pair * 16)
                    nc.scalar.activation(OE[:, u, 0:att.NO], ps[:, 4, 0:att.NO], ACT.Copy).then_inc(oev, 1)
                if k == "K":
                    b = prep
                    if j == 0 and not is_first(b):
                        up, pp = half(b - 1 if isinstance(b, int) else (b[0], b[1] - 1))
                        eng.wait_ge(s_kst[up], base(s_kst[up]) + (pp + 1) * 16 * kst_dmas)
                    c0, n = att.kchunks[j]
                    eng.wait_ge(filled, base(filled) + filled_at(b, step))
                    nc.scalar.activation(HL[:, 0, c0:c0 + n], ps[:, 5 + bank_of(b, step), 0:n], ACT.Identity,
                                         bias=bias(f"bk{t[-1]}")).then_inc(khi, 1)
                if k == "R" and j == 0:
                    b = prep
                    u, _ = half(b)
                    eng.wait_ge(filled, base(filled) + filled_at(b, step))
                    nc.scalar.activation(QW[96:98, u, j * 512:(j + 1) * 512], ps[96:98, 5 + bank_of(b, step), :],
                                         ACT.Copy).then_inc(free[bank_of(b, step)], 1)

            def dve_step(main, prep, step):
                k, j = step
                b = prep
                if k in ("K", "V", "M"):
                    u, pair = half(b)
                    bank = bank_of(b, step)
                    pb = ps[:, 5 + bank, :]
                if k == "K":
                    c0, n = att.kchunks[j]
                    eng.wait_ge(khi, base(khi) + val(b) * len(att.kchunks) + j + 1)
                    nc.vector.scalar_tensor_tensor(HL[:, 1, c0:c0 + n], pb[:, 0:n], bias(f"bk{t[-1]}"),
                                                   HL[:, 0, c0:c0 + n], ALU.add, ALU.subtract).then_inc(free[bank], 1)
                if k == "V":
                    eng.wait_ge(filled, base(filled) + filled_at(b, step))
                    if j == 0 and not is_first(b, 2):
                        eng.wait_ge(pv, base(pv) + (val(b) - 1) * att.NE)
                    ts = att.vjobs[j]
                    n = att.tiles[ts[0]][1]
                    nc.vector.tensor_tensor(
                        V[0:n, u, ts[0]:ts[0] + len(ts), 0:att.NV],
                        pb[0:n, 0:len(ts) * att.NV].rearrange("p (t v) -> p t v", t=len(ts)),
                        w(f"{t}_vb")[0:n, :].unsqueeze(1).broadcast_to([n, len(ts), att.NV]),
                        ALU.add).then_inc(free[bank], 1)
                if k == "M":
                    eng.wait_ge(filled, base(filled) + filled_at(b, step))
                    m = len(att.mjobs[j])
                    if j == 0 and not is_first(b, 2):
                        eng.wait_ge(negm, base(negm) + val(b) - 1)
                    src_ps = pb[:, 0:att.mjobs[j][0][2]] if m == 1 else pb[:, 0:m * S].rearrange("p (a c) -> p a c", a=m)
                    nc.vector.reduce_max(MX[:, u, j * m:(j + 1) * m], src_ps, AX.X).then_inc(free[bank], 1)
                if k == "R" and j == 1:
                    u, _ = half(b)
                    eng.wait_ge(filled, base(filled) + filled_at(b, step))
                    nc.vector.tensor_copy(QW[96:98, u, j * 512:(j + 1) * 512], ps[96:98, 5 + bank_of(b, step), :]
                                          ).then_inc(free[bank_of(b, step)], 1)
                if k == "Z":
                    u, pair = half(b)
                    for m in range(max(0, len(att.mjobs) - WORK), len(att.mjobs)):
                        eng.wait_ge(free[bank_of(b, ("M", m))], base(free[bank_of(b, ("M", m))]) + freed_at(b, ("M", m)))
                    top = MX[:, u, 0:att.units]
                    if att.cross:
                        top = MG[:, u, 0:att.units]
                        nc.vector.reduce_max(top, MX[:, u, 0:att.units * 4].rearrange("p (a c) -> p a c", c=4),
                                             AX.X).then_inc(mx, 1)
                        eng.wait_ge(mx, base(mx) + val(b) * 2 + 1)
                    if not is_first(b, 2):
                        for r in range(att.rjobs):
                            bb = b - 2 if isinstance(b, int) else (b[0] - 1, b[1])
                            eng.wait_ge(free[bank_of(b, ("R", r))], base(free[bank_of(b, ("R", r))]) + freed_at(bb, ("R", r)))
                    nc.vector.tensor_scalar(MH[:, u, 0:att.units, 0], top, -1.0, None, ALU.mult).then_inc(mx, 1)
                    eng.wait_ge(mx, base(mx) + ((val(b) + 1) * (2 if att.cross else 1)))
                    nc.vector.scalar_tensor_tensor(MH[:, u, 0:att.units, 1], top, -1.0, MH[:, u, 0:att.units, 0],
                                                   ALU.mult, ALU.subtract).then_inc(negm, 1)

            def pool_item(b):
                u, pair = half(b)
                eng.wait_ge(s_q[u], base(s_q[u]) + (pair + 1) * 16)
                if not is_first(b, 2):
                    eng.wait_ge(scores, base(scores) + (val(b) - 1) * att.NE)
                settled(eng, role)
                hm = wb("hm2" if hg == 2 else "hm4", rows=rows)
                out = QW[0:rows, u, 0:W_].rearrange("p (g h q) -> p g h q", g=4, h=hg)
                q4 = QSL[0:rows, u, :, :].unsqueeze(2).broadcast_to([rows, 4, hg, S])
                m4 = hm.unsqueeze(1).unsqueeze(3).broadcast_to([rows, 4, hg, S])
                nc.gpsimd.tensor_tensor(out, q4, m4, ALU.mult).then_inc(qbuilt, 1)

            def sp_context(b):
                u, pair = half(b)
                if not is_first(b, 2):
                    bb = b - 2 if isinstance(b, int) else (b[0] - 1, b[1])
                    last_v = ("V", len(att.vjobs) - 1)
                    eng.wait_ge(filled, base(filled) + filled_at(bb, last_v))
                    settled(eng, role)
                if not att.cross:
                    kk = att.values_k
                    eng.dma_start(CT[0:kk, u, 0:S], src[0:kk, bass.ds(val(b) * S, S)]).then_inc(s_ctx[u], 16)
                elif not is_first(b, 2):
                    eng.dma_start(CT[:, u, :], ctxT[val(b)]).then_inc(s_ctx[u], 16)

            def sp_queries(b):
                u, pair = half(b)
                if not is_first(b, 2):
                    eng.wait_ge(qbuilt, base(qbuilt) + val(b) - 1)
                    settled(eng, role)
                eng.dma_start(QSL[0:rows, u, :, :], QS[0:rows, :, bass.ds(val(b) * S, S)]).then_inc(s_q[u], 16)

            def sp_keys(b):
                u, pair = half(b)
                if not att.cross:
                    if not is_first(b, 2):
                        eng.wait_ge(scores, base(scores) + (val(b) - 1) * att.NE)
                        settled(eng, role)
                    eng.dma_start(KSS[0:rows, u, :, :], KSA[0:rows, :, bass.ds(val(b) * S, S)]).then_inc(s_kst[u], 16)

            def sp_stack(b):
                u, pair = half(b)
                if not is_first(b, 2):
                    eng.wait_ge(scores, base(scores) + (val(b) - 1) * att.NE)
                    settled(eng, role)
                for j in range(max(0, 4 - WORK), 4):
                    eng.wait_ge(free[bank_of(b, ("K", j))], base(free[bank_of(b, ("K", j))]) + freed_at(b, ("K", j)))
                    settled(eng, role)
                for p, part in enumerate((0, 1, 0)):
                    for g in range(4):
                        ins = eng.dma_start(KST[32 * p:32 * p + 32, u, g, :], HL[32 * g:32 * g + 32, part, 0:NK])
                        ins.then_inc(s_kst[u], 16)

            def sp_out(b):
                u, pair = half(b)
                eng.wait_ge(oev, base(oev) + val(b) + 1)
                settled(eng, role)
                eng.dma_start(Oall[:, val(b), :] if isinstance(b, int) else Oall[:, bass.ds(val(b), 1), :],
                              OE[:, u, 0:att.NO] if isinstance(b, int) else OE[:, u, 0:att.NO].unsqueeze(1)
                              ).then_inc(s_oout[u], 16)

            step_of = {"pe": pe_step, "act": act_step, "dve": dve_step}
            if part == "first" and att.cross:
                if role in step_of:
                    for j in range(att.nk):
                        step_of[role](None, 0, ("K", j))
                if role == "sp":
                    sp_stack(0)
                return None
            if part == "first":
                if role == "sp":
                    eng.wait_ge(*inputs_ready)
                    eng.wait_ge(sem("mask_rows"), 16 * (2 if att is SA0 else 2 + 8))
                    for b in range(2):
                        sp_context(b)
                        sp_queries(b)
                if role == "pool":
                    pool_item(0)
                    pool_item(1)
                return None

            if role == "dve":
                eng.wait_ge(*banks_ready)
                nc.vector.memset(ps[:, 4, :], 0.0).then_inc(ready, 1)
            if role == "pe" and att is not SA1:
                eng.wait_ge(sem("ones_set"), 3)
            if role == "sp" or (role == "pool" and att.cross):
                eng.wait_ge(*inputs_ready)
            if role in step_of:
                f = step_of[role]

                def item(main, prep, keys):
                    for step in att.merged(main is not None, prep is not None, keys is not None):
                        f(main, keys if step[0] == "K" else prep, step)
                item(None, 0, 1)
                item(0, 1, 2)
                item(1, 2, 3)
                with eng.Fori(1, B // 2 - 1) as i:
                    item((i, 0), (i, 1), (i, 2))
                    item((i, 1), (i, 2), (i, 3))
                item(B - 2, B - 1, None)
                item(B - 1, None, None)
            if role == "pool":
                if att.cross:
                    pool_item(0)
                    pool_item(1)
                with eng.Fori(1, B // 2) as i:
                    pool_item((i, 0))
                    pool_item((i, 1))
            if role == "sp":
                def sp_item(main, ahead):
                    if ahead is not None:
                        sp_context(ahead)
                        sp_queries(ahead)
                        if not is_first(ahead):
                            sp_stack(ahead)
                    if main is not None:
                        sp_out(main)
                def sp_self(main, ahead):
                    if ahead is not None:
                        sp_context(ahead)
                        sp_queries(ahead)
                    if main is not None:
                        sp_out(main)
                    if ahead is not None:
                        sp_keys(ahead)
                if att.cross:
                    sp_item(None, 0)
                    sp_item(None, 1)
                    sp_item(0, 2)
                    sp_item(1, 3)
                    with eng.Fori(1, B // 2 - 1) as i:
                        sp_item((i, 0), (i, 2))
                        sp_item((i, 1), (i, 3))
                    sp_item(B - 2, None)
                    sp_item(B - 1, None)
                else:
                    sp_keys(0)
                    sp_keys(1)
                    sp_self(None, 2)
                    sp_self(0, 3)
                    sp_self(1, 4)
                    with eng.Fori(1, B // 2 - 2) as i:
                        sp_self((i, 0), (i, 3))
                        sp_self((i, 1), (i, 4))
                    sp_self(B - 4, B - 1)
                    sp_self(B - 3, None)
                    sp_self(B - 2, None)
                    sp_self(B - 1, None)
            return s_oout

        def attention_out(role, eng, att, call, wname, den, bname, dst, residual):
            t = att.name
            Oall = (ABO[:, 6144:6144 + B * att.NO] if att.H == 8 else ABO[:, 0:B * att.NO]).rearrange(
                "p (b o) -> p b o", b=B)
            s_oout = [sem(f"{'cross' if att.cross else 'self'}_oout{i}") for i in range(2)]
            scaled_s, sel_s, den_s, rec_s, own_s, spread_s, on_s, pe_s, out_s = (
                sem(f"ao_{k}") for k in ("scaled", "sel", "den", "rec", "own", "spread", "on", "pe", "out"))
            nb = CH // S
            n = call * NC
            more = sum(att.blocks) - 2
            sel_before = NC * sum(sum(a.blocks) - 2 for a in (XA0, SA0, XA1)[:call])
            ms, quad = W_AT["m_sel"][0], W_AT["quad"][0]
            flat = CT[:, :, :].rearrange("p a n -> p (a n)")
            REC = flat[:, 0:CH]

            def own(c):
                return flat[:, (c + 1) * CH:(c + 2) * CH]

            def sel(r, c):
                return ck(C, c) if r == 0 else Pb[:, c // 2, c % 2 * CH:(c % 2 + 1) * CH]

            def bank(r, c):
                return lo_bank(c) if r == 0 else hi_bank(c)

            def block(r, h, c):
                return Oall[:, nb * c:nb * (c + 1), att.bases[r] + h * S:att.bases[r] + (h + 1) * S]

            def by_item(x):
                return x.rearrange("p (b q) -> p b q", b=nb)

            for c in range(NC):
                if role == "act":
                    if c == 0:
                        for s in s_oout:
                            eng.wait_ge(s, 16 * B // 2 * (2 if att is SA1 or att is XA1 else 1))
                    for r in range(2):
                        nc.scalar.activation(by_item(sel(r, c)), block(r, 0, c), ACT.Copy,
                                             scale=1.0 if att.H == 8 else W[:, ms + 4 * r:ms + 4 * r + 1]
                                             ).then_inc(scaled_s, 1)
                if role == "dve":
                    done = 0
                    for r in range(2):
                        for h in range(1, att.blocks[r]):
                            if h == 1:
                                eng.wait_ge(scaled_s, 2 * (n + c) + r + 1)
                            else:
                                eng.wait_ge(sel_s, sel_before + c * more + done)
                            nc.vector.scalar_tensor_tensor(
                                by_item(sel(r, c)), block(r, h, c), W[:, ms + 4 * r + h:ms + 4 * r + h + 1],
                                by_item(sel(r, c)), ALU.mult, ALU.add).then_inc(sel_s, 1)
                            done += 1
                if role == "pe":
                    eng.wait_ge(scaled_s, 2 * (n + c) + 2)
                    if more:
                        eng.wait_ge(sel_s, sel_before + (c + 1) * more)
                    for r in range(2):
                        mm = nc.tensor.matmul(ps[32 * c:32 * c + 32, 4, :], w(den, r * 32, r * 32 + 32), sel(r, c),
                                              start=(r == 0), stop=(r == 1), tile_position=(0, 32 * c))
                    mm.then_inc(den_s, 1)
            if role == "dve":
                eng.wait_ge(den_s, n + NC)
                nc.vector.reciprocal(REC, ps[:, 4, :]).then_inc(rec_s, 1)
            if role == "act":
                eng.wait_ge(rec_s, call + 1)
                for c in range(NC):
                    nc.scalar.activation(own(c), REC, ACT.Copy, scale=W[:, quad + c:quad + c + 1]).then_inc(own_s, 1)

            def spread_heads(c):
                eng.wait_ge(own_s, n + c + 1)
                for r in range(2):
                    nc.tensor.matmul(bank(r, c), w(den, 64 + r * D, 64 + (r + 1) * D), own(c),
                                     start=True, stop=True).then_inc(spread_s, 1)

            if role == "pe":
                spread_heads(0)
            for c in range(NC):
                if role == "pe":
                    if c + 1 < NC:
                        spread_heads(c + 1)
                    for r in range(2):
                        eng.wait_ge(on_s, 2 * (n + c) + r + 1)
                        mm = nc.tensor.matmul(lo_bank(c), w(wname, r * D, (r + 1) * D), sel(r, c),
                                              start=(r == 0), stop=(r == 1))
                    mm.then_inc(pe_s, 1)
            for c in range(NC + 1):
                if role == "dve" and c < NC:
                    for r in range(2):
                        eng.wait_ge(spread_s, 2 * (n + c) + r + 1)
                        nc.vector.tensor_tensor(sel(r, c), sel(r, c), bank(r, c), ALU.mult).then_inc(on_s, 1)
                if role == "dve" and c > 0:
                    p = c - 1
                    eng.wait_ge(pe_s, n + p + 1)
                    if bname is None:
                        ins = nc.vector.tensor_tensor(ck(dst, p), lo_bank(p), ck(residual, p), ALU.add)
                    else:
                        ins = nc.vector.scalar_tensor_tensor(ck(dst, p), lo_bank(p), bias(bname), ck(residual, p),
                                                             ALU.add, ALU.add)
                    ins.then_inc(out_s, 1)
            return out_s, n + 1


        def diagonal_attention(role, eng, ready):
            s = {k: sem(f"dg_{k}") for k in ("q", "k", "v", "qev", "prod", "s", "top", "rel", "e", "rec", "vev", "p",
                                             "an", "o", "out")}
            root = float(np.sqrt(np.float32(D)))
            for c in range(NC):
                if role == "pe":
                    eng.wait_ge(ready[0], ready[1] + c)
                    nc.tensor.matmul(lo_bank(c), w("c_q"), ck(T, c), start=True, stop=True).then_inc(s["q"], 1)
                    nc.tensor.matmul(hi_bank(c), w("c_k"), ck(T, c), start=True, stop=True).then_inc(s["k"], 1)
                if role == "act":
                    eng.wait_ge(s["q"], c + 1)
                    nc.scalar.activation(ck(A, c), lo_bank(c), ACT.Identity, bias=bias("c_bq")).then_inc(s["qev"], 1)
                if role == "dve":
                    eng.wait_ge(s["qev"], c + 1)
                    eng.wait_ge(s["k"], c + 1)
                    nc.vector.scalar_tensor_tensor(ck(A, c), hi_bank(c), bias("c_bk"), ck(A, c),
                                                   ALU.add, ALU.mult).then_inc(s["prod"], 1)
            for c in range(NC):
                if role == "pe":
                    eng.wait_ge(s["prod"], c + 1)
                    nc.tensor.matmul(lo_bank(c), w("c_v"), ck(T, c), start=True, stop=True).then_inc(s["v"], 1)
                    for i in range(4):
                        t = 4 * c + i
                        mm = nc.tensor.matmul(hi_bank(c // 2 * 2)[:, t % 8:t % 8 + 1], A[:, t * 128:(t + 1) * 128],
                                              w("ones", 0, 1), start=True, stop=True)
                    if c % 2:
                        mm.then_inc(s["s"], 1)
                if role == "act":
                    eng.wait_ge(s["v"], c + 1)
                    nc.scalar.activation(ck(Bt, c), lo_bank(c), ACT.Identity, bias=bias("c_bv")).then_inc(s["vev"], 1)
            for h in range(2):
                cols = slice(8 * h, 8 * h + 8)
                if role == "dve":
                    eng.wait_ge(s["s"], h + 1)
                    nc.vector.tensor_scalar(DEV[:, cols], hi_bank(2 * h)[:, 0:8], root, None, ALU.mult
                                            ).then_inc(s["top"], 1)
                    eng.wait_ge(s["top"], h + 1)
                    nc.vector.scalar_tensor_tensor(COL[:, cols], hi_bank(2 * h)[:, 0:8], root, DEV[:, cols],
                                                   ALU.mult, ALU.subtract).then_inc(s["rel"], 1)
                if role == "act":
                    eng.wait_ge(s["rel"], h + 1)
                    nc.scalar.activation(COL[:, cols], COL[:, cols], ACT.Exp).then_inc(s["e"], 1)
            for h in range(2):
                cols = slice(8 * h, 8 * h + 8)
                if role == "dve":
                    eng.wait_ge(s["e"], h + 1)
                    nc.vector.reciprocal(DEV[:, cols], COL[:, cols]).then_inc(s["rec"], 1)
                    eng.wait_ge(s["rec"], h + 1)
                    nc.vector.tensor_tensor(COL[:, cols], COL[:, cols], DEV[:, cols], ALU.mult).then_inc(s["p"], 1)
            for c in range(NC):
                spread_s, first = spread(role, eng, 1, c, (s["p"], c // 2 + 1))
            for c in range(NC):
                if role == "dve":
                    eng.wait_ge(s["vev"], c + 1)
                    eng.wait_ge(spread_s, first + c)
                    nc.vector.tensor_tensor(ck(A, c), ck(Bt, c), hi_bank(c), ALU.mult).then_inc(s["an"], 1)
                if role == "pe":
                    eng.wait_ge(s["an"], c + 1)
                    nc.tensor.matmul(lo_bank(c), w("c_o"), ck(A, c), start=True, stop=True).then_inc(s["o"], 1)
            for c in range(NC):
                if role == "dve":
                    eng.wait_ge(s["o"], c + 1)
                    nc.vector.scalar_tensor_tensor(ck(A, c), lo_bank(c), bias("c_bo"), ck(T, c),
                                                   ALU.add, ALU.add).then_inc(s["out"], 1)
            return s["out"], 1

        def dense_ff(role, eng, ready):
            s = {k: sem(f"ff_{k}") for k in ("h", "relu", "y", "out")}
            nf = FF // D
            for f in range(nf + 1):
                for c in range(NC):
                    buf = Bt if f % 2 == 0 else C
                    if f < nf:
                        if role == "pe":
                            if f == 0:
                                eng.wait_ge(ready[0], ready[1] + c)
                            else:
                                eng.wait_ge(s["relu"], (f - 1) * NC + c + 1)
                            nc.tensor.matmul(hi_bank(c), w("lin1", f * D, (f + 1) * D), ck(T, c),
                                             start=True, stop=True).then_inc(s["h"], 1)
                        if role == "act":
                            if f >= 2:
                                eng.wait_ge(s["y"], (f - 2) * NC + c + 1)
                            eng.wait_ge(s["h"], f * NC + c + 1)
                            nc.scalar.activation(ck(buf, c), hi_bank(c), ACT.Relu,
                                                 bias=bias(f"l1b{f}")).then_inc(s["relu"], 1)
                    if f > 0 and role == "pe":
                        g = f - 1
                        buf = Bt if g % 2 == 0 else C
                        eng.wait_ge(s["relu"], g * NC + c + 1)
                        nc.tensor.matmul(lo_bank(c), w("lin2", g * D, (g + 1) * D), ck(buf, c),
                                         start=(g == 0), stop=(g == nf - 1)).then_inc(s["y"], 1)
            for c in range(NC):
                if role == "dve":
                    eng.wait_ge(s["y"], (nf - 1) * NC + c + 1)
                    nc.vector.scalar_tensor_tensor(ck(A, c), lo_bank(c), bias("l2b"), ck(T, c),
                                                   ALU.add, ALU.add).then_inc(s["out"], 1)
            return s["out"], 1

        def add_to_stream(role, eng, ready):
            s = sem("l0_added")
            if role == "dve":
                for c in range(NC):
                    eng.wait_ge(ready[0], ready[1] + c)
                    nc.vector.tensor_tensor(ck(X, c), ck(X, c), ck(T, c), ALU.add).then_inc(s, 1)
            return s, 1

        def rotary(role, eng, call, wname, rows, srcT, ready, parts):
            s = {k: sem(f"rot_{k}") for k in ("pe", "cos", "sin", "rot", "hi", "lo")}
            n = call * NC
            o = W_AT["rope"][0]
            nb = CH // S
            for c in range(NC):
                if role == "pe":
                    eng.wait_ge(ready[0], ready[1] + c)
                    nc.tensor.matmul(lo_bank(c), w(wname, 0, D, rows=rows), srcT[0:rows, c * CH:(c + 1) * CH],
                                     start=True, stop=True)
                    nc.tensor.matmul(hi_bank(c), w(wname, D, 2 * D, rows=rows), srcT[0:rows, c * CH:(c + 1) * CH],
                                     start=True, stop=True).then_inc(s["pe"], 1)
                if role == "dve":
                    def tab(k):
                        return W[:, o + k * S:o + (k + 1) * S].unsqueeze(1).broadcast_to([128, nb, S])
                    eng.wait_ge(s["pe"], n + c + 1)
                    if call:
                        eng.wait_ge(s["lo"], c + 1)
                    nc.vector.tensor_tensor(ck(A, c).rearrange("p (b q) -> p b q", b=nb),
                                            lo_bank(c).rearrange("p (b q) -> p b q", b=nb), tab(0), ALU.mult
                                            ).then_inc(s["cos"], 1)
                    nc.vector.tensor_tensor(ck(Bt, c).rearrange("p (b q) -> p b q", b=nb),
                                            hi_bank(c).rearrange("p (b q) -> p b q", b=nb), tab(1), ALU.mult
                                            ).then_inc(s["sin"], 1)
                    eng.wait_ge(s["cos"], n + c + 1)
                    eng.wait_ge(s["sin"], n + c + 1)
                    nc.vector.tensor_tensor(ck(A, c), ck(A, c), ck(Bt, c), ALU.add).then_inc(s["rot"], 1)
                if role == "act":
                    eng.wait_ge(s["rot"], n + c + 1)
                    nc.scalar.activation(ck(parts[:, 0, :], c), ck(A, c), ACT.Copy).then_inc(s["hi"], 1)
                if role == "pool":
                    eng.wait_ge(s["hi"], n + c + 1)
                    nc.gpsimd.tensor_tensor(ck(parts[:, 1, :], c), ck(A, c), ck(parts[:, 0, :], c),
                                            ALU.subtract).then_inc(s["lo"], 1)
            return s["lo"], n + 1

        def moe_stage(role, eng, ready):
            s = {k: sem(f"moe_{k}") for k in ("logit", "score", "chain", "parts", "turned", "weights", "gu", "gate",
                                             "hid", "mid", "down", "out", "xhi", "xlo", "whi", "wlo")}
            NT = N // 128
            at = [0]

            def area(n):
                at[0] += n
                return ABO[:, at[0] - n:at[0]]

            SC = area(NT * E).rearrange("p (t e) -> p t e", t=NT)
            SFC = area(NT * E).rearrange("p (t e) -> p t e", t=NT)
            GSC = area(NT * 12).rearrange("p (t e) -> p t e", t=NT)
            GM8 = area(NT * 8).rearrange("p (t e) -> p t e", t=NT)
            GR = area(NT * 12).rearrange("p (t e) -> p t e", t=NT)
            GM = area(NT * 8).rearrange("p (t e) -> p t e", t=NT)
            MK = area(NT * 34).rearrange("p (t e) -> p t e", t=NT)
            MK8 = area(NT * 8).rearrange("p (t e) -> p t e", t=NT)
            MR = area(NT * 34).rearrange("p (t e) -> p t e", t=NT)
            TW = area(NT * E).rearrange("p (t e) -> p t e", t=NT)
            SM = area(NT)
            CBS = area(NT * E).bitcast(BF16).rearrange("p (t e) -> p t e", t=NT)
            CTT = HL[0:2 * E, 0, :]
            assert at[0] <= 2 * N
            XP = HLQ
            WP = ABO[:, 3 * N:3 * N + SLOTS * 2 * D].bitcast(BF16).rearrange("p (s a n) -> p s a n", s=SLOTS, a=2)

            if role == "pe":
                for c in range(NC):
                    eng.wait_ge(ready[0], ready[1] + c)
                for t in range(NT):
                    mm = nc.tensor.matmul(ps[:, 0, t * E:(t + 1) * E], T[:, t * 128:(t + 1) * 128], w("gate"),
                                          start=True, stop=True)
                mm.then_inc(s["logit"], 1)
            if role == "act":
                eng.wait_ge(s["logit"], 1)
                nc.scalar.activation(SC, ps[:, 0, :].rearrange("p (t e) -> p t e", t=NT), ACT.Sigmoid
                                     ).then_inc(s["score"], 1)
                for c in range(NC):
                    eng.wait_ge(ready[0], ready[1] + c)
                    nc.scalar.activation(ck(XP[:, 0, :], c), ck(T, c), ACT.Copy).then_inc(s["xhi"], 1)
            if role == "pool":
                for c in range(NC):
                    eng.wait_ge(s["xhi"], c + 1)
                    nc.gpsimd.tensor_tensor(ck(XP[:, 1, :], c), ck(T, c), ck(XP[:, 0, :], c), ALU.subtract
                                            ).then_inc(s["xlo"], 1)
            if role == "dve":
                n = [0]

                def link(ins, wait=True):
                    n[0] += 1
                    ins.then_inc(s["chain"], 1)
                    if wait:
                        eng.wait_ge(s["chain"], n[0])

                eng.wait_ge(s["score"], 1)
                link(nc.vector.tensor_tensor(SFC, SC, w("gate_b").unsqueeze(1).broadcast_to([128, NT, E]), ALU.add))
                link(nc.vector.memset(GSC[:, :, NG:12], BIG))
                link(nc.vector.memset(MK[:, :, E:34], BIG))
                link(nc.vector.reduce_max(GSC[:, :, 0:NG], SFC.rearrange("p t (g s) -> p t g s", g=NG), AX.X))
                for t in range(NT):
                    link(nc.vector.max(GM8[:, t, :], GSC[:, t, :]), t == NT - 1)
                for t in range(NT):
                    link(nc.vector.match_replace(GR[:, t, :], GM8[:, t, :], GSC[:, t, :], -BIG), t == NT - 1)
                link(nc.vector.tensor_scalar(GM, GR[:, :, 0:NG], -BIG, None, ALU.is_equal))
                link(nc.vector.tensor_tensor(MK[:, :, 0:E].rearrange("p t (g s) -> p t g s", g=NG),
                                             SFC.rearrange("p t (g s) -> p t g s", g=NG),
                                             GM.unsqueeze(3).broadcast_to([128, NT, NG, GS]), ALU.mult))
                link(nc.vector.tensor_scalar(MK[:, :, 0:E], MK[:, :, 0:E], 0.0, None, ALU.add))
                for t in range(NT):
                    link(nc.vector.max(MK8[:, t, :], MK[:, t, :]), t == NT - 1)
                for t in range(NT):
                    link(nc.vector.match_replace(MR[:, t, :], MK8[:, t, :], MK[:, t, :], -BIG), t == NT - 1)
                link(nc.vector.tensor_scalar(MR[:, :, 0:E], MR[:, :, 0:E], -BIG, None, ALU.is_equal))
                link(nc.vector.tensor_tensor(TW, SC, MR[:, :, 0:E], ALU.mult))
                link(nc.vector.reduce_sum(SM, TW, AX.X))
                link(nc.vector.tensor_scalar(SM, SM, 1e-20, None, ALU.add))
                link(nc.vector.reciprocal(SM, SM))
                link(nc.vector.tensor_tensor(TW, TW, SM.unsqueeze(2).broadcast_to([128, NT, E]), ALU.mult))
                link(nc.vector.tensor_scalar(TW, TW, ROUTE_SCALE, None, ALU.mult))
                link(nc.vector.tensor_copy(CBS[:, :, 0:E], TW))
                nc.vector.tensor_tensor(CBS[:, :, E:2 * E], TW, CBS[:, :, 0:E], ALU.subtract).then_inc(s["parts"], 1)
            if role == "act":
                eng.wait_ge(s["turned"], 1)
                for i in range(2):
                    nc.scalar.activation(CTT[:, i * 1024:(i + 1) * 1024], ps[0:2 * E, 6 + i, :].bitcast(BF16), ACT.Copy
                                         ).then_inc(s["weights"], 1)

            NI = E // 2 + 1
            loads = [sem(f"moe_load{i}") for i in range(SLOTS)]

            def ew(item_slot, k):
                if item_slot is None:
                    return w("shared", k * D, (k + 1) * D)
                return CT[:, item_slot // 2, (item_slot % 2 * 3 + k) * D:(item_slot % 2 * 3 + k + 1) * D]

            def unit(sweep, item, cc):
                return (item + sweep * NI) * 2 + cc

            def up(sweep, item, slot, cc):
                x = ck(T, 2 * sweep + cc)
                if cc == 0 and slot is not None:
                    eng.wait_ge(loads[slot], (sweep * (NI - 1) * 32 // SLOTS) + ((item - 1 - slot) * (32 // SLOTS)) + 32)
                if sweep or not (isinstance(item, int) and item == 0):
                    eng.wait_ge(s["hid"], unit(sweep, item, cc) - 1)
                if not sweep and slot == 0 and isinstance(item, int) and cc == 0:
                    eng.wait_ge(s["weights"], 2)
                    eng.wait_ge(s["xlo"], NC)
                if slot is None:
                    nc.tensor.matmul(ps[:, 2 + cc, :], ew(slot, 0), x, start=True, stop=True)
                    mm = nc.tensor.matmul(ps[:, 4 + cc, :], ew(slot, 1), x, start=True, stop=True)
                else:
                    if cc == 0:
                        eng.wait_ge(s["wlo"], sweep * (NI - 1) + item)
                    for k in range(2):
                        for i, (a, b) in enumerate(((0, 0), (1, 0), (0, 1))):
                            nc.tensor.matmul(ps[:, 2 + 2 * k + cc, :], WP[:, slot, a, k * D:(k + 1) * D],
                                             ck(XP[:, b, :], 2 * sweep + cc), start=(i == 0), stop=(i == 2))
                    mm = nc.tensor.matmul(ps[:, 6 + cc, :], HL[0:2 * E, 1, slot * 128:(slot + 1) * 128],
                                          ck(CTT, 2 * sweep + cc), start=True, stop=True)
                mm.then_inc(s["gu"], 1)

            def down(sweep, item, slot, cc, last=False):
                if slot is None and sweep:
                    eng.wait_ge(s["out"], cc + 1)
                eng.wait_ge(s["hid"], unit(sweep, item, cc) + 1)
                nc.tensor.matmul(ps[:, cc, :], ew(slot, 2), Pb[:, 1, cc * CH:(cc + 1) * CH],
                                 start=(slot is None), stop=last).then_inc(s["down"], 1)

            def pe_item(sweep, item, slot, prev, prev_slot):
                for cc in range(2):
                    up(sweep, item, slot, cc)
                    down(sweep, prev, prev_slot, cc)

            def raw(slot):
                return CT[:, slot // 2, slot % 2 * 3 * D:(slot % 2 * 3 + 2) * D]

            def act_parts(sweep, item, slot):
                if not isinstance(item, int) or item > SLOTS:
                    eng.wait_ge(s["down"], unit(sweep, item, 0) - 2 * SLOTS + 2)
                elif sweep:
                    eng.wait_ge(s["down"], unit(sweep, item, 0) - 2 * SLOTS)
                eng.wait_ge(loads[slot], (sweep * (NI - 1) * 32 // SLOTS) + ((item - 1 - slot) * (32 // SLOTS)) + 32)
                nc.scalar.activation(WP[:, slot, 0, :], raw(slot), ACT.Copy).then_inc(s["whi"], 1)

            def pool_parts(sweep, item, slot):
                eng.wait_ge(s["whi"], sweep * (NI - 1) + item)
                eng.sem_inc(sem("pool_settled"), 1)
                nc.gpsimd.tensor_tensor(WP[:, slot, 1, :], raw(slot), WP[:, slot, 0, :], ALU.subtract
                                        ).then_inc(s["wlo"], 1)

            def act_item(sweep, item):
                for cc in range(2):
                    eng.wait_ge(s["gu"], unit(sweep, item, cc) + 1)
                    nc.scalar.activation(Pb[:, 0, cc * CH:(cc + 1) * CH], ps[:, 2 + cc, :], ACT.Silu
                                         ).then_inc(s["gate"], 1)

            def dve_item(sweep, item, shared=False):
                for cc in range(2):
                    h = Pb[:, 1, cc * CH:(cc + 1) * CH]
                    eng.wait_ge(s["gate"], unit(sweep, item, cc) + 1)
                    if sweep or not (isinstance(item, int) and item == 0):
                        eng.wait_ge(s["down"], unit(sweep, item, cc) - 1)
                    ins = nc.vector.tensor_tensor(h, ps[:, 4 + cc, :], Pb[:, 0, cc * CH:(cc + 1) * CH], ALU.mult)
                    if not shared:
                        ins.then_inc(s["mid"], 1)
                        eng.wait_ge(s["mid"], unit(sweep, item, cc) + 1 - 2 * (sweep + 1))
                        ins = nc.vector.tensor_tensor(h, h, ps[:, 6 + cc, :], ALU.mult)
                    ins.then_inc(s["hid"], 1)

            def sp_item(sweep, item, slot):
                if not isinstance(item, int):
                    eng.wait_ge(s["down"], unit(sweep, item, 0) - 2 * SLOTS + 2)
                elif sweep:
                    eng.wait_ge(s["down"], unit(sweep, item, 0) - 2 * SLOTS)
                eng.dma_start(CT[:, slot // 2, slot % 2 * 3 * D:(slot % 2 + 1) * 3 * D], experts[item - 1]
                              ).then_inc(loads[slot], 16)
                eng.dma_start(HL[0:2 * E, 1, slot * 128:(slot + 1) * 128], picks[item - 1]).then_inc(loads[slot], 16)

            if role == "sp":
                eng.wait_ge(ready[0], ready[1])
            for sweep in range(2):
                if role == "pe":
                    up(sweep, 0, None, 0)
                    up(sweep, 0, None, 1)
                    if sweep == 0:
                        eng.wait_ge(s["parts"], 1)
                        for t in range(NT):
                            tr = nc.tensor.transpose(ps[0:2 * E, 6 + t // 8, :].bitcast(BF16)[:, t % 8 * 128:(t % 8 + 1) * 128],
                                                     CBS[:, t, :], wb("ident16"))
                        tr.then_inc(s["turned"], 1)
                    pe_item(sweep, 1, 0, 0, None)
                    for k in range(1, SLOTS):
                        pe_item(sweep, k + 1, k, k, k - 1)
                    with eng.Fori(1, NI // SLOTS) as i:
                        for k in range(SLOTS):
                            pe_item(sweep, i * SLOTS + (k + 1), k, i * SLOTS + k, (k - 1) % SLOTS)
                    for cc in range(2):
                        down(sweep, NI - 1, SLOTS - 1, cc, last=True)
                if role == "act":
                    act_parts(sweep, 1, 0)
                    act_item(sweep, 0)
                    for k in range(SLOTS):
                        act_parts(sweep, k + 2, (k + 1) % SLOTS)
                        act_item(sweep, k + 1)
                    with eng.Fori(1, NI // SLOTS - 1) as i:
                        for k in range(SLOTS):
                            act_parts(sweep, i * SLOTS + (k + 2), (k + 1) % SLOTS)
                            act_item(sweep, i * SLOTS + (k + 1))
                    for k in range(SLOTS):
                        if k < SLOTS - 1:
                            act_parts(sweep, NI - SLOTS + k + 1, k + 1)
                        act_item(sweep, NI - SLOTS + k)
                if role == "pool":
                    with eng.Fori(0, NI // SLOTS) as i:
                        for k in range(SLOTS):
                            pool_parts(sweep, i * SLOTS + (k + 1), k)
                if role == "dve":
                    dve_item(sweep, 0, shared=True)
                    with eng.Fori(0, NI // 2) as i:
                        dve_item(sweep, i * 2 + 1)
                        dve_item(sweep, i * 2 + 2)
                    for cc in range(2):
                        eng.wait_ge(s["down"], unit(sweep, NI - 1, cc) + 1)
                        x = ck(X, 2 * sweep + cc)
                        nc.vector.tensor_tensor(x, x, ps[:, cc, :], ALU.add).then_inc(s["out"], 1)
                if role == "sp":
                    for k in range(SLOTS):
                        sp_item(sweep, k + 1, k)
                    with eng.Fori(1, NI // SLOTS) as i:
                        for k in range(SLOTS):
                            sp_item(sweep, i * SLOTS + (k + 1), k)
            return s["out"], 1

        def tree_stage(role, eng, ready):
            s = {k: sem(f"tree_{k}") for k in ("log", "dec", "acts", "path", "msk", "down", "out")}
            loads = [sem(f"moe_load{i}") for i in range(SLOTS)]
            loads_before = 2 * (E // 2) // SLOTS * 32
            WOFF = (0, INNER, NODES, NODES + D, NODES + 2 * D)
            TCOLS = WOFF[4] + 2
            tree_c = B_AT["tree"][0]

            def tw(slot, k, rows=128, cols=128):
                o = slot % 2 * TCOLS + WOFF[k]
                return CT[0:rows, slot // 2, o:o + cols]

            def unit(sweep, tree, cc):
                return (tree + sweep * TREES) * 2 + cc

            def logits(sweep, tree, slot, cc):
                if cc == 0:
                    eng.wait_ge(loads[slot], loads_before + sweep * 16 * TREES // SLOTS + (tree - slot) * (16 // SLOTS) + 16)
                x = ck(T, 2 * sweep + cc)
                nc.tensor.matmul(ps[0:INNER, 2 + cc, :], tw(slot, 0, cols=INNER), x, start=True, stop=True)
                nc.tensor.matmul(ps[:, 4 + cc, :], tw(slot, 1), x, start=True, stop=True).then_inc(s["log"], 1)

            def paths(sweep, tree, cc):
                eng.wait_ge(s["dec"], unit(sweep, tree, cc) + 1)
                nc.tensor.matmul(ps[0:INNER, 6, :], WB[0:INNER, tree_c:tree_c + INNER], DEC[0:INNER, cc, :],
                                 start=True, stop=True)
                nc.tensor.matmul(ps[:, 7, :], WB[0:INNER, tree_c + INNER:tree_c + NODES], DEC[0:INNER, cc, :],
                                 start=True, stop=True).then_inc(s["path"], 1)

            def down(sweep, tree, slot, cc, first=False, last=False):
                eng.wait_ge(s["msk"], (unit(sweep, tree, cc) + 1) * 2)
                if first and sweep:
                    eng.wait_ge(s["out"], cc + 1)
                nc.tensor.matmul(ps[:, cc, :], tw(slot, 2, rows=INNER), Pb[0:INNER, cc, 0:CH], start=first, stop=False)
                nc.tensor.matmul(ps[:, cc, :], tw(slot, 3), Pb[:, cc, CH:2 * CH], start=False, stop=last
                                 ).then_inc(s["down"], 1)

            def pe_tree(sweep, tree, slot, first=False, last=False):
                logits(sweep, tree, slot, 0)
                if not first:
                    down(sweep, tree - 1, (slot - 1) % SLOTS, 1, first=(isinstance(tree, int) and tree == 1))
                paths(sweep, tree, 0)
                logits(sweep, tree, slot, 1)
                down(sweep, tree, slot, 0, first=(isinstance(tree, int) and tree == 0), last=last)
                paths(sweep, tree, 1)

            def biases(slot, leaf, rows):
                o = slot % 2 * TCOLS + WOFF[4] + leaf
                return CT[0:rows, slot // 2, o:o + 1]

            def act_tree(sweep, tree, slot):
                for cc in range(2):
                    n = unit(sweep, tree, cc)
                    eng.wait_ge(s["log"], n + 1)
                    if sweep or not (isinstance(tree, int) and tree == 0):
                        eng.wait_ge(s["down"], n - 1)
                    nc.scalar.activation(Pb[0:INNER, cc, 0:CH], ps[0:INNER, 2 + cc, :], ACT.Silu,
                                         bias=biases(slot, 0, INNER))
                    nc.scalar.activation(Pb[:, cc, CH:2 * CH], ps[:, 4 + cc, :], ACT.Silu, bias=biases(slot, 1, 128)
                                         ).then_inc(s["acts"], 1)

            def dve_tree(sweep, tree, slot):
                for cc in range(2):
                    n = unit(sweep, tree, cc)
                    eng.wait_ge(s["acts"], n + 1)
                    nc.vector.tensor_scalar(DEC[0:INNER, cc, :], ps[0:INNER, 2 + cc, :], biases(slot, 0, INNER), 0.0,
                                            ALU.add, ALU.is_gt).then_inc(s["dec"], 1)
                    eng.wait_ge(s["path"], n + 1)
                    for k, rows, thr in ((0, INNER, "thr0"), (1, 128, "thr1")):
                        h = Pb[0:rows, cc, k * CH:(k + 1) * CH]
                        nc.vector.scalar_tensor_tensor(h, ps[0:rows, 6 + k, :], bias(thr, rows), h, ALU.is_ge,
                                                       ALU.mult).then_inc(s["msk"], 1)

            def sp_tree(sweep, tree, slot):
                if sweep or tree >= SLOTS:
                    eng.wait_ge(s["down"], unit(sweep, tree, 0) - 2 * SLOTS + 2)
                eng.dma_start(CT[:, slot // 2, slot % 2 * TCOLS:(slot % 2 + 1) * TCOLS], trees[tree]
                              ).then_inc(loads[slot], 16)

            if role == "sp":
                eng.wait_ge(ready[0], ready[1])
            if role == "pe":
                for c in range(NC):
                    eng.wait_ge(ready[0], ready[1] + c)
            for sweep in range(2):
                if role == "pe":
                    for tree in range(TREES):
                        pe_tree(sweep, tree, tree % SLOTS, first=(tree == 0), last=(tree == TREES - 1))
                    down(sweep, TREES - 1, (TREES - 1) % SLOTS, 1, last=True)
                if role == "act":
                    for tree in range(TREES):
                        act_tree(sweep, tree, tree % SLOTS)
                if role == "dve":
                    for tree in range(TREES):
                        dve_tree(sweep, tree, tree % SLOTS)
                    for cc in range(2):
                        eng.wait_ge(s["down"], unit(sweep, TREES - 1, cc) + 1)
                        x = ck(X, 2 * sweep + cc)
                        nc.vector.tensor_tensor(x, x, ps[:, cc, :], ALU.add).then_inc(s["out"], 1)
                if role == "sp":
                    for tree in range(TREES):
                        sp_tree(sweep, tree, tree % SLOTS)
            return s["out"], 1

        def choice_stage(role, eng, ready):
            s = {k: sem(f"ch_{k}") for k in ("h", "relu", "i", "imp", "rows", "chain", "not")}
            if role == "pe":
                for c in range(NC):
                    eng.wait_ge(ready[0], ready[1] + c)
                    nc.tensor.matmul(ps[0:64, c, :], w("ws1"), ck(T, c), start=True, stop=True).then_inc(s["h"], 1)
                for c in range(NC):
                    eng.wait_ge(s["relu"], c + 1)
                    nc.tensor.matmul(ps[0:1, 4 + c, :], w("ws2", rows=64), A[0:64, c * CH:(c + 1) * CH],
                                     start=True, stop=True).then_inc(s["i"], 1)
            if role == "act":
                for c in range(NC):
                    eng.wait_ge(s["h"], c + 1)
                    nc.scalar.activation(A[0:64, c * CH:(c + 1) * CH], ps[0:64, c, :], ACT.Relu, bias=bias("bs1", 64)
                                         ).then_inc(s["relu"], 1)
                for c in range(NC):
                    eng.wait_ge(s["i"], c + 1)
                    nc.scalar.activation(Bt[0:1, c * CH:(c + 1) * CH], ps[0:1, 4 + c, :], ACT.Sigmoid, bias=bias("bs2", 1)
                                         ).then_inc(s["imp"], 1)
            IM = C[0:B, 0:S]
            TOP = [C[0:B, 64 + 8 * i:72 + 8 * i] for i in range(2)]
            LEFT = [C[0:B, 128 + S * i:128 + S * (i + 1)] for i in range(2)]
            if role == "sp":
                eng.wait_ge(s["imp"], NC)
                eng.dma_start(IM, Bt[0:1, :].rearrange("a (b q) -> a b q", b=B)).then_inc(s["rows"], 16)
                eng.wait_ge(s["not"], 2)
                for k, stacked in enumerate((KSA, QS)):
                    for g in range(4):
                        eng.dma_start(stacked[98:99, g, :].rearrange("a (b q) -> a b q", b=B), NSB[:, k, :]
                                      ).then_inc(sem("mask_rows"), 16)
            if role == "dve":
                eng.wait_ge(s["rows"], 16)
                cur = IM
                for i in range(SEL_K // 8):
                    nc.vector.max(TOP[i], cur).then_inc(s["chain"], 1)
                    eng.wait_ge(s["chain"], 2 * i + 1)
                    nc.vector.match_replace(LEFT[i], TOP[i], cur, -1.0).then_inc(s["chain"], 1)
                    eng.wait_ge(s["chain"], 2 * i + 2)
                    cur = LEFT[i]
                nc.vector.tensor_scalar(NSB[:, 0, :], cur, 0.0, None, ALU.is_ge).then_inc(s["not"], 1)
                nc.vector.tensor_scalar(NSB[:, 1, :], cur, 0.0, MASKED, ALU.is_ge, ALU.mult).then_inc(s["not"], 1)
            return ready

        def program(role, eng):
            first_w, stream, rest_w = sem("loaded_first"), sem("loaded_stream"), sem("loaded_rest")
            if role == "sp":
                eng.dma_start(W[:, 0:W_EARLY], wpack[:, 0:W_EARLY]).then_inc(first_w, 16)
                load_context(role, eng, XA0, 0)
                eng.dma_start(X[:, :], xT).then_inc(stream, 16)
                eng.dma_start(W[:, W_EARLY:], wpack[:, W_EARLY:]).then_inc(rest_w, 16)
                eng.dma_start(WB[:, :], bpack).then_inc(rest_w, 16)
                load_context(role, eng, XA0, 1)
            if role == "dve":
                nc.vector.memset(epst[:, :], EPS).then_inc(sem("eps_set"), 1)
            if role == "pool":
                for keys in (KST, KSS):
                    nc.gpsimd.memset(keys[96:98, :, :, :].rearrange("p a g k -> p (a g k)"), 1.0
                                     ).then_inc(sem("ones_set"), 1)
                nc.gpsimd.memset(QS[96:98, :, :].rearrange("p g n -> p (g n)"), 0.0).then_inc(sem("ones_set"), 1)
            if role == "act":
                eng.wait_ge(sem("eps_set"), 1)
            eng.wait_ge(first_w, 16)
            attention(role, eng, XA0, "first", None)
            if role == "pe":
                eng.wait_ge(stream, 16)
            s = layernorm(role, eng, 0, X, T, None)
            s = diagonal_attention(role, eng, s)
            s = layernorm(role, eng, 1, A, T, s, gain="g1", shift="b1")
            eng.wait_ge(rest_w, 32)
            q_lo = project_split(role, eng, 0, w("c_wq"), "bq0", s, HLQ)
            s = split_rows(role, eng, 0, q_lo, QS, "q")
            attention(role, eng, XA0, "rest", s, None, (q_lo[0], q_lo[1] + NC - 1))
            s = attention_out(role, eng, XA0, 0, "xa0_o", "xa0_den", "bo0", A, T)
            s = layernorm(role, eng, 2, A, T, s, gain="g2", shift="b2")
            s = dense_ff(role, eng, s)
            s = layernorm(role, eng, 3, A, T, s, gain="g3", shift="b3")
            s = add_to_stream(role, eng, s)

            if role == "sp":
                for stacked, row in ((KSA, "krow"), (QS, "qrow")):
                    eng.dma_start(stacked[98:99, :, :].rearrange("a g (b q) -> a (g b) q", b=B),
                                  wb(row, rows=1).unsqueeze(1).broadcast_to([1, 4 * B, S])).then_inc(sem("mask_rows"), 16)
            s = layernorm(role, eng, 4, X, T, s)
            q_lo = rotary(role, eng, 0, "sa0_q", D, T, s, HLQ)
            s = split_rows(role, eng, 1, q_lo, QS, "q")
            lat_pe, lat = sem("lat_pe"), sem("lat_out")
            if role == "pe":
                for c in range(NC):
                    eng.wait_ge(q_lo[0], q_lo[1] + c)
                    nc.tensor.matmul(lo_bank(c)[0:64, :], w("down"), ck(T, c), start=True, stop=True).then_inc(lat_pe, 1)
            if role == "act":
                for c in range(NC):
                    eng.wait_ge(lat_pe, c + 1)
                    nc.scalar.activation(C[0:64, c * CH:(c + 1) * CH], lo_bank(c)[0:64, :], ACT.Copy).then_inc(lat, 1)
            k_lo = rotary(role, eng, 1, "sa0_k", 64, C, (lat, 1), HL)
            if role == "sp":
                eng.wait_ge(lat, NC)
            attention(role, eng, SA0, "first", s, C)
            s = split_rows(role, eng, 2, k_lo, KSA, "k")
            attention(role, eng, SA0, "rest", s, C, (k_lo[0], k_lo[1] + NC - 1))
            s = attention_out(role, eng, SA0, 1, "sa0_o", "den16", None, X, X)

            s = layernorm(role, eng, 5, X, T, s)
            s = moe_stage(role, eng, s)
            if role == "pe":
                eng.wait_ge(s[0], NC)

            if role == "sp":
                eng.wait_ge(s[0], NC)
            load_context(role, eng, XA1, 0)
            load_context(role, eng, XA1, 1)
            attention(role, eng, XA1, "first", None)
            s = layernorm(role, eng, 6, X, T, s)
            q_lo = project_split(role, eng, 1, w("xa1_q"), "bq1", s, HLQ)
            s = split_rows(role, eng, 3, q_lo, QS, "q")
            attention(role, eng, XA1, "rest", s, None, (q_lo[0], q_lo[1] + NC - 1))
            s = attention_out(role, eng, XA1, 2, "xa1_o", "den16", "bo1", X, X)

            s = layernorm(role, eng, 7, X, T, s)
            s = choice_stage(role, eng, s)
            q_lo = project_split(role, eng, 2, w("sa1_q"), "s_bq", s, HLQ)
            s = split_rows(role, eng, 4, q_lo, QS, "q")
            if role == "pe":
                eng.wait_ge(q_lo[0], q_lo[1] + NC - 1)
            k_lo = project_split(role, eng, 3, w("sa1_k"), "s_bk", (sem("ln_out"), 7 * NC + 1), HL)
            s = split_rows(role, eng, 5, k_lo, KSA, "k")
            attention(role, eng, SA1, "first", s, T)
            attention(role, eng, SA1, "rest", s, T, (k_lo[0], k_lo[1] + NC - 1))
            s = attention_out(role, eng, SA1, 3, "sa1_o", "den16", "s_bo", X, X)

            s = layernorm(role, eng, 8, X, T, s)
            s = tree_stage(role, eng, s)
            return X, s

        block = ctx.enter_context(nc.Block())

        @block.tensor
        def _(eng):
            program("pe", eng)

        @block.vector
        def _(eng):
            program("dve", eng)

        @block.scalar
        def _(eng):
            program("act", eng)

        @block.gpsimd
        def _(eng):
            program("pool", eng)

        @block.sync
        def _(eng):
            res, s = program("sp", eng)
            stored = sem("stored")
            eng.wait_ge(s[0], s[1] + NC - 1)
            eng.dma_start(outT, res[:, :]).then_inc(stored, 16)
            eng.wait_ge(stored, 16)



def _values(att, wv, bv):
    wa = np.zeros((wv.shape[0], att.NV), wv.dtype)
    ba = np.zeros((128, att.NV), wv.dtype)
    for r, quad, h0, nh, v0, oc in att.groups:
        for i in range(nh):
            a, h = v0 + i * (att.d + 1), h0 + i
            wa[:, a:a + att.d] = wv[:, h * att.d:(h + 1) * att.d]
            if bv is not None:
                ba[:, a:a + att.d] = bv[h * att.d:(h + 1) * att.d][None, :]
            ba[:, a + att.d] = 1.0
    return wa, ba


def _outputs(att, wo):
    out = np.zeros((128, 2, D), wo.dtype)
    for r, quad, h0, nh, v0, oc in att.groups:
        for i in range(nh):
            a = 32 * quad + i * (att.d + 1)
            out[a:a + att.d, r] = wo[(h0 + i) * att.d:(h0 + i + 1) * att.d]
    return out.reshape(128, 2 * D)


def _denominators(att):
    pick = np.zeros((128, 2, 32), np.float32)
    spread = np.zeros((4, 32, 2, D), np.float32)
    for r, quad, h0, nh, v0, oc in att.groups:
        for i in range(nh):
            a = 32 * quad + i * (att.d + 1)
            pick[a + att.d, r, h0 + i] = 1.0
            if h0 + i == 0:
                pick[a + att.d, r, att.H:] = 1.0
            spread[:, h0 + i, r, a:a + att.d] = 1.0
    return np.concatenate([pick.reshape(128, 64), spread.reshape(128, 2 * D)], axis=1)


def _tree_paths():
    path = np.zeros((128, NODES + 1), np.float32)
    need = np.zeros(NODES, np.float32)
    for n in range(NODES):
        k = n
        while k > 0:
            parent, right = (k - 1) // 2, (k - 1) % 2
            path[parent, n] = 1.0 if right else -1.0
            need[n] += right
            k = parent
    return path, need - 0.5


def kernel(**inputs):
    import ml_dtypes
    import concourse.bacc as _bacc
    from concourse.bass_utils import run_bass_kernel_spmd as _run

    i = {k: np.asarray(v) for k, v in inputs.items()}
    z = np.float32
    xT = np.ascontiguousarray(i["x"].reshape(N, D).T)
    ctxT = np.ascontiguousarray(i["ctx_1024"].transpose(0, 2, 1))

    wp = np.zeros((128, W_COLS), z)

    def put(name, a):
        o, n = W_AT[name]
        a = np.asarray(a)
        assert a.shape[1] == n, (name, a.shape, n)
        wp[:a.shape[0], o:o + n] = a

    bs = np.zeros((128, 64), z)

    def put_bias(name, a):
        bs[:len(a), BIAS_AT[name]] = a

    put("mean", np.full((D, 1), 1.0 / D, z))
    put("centre", np.eye(D, dtype=z) - z(1.0 / D))
    put("ones", np.ones((D, D), z))
    put("ident", np.eye(D, dtype=z))
    qkv, qb = i["L0_xattn_qkv_w"], i["L0_xattn_qkv_b"]
    for k, n in enumerate("qkv"):
        put(f"c_{n}", qkv[k * D:(k + 1) * D].T)
        put_bias(f"c_b{n}", qb[k * D:(k + 1) * D])
    put("c_o", i["L0_xattn_sa_out_w"].T)
    put_bias("c_bo", i["L0_xattn_sa_out_b"])
    ip, ib = i["L0_xattn_in_proj_w"], i["L0_xattn_in_proj_b"]
    put("c_wq", ip[0:D].T)
    put_bias("bq0", ib[0:D])
    put("xa0_k", ip[D:2 * D].T)
    put_bias("bk0", ib[D:2 * D])
    wa, ba = _values(XA0, ip[2 * D:].T, ib[2 * D:])
    put("xa0_v", wa)
    put("xa0_vb", ba)
    put("xa0_o", _outputs(XA0, i["L0_xattn_mha_out_w"].T))
    put_bias("bo0", i["L0_xattn_mha_out_b"])
    put("xa0_den", _denominators(XA0))
    for k in (1, 2, 3):
        put_bias(f"g{k}", i[f"L0_xattn_ln{k}_g"])
        put_bias(f"b{k}", i[f"L0_xattn_ln{k}_b"])
    put("lin1", i["L0_xattn_lin1_w"].T)
    put("lin2", i["L0_xattn_lin2_w"].T.reshape(4, D, D).transpose(1, 0, 2).reshape(D, FF))
    for f in range(4):
        put_bias(f"l1b{f}", i["L0_xattn_lin1_b"][f * D:(f + 1) * D])
    put_bias("l2b", i["L0_xattn_lin2_b"])

    d = SA0.d
    inv = 1.0 / 10000.0 ** (np.arange(0, d, 2, dtype=z) / d)
    ang = np.outer(np.arange(S, dtype=z), inv)
    cos, sin = np.cos(ang).astype(z), np.sin(ang).astype(z)
    pair = (np.arange(D) % d) // 2
    sign = np.where(np.arange(D) % 2 == 0, -1.0, 1.0).astype(z)
    put("rope", np.concatenate([cos[:, pair].T, sin[:, pair].T * sign[:, None]], axis=1))
    swap = np.arange(D) ^ 1
    wq, wk = i["L0_attn_wq"], i["L0_attn_wk_up"]
    put("sa0_q", np.concatenate([wq, wq[:, swap]], axis=1))
    put("down", i["L0_attn_w_down"])
    put("sa0_k", np.concatenate([wk, wk[:, swap]], axis=1))
    wa, ba = _values(SA0, i["L0_attn_wv_up"], None)
    put("sa0_v", wa)
    put("sa0_vb", ba)
    put("sa0_o", _outputs(SA0, i["L0_attn_wo"]))
    put("den16", _denominators(SA0))
    ms = np.zeros((128, 8), z)
    for r, quad, h0, nh, v0, oc in SA0.groups:
        for k in range(nh):
            a = 32 * quad + k * (d + 1)
            ms[a:a + d + 1, 4 * r + k] = 1.0
    put("m_sel", ms)
    put("quad", (np.arange(128)[:, None] // 32 == np.arange(4)[None, :]).astype(z))

    put("gate", i["L0_ffn_gate_weight"].T)
    put("gate_b", np.broadcast_to(i["L0_ffn_e_score_correction_bias"][None, :], (128, E)))
    put("shared", np.concatenate([i["L0_ffn_shared_gate_w"].T, i["L0_ffn_shared_up_w"].T,
                                  i["L0_ffn_shared_down_w"].T], axis=1))
    gu = i["L0_ffn_experts_gate_up"].reshape(E // 2, 2, 2, EI, D)
    gate_up = gu.transpose(0, 4, 2, 1, 3).reshape(E // 2, D, 2 * D)
    dn = i["L0_ffn_experts_down"].reshape(E // 2, 2, D, EI).transpose(0, 1, 3, 2).reshape(E // 2, D, D)
    experts = np.concatenate([gate_up, dn], axis=2)
    picks = np.zeros((E // 2, 2 * E, D), ml_dtypes.bfloat16)
    for p in range(E // 2):
        for k in range(2):
            picks[p, 2 * p + k, k * EI:(k + 1) * EI] = 1.0
            picks[p, E + 2 * p + k, k * EI:(k + 1) * EI] = 1.0

    put("xa1_q", i["L1_xattn_W_Q"])
    put_bias("bq1", i["L1_xattn_b_Q"])
    put("xa1_k", i["L1_xattn_W_K"])
    put_bias("bk1", i["L1_xattn_b_K"])
    wa, ba = _values(XA1, i["L1_xattn_W_V"], i["L1_xattn_b_V"])
    put("xa1_v", wa)
    put("xa1_vb", ba)
    put("xa1_o", _outputs(XA1, i["L1_xattn_W_O"]))
    put_bias("bo1", i["L1_xattn_b_O"])
    put("sa1_q", i["L1_attn_Wq"])
    put_bias("s_bq", i["L1_attn_bq"])
    put("sa1_k", i["L1_attn_Wk"])
    put_bias("s_bk", i["L1_attn_bk"])
    wa, ba = _values(SA1, i["L1_attn_Wv"], i["L1_attn_bv"])
    put("sa1_v", wa)
    put("sa1_vb", ba)
    put("sa1_o", _outputs(SA1, i["L1_attn_Wo"]))
    put_bias("s_bo", i["L1_attn_bo"])
    put("ws1", i["L1_attn_Ws1"])
    put_bias("bs1", i["L1_attn_bs1"])
    put("ws2", i["L1_attn_Ws2"])
    put_bias("bs2", i["L1_attn_bs2"])

    path, thr = _tree_paths()
    put_bias("thr0", thr[:INNER])
    put_bias("thr1", thr[INNER:])
    put("bias", bs)
    wi = i["L1_ffn_W_in"].reshape(TREES, NODES, D).transpose(0, 2, 1)
    wo = i["L1_ffn_W_out"].reshape(D, TREES, NODES).transpose(1, 2, 0)
    bi = i["L1_ffn_b_in"].reshape(TREES, NODES)
    trees = np.zeros((TREES, 128, NODES + 2 * D + 2), z)
    trees[:, :, 0:NODES] = wi
    trees[:, 0:INNER, NODES:NODES + D] = wo[:, 0:INNER]
    trees[:, :, NODES + D:NODES + 2 * D] = wo[:, INNER:]
    trees[:, 0:INNER, NODES + 2 * D] = bi[:, 0:INNER]
    trees[:, :, NODES + 2 * D + 1] = bi[:, INNER:]

    bp = np.zeros((128, B_COLS), ml_dtypes.bfloat16)

    def put16(name, a):
        o, n = B_AT[name]
        bp[:a.shape[0], o:o + n] = a
    put16("ident16", np.eye(D))
    put16("tree", path)
    rows = np.arange(RAW) % 32
    for hg, dd in ((2, 16), (4, 8)):
        heads = (rows[:, None] // dd == np.arange(hg)[None, :]).astype(z)
        put16(f"hm{hg}", np.concatenate([heads, np.ones((3, hg), z)]))
    page = (np.arange(S) // 32).astype(z)
    put16("krow", page[None, :])
    put16("qrow", ((1.0 - page) * MASKED)[None, :])

    nc = _bacc.Bacc("TRN2", target_bir_lowering=False, num_devices=1)
    arrays, args = {}, []
    for name, a in (("xT", xT), ("ctxT", ctxT), ("wpack", wp), ("bpack", bp), ("experts", experts), ("picks", picks),
                    ("trees", trees)):
        a = np.ascontiguousarray(a)
        arrays[name] = a
        args.append(nc.dram_tensor(name, a.shape, mybir.dt.from_np(a.dtype), kind="ExternalInput").ap())
    args.append(nc.dram_tensor("outT", (D, N), F32, kind="ExternalOutput").ap())
    bass_perceiver_kernel(nc, *args)
    r = _run(nc, [arrays], core_ids=[0])
    return np.ascontiguousarray(r.results[0]["outT"].T).reshape(B, S, D)
```
